# Optimizing a Trainium2 kernel written in Bass

```python
import numpy as np
import jax
import jax.numpy as jnp

def _softmax(x, axis=-1):
    return jax.nn.softmax(x, axis=axis)

def _gelu(x):
    return jax.nn.gelu(x, approximate=True)

def _silu(x):
    return jax.nn.silu(x)

def _sigmoid(x):
    return jax.nn.sigmoid(x)

def _layernorm(x, axis=-1, eps=1e-05):
    m = jnp.mean(x, axis=axis, keepdims=True)
    v = jnp.var(x, axis=axis, keepdims=True)
    return (x - m) / jnp.sqrt(v + eps)

def _scatter_add(tgt, idx, src, axis=0):
    return tgt.at[idx].add(src)

def _segment_sum(src, seg, n):
    return jax.ops.segment_sum(src, seg, n)
kernel_name = 'mk_decoder_preln_d1_seqx_r2_706232'

def setup_inputs(seed: int=0):
    np.random.seed(seed)
    _w = jnp.asarray

    def _rec_inputs():
        import jax
        import jax.numpy as jnp
        _rk = jax.random.key(seed)
        x = 0.0002417 + 0.9998 * jax.random.normal(jax.random.fold_in(_rk, 1), (1, 4096, 512), jnp.float32)
        _lenS = 4096 - jax.random.randint(jax.random.fold_in(_rk, 7), (1,), 0, max(1, 4096 // 4) + 1, jnp.int32)
        _lenS2 = 3202 - jax.random.randint(jax.random.fold_in(_rk, 8), (1,), 0, max(1, 3202 // 4) + 1, jnp.int32)
        _ctx_1024P = jax.random.normal(jax.random.fold_in(_rk, 11), (1, 16, 512), jnp.float32)
        _ctx_1024c = jax.random.dirichlet(jax.random.fold_in(_rk, 511), 0.3 * jnp.ones((16,), jnp.float32), (1, 3202))
        _ctx_1024t = jnp.einsum('bsk,bkd->bsd', _ctx_1024c, _ctx_1024P)
        _ctx_1024t = _ctx_1024t * jax.lax.rsqrt(jnp.mean(jnp.square(_ctx_1024t)) + 1e-12) * 0.953939
        ctx_1024 = 7.22013e-05 + 1.00017 * (_ctx_1024t + 0.3 * jax.random.normal(jax.random.fold_in(_rk, 611), (1, 3202, 512), jnp.float32))
        return (x, ctx_1024)
    x, ctx_1024 = _rec_inputs()

    def _L0_attn_setup():
        import jax, jax.numpy as jnp
        import numpy as np
        NUM_HEADS = 8
        ROPE_BASE = 10000.0

        def _rope(x):
            b, n, c = x.shape
            k_max = c // 2
            theta = 1.0 / ROPE_BASE ** (jnp.arange(k_max, dtype=jnp.float32) / k_max)
            angles = jnp.arange(n, dtype=jnp.float32)[:, None] * theta
            cos = jnp.cos(angles)
            sin = jnp.sin(angles)
            xr = x[..., 0::2]
            xi = x[..., 1::2]
            pr = cos * xr - sin * xi
            pi = cos * xi + sin * xr
            return jnp.concatenate([pr, pi], axis=-1)
        key = jax.random.key(seed)
        ks = jax.random.split(key, 5)
        b, n, c = (4, 2048, 512)
        x = jax.random.normal(ks[0], (b, n, c), dtype=jnp.float32)
        qk_w = jax.random.normal(ks[1], (c, 2 * c), dtype=jnp.float32) * (1.0 / np.sqrt(c))
        qk_b = jnp.zeros((2 * c,), dtype=jnp.float32)
        lepe_w = jax.random.normal(ks[2], (3, c, c), dtype=jnp.float32) * (1.0 / np.sqrt(3 * c))
        lepe_b = jnp.zeros((c,), dtype=jnp.float32)
        return {'x': x, 'qk_w': qk_w, 'qk_b': qk_b, 'lepe_w': lepe_w, 'lepe_b': lepe_b}
    _L0_attn_all = _L0_attn_setup()
    _L0_attn_in = {k: v for k, v in _L0_attn_all.items() if k in ('qk_w', 'qk_b', 'lepe_w', 'lepe_b')}
    del _L0_attn_all

    def _L0_xattn_setup():
        import jax, jax.numpy as jnp
        import numpy as np
        D_MODEL = 512
        B, S = (4, 1024)
        key = jax.random.key(seed)
        ks = jax.random.split(key, 10)
        s = 1.0 / np.sqrt(D_MODEL)
        return {'k': jax.random.normal(ks[0], (B, S, D_MODEL), jnp.float32), 'v': jax.random.normal(ks[1], (B, S, D_MODEL), jnp.float32), 'q': jax.random.normal(ks[2], (B, S, D_MODEL), jnp.float32), 'Wk': jax.random.normal(ks[3], (D_MODEL, D_MODEL), jnp.float32) * s, 'Wv': jax.random.normal(ks[4], (D_MODEL, D_MODEL), jnp.float32) * s, 'bv': jnp.zeros((D_MODEL,), jnp.float32), 'Wq': jax.random.normal(ks[5], (D_MODEL, D_MODEL), jnp.float32) * s, 'bq': jnp.zeros((D_MODEL,), jnp.float32), 'Wo': jax.random.normal(ks[6], (D_MODEL, D_MODEL), jnp.float32) * s, 'bo': jnp.zeros((D_MODEL,), jnp.float32)}
    _L0_xattn_all = _L0_xattn_setup()
    _L0_xattn_in = {k: v for k, v in _L0_xattn_all.items() if k in ('Wk', 'Wv', 'bv', 'Wq', 'bq', 'Wo', 'bo')}
    del _L0_xattn_all

    def _L0_ffn_setup():
        import jax, jax.numpy as jnp
        import numpy as np

        def _binarize(w):
            alpha = jax.lax.stop_gradient(jnp.mean(jnp.abs(w), axis=1, keepdims=True))
            bw = alpha * jnp.sign(w)
            return w + jax.lax.stop_gradient(bw - w)
        key = jax.random.key(seed)
        k1, k2, k3, k4, k5 = jax.random.split(key, 5)
        D, H = (512, 2048)
        x = jax.random.normal(k1, (64, 196, D), dtype=jnp.float32)
        w1 = jax.random.normal(k2, (H, D), dtype=jnp.float32) * 0.02
        b1 = jax.random.normal(k3, (H,), dtype=jnp.float32) * 0.02
        w2 = jax.random.normal(k4, (D, H), dtype=jnp.float32) * 0.02
        b2 = jax.random.normal(k5, (D,), dtype=jnp.float32) * 0.02
        return {'x': x, 'w1': w1, 'b1': b1, 'w2': w2, 'b2': b2}
    _L0_ffn_all = _L0_ffn_setup()
    _L0_ffn_in = {k: v for k, v in _L0_ffn_all.items() if k in ('w1', 'b1', 'w2', 'b2')}
    del _L0_ffn_all
    return {'x': x, 'ctx_1024': ctx_1024, 'L0_attn_qk_w': _L0_attn_in['qk_w'], 'L0_attn_qk_b': _L0_attn_in['qk_b'], 'L0_attn_lepe_w': _L0_attn_in['lepe_w'], 'L0_attn_lepe_b': _L0_attn_in['lepe_b'], 'L0_xattn_Wk': _L0_xattn_in['Wk'], 'L0_xattn_Wv': _L0_xattn_in['Wv'], 'L0_xattn_bv': _L0_xattn_in['bv'], 'L0_xattn_Wq': _L0_xattn_in['Wq'], 'L0_xattn_bq': _L0_xattn_in['bq'], 'L0_xattn_Wo': _L0_xattn_in['Wo'], 'L0_xattn_bo': _L0_xattn_in['bo'], 'L0_ffn_w1': _L0_ffn_in['w1'], 'L0_ffn_b1': _L0_ffn_in['b1'], 'L0_ffn_w2': _L0_ffn_in['w2'], 'L0_ffn_b2': _L0_ffn_in['b2']}

def reference(x, ctx_1024, L0_attn_qk_w, L0_attn_qk_b, L0_attn_lepe_w, L0_attn_lepe_b, L0_xattn_Wk, L0_xattn_Wv, L0_xattn_bv, L0_xattn_Wq, L0_xattn_bq, L0_xattn_Wo, L0_xattn_bo, L0_ffn_w1, L0_ffn_b1, L0_ffn_w2, L0_ffn_b2):
    import jax
    import jax.numpy as jnp

    def _L0_attn_ref(x, qk_w, qk_b, lepe_w, lepe_b):
        import jax, jax.numpy as jnp
        import numpy as np
        NUM_HEADS = 8
        ROPE_BASE = 10000.0

        def _rope(x):
            b, n, c = x.shape
            k_max = c // 2
            theta = 1.0 / ROPE_BASE ** (jnp.arange(k_max, dtype=jnp.float32) / k_max)
            angles = jnp.arange(n, dtype=jnp.float32)[:, None] * theta
            cos = jnp.cos(angles)
            sin = jnp.sin(angles)
            xr = x[..., 0::2]
            xi = x[..., 1::2]
            pr = cos * xr - sin * xi
            pi = cos * xi + sin * xr
            return jnp.concatenate([pr, pi], axis=-1)
        b, n, c = x.shape
        h = NUM_HEADS
        d = c // h
        qk = x @ qk_w + qk_b
        q, k = jnp.split(qk, 2, axis=-1)
        q = jax.nn.elu(q) + 1.0
        k = jax.nn.elu(k) + 1.0
        q_rope = _rope(q)
        k_rope = _rope(k)

        def to_heads(t):
            return t.reshape(b, n, h, d).transpose(0, 2, 1, 3)
        qh = to_heads(q)
        kh = to_heads(k)
        qr = to_heads(q_rope)
        kr = to_heads(k_rope)
        vh = to_heads(x)
        k_mean = jnp.mean(kh, axis=2, keepdims=True)
        z = 1.0 / (jnp.einsum('bhnd,bhmd->bhnm', qh, k_mean) + 1e-06)
        kv = jnp.einsum('bhnd,bhne->bhde', kr, vh) * (1.0 / jnp.sqrt(jnp.float32(n)))
        out = jnp.einsum('bhnd,bhde->bhne', qr, kv) * z
        out = out.transpose(0, 2, 1, 3).reshape(b, n, c)
        lepe = jax.lax.conv_general_dilated(x, lepe_w, window_strides=(1,), padding='SAME', dimension_numbers=('NWC', 'WIO', 'NWC')) + lepe_b
        return out + lepe

    def _L0_xattn_ref(k, v, q, Wk, Wv, bv, Wq, bq, Wo, bo):
        import jax, jax.numpy as jnp
        import numpy as np
        D_MODEL = 512
        B, S = (4, 1024)
        kp = jnp.einsum('bsd,ed->bse', k, Wk)
        vp = jnp.einsum('bsd,ed->bse', v, Wv) + bv
        qp = jnp.einsum('bsd,ed->bse', q, Wq) + bq
        scale = 1.0 / jnp.sqrt(jnp.float32(kp.shape[-1]))
        scores = jnp.einsum('bqd,bkd->bqk', qp, kp) * scale
        probs = jax.nn.softmax(scores, axis=-1)
        ctx = jnp.einsum('bqk,bkd->bqd', probs, vp)
        return jnp.einsum('bqd,ed->bqe', ctx, Wo) + bo

    def _L0_ffn_ref(x, w1, b1, w2, b2):
        import jax, jax.numpy as jnp
        import numpy as np

        def _binarize(w):
            alpha = jax.lax.stop_gradient(jnp.mean(jnp.abs(w), axis=1, keepdims=True))
            bw = alpha * jnp.sign(w)
            return w + jax.lax.stop_gradient(bw - w)
        bw1 = _binarize(w1)
        h = jnp.einsum('bsd,hd->bsh', x, bw1) + b1
        h = jax.nn.gelu(h, approximate=False)
        bw2 = _binarize(w2)
        out = jnp.einsum('bsh,dh->bsd', h, bw2) + b2
        return out
    x = x + _L0_attn_ref(_layernorm(x, axis=-1), L0_attn_qk_w, L0_attn_qk_b, L0_attn_lepe_w, L0_attn_lepe_b)
    x = x + _L0_xattn_ref(ctx_1024, ctx_1024, _layernorm(x, axis=-1), L0_xattn_Wk, L0_xattn_Wv, L0_xattn_bv, L0_xattn_Wq, L0_xattn_bq, L0_xattn_Wo, L0_xattn_bo)
    x = x + _L0_ffn_ref(_layernorm(x, axis=-1), L0_ffn_w1, L0_ffn_b1, L0_ffn_w2, L0_ffn_b2)
    return x

_drawn_inputs = setup_inputs


def setup_inputs(seed=0):
    import zlib

    import numpy as np

    out = dict(_drawn_inputs(seed))
    spreads = {'L0_attn_qk_b': (0.0, 0.763),
     'L0_attn_lepe_b': (0.0, 0.1),
     'L0_xattn_bv': (0.0, 0.1),
     'L0_xattn_bq': (0.0, 0.522),
     'L0_xattn_bo': (0.0, 0.1)}
    factors = {'L0_ffn_b1': 8.0, 'L0_ffn_b2': 4.657}
    for name, (base, spread) in spreads.items():
        noise = np.random.default_rng([zlib.crc32(name.encode()), seed]).standard_normal(out[name].shape)
        drawn = base * np.exp(spread * noise) if base else spread * noise
        out[name] = jnp.asarray(drawn.astype(out[name].dtype))
    for name, factor in factors.items():
        out[name] = (out[name] * factor).astype(out[name].dtype)
    return out
```

```python
from contextlib import ExitStack

import concourse.bass as bass
from concourse import mybir

F32 = mybir.dt.float32
F16 = mybir.dt.float16
ALU = mybir.AluOpType
ACT = mybir.ActivationFunctionType
AX_X = mybir.AxisListType.X

P = 128
N, C, M, H = 4096, 512, 3202, 2048
T = 512
NB = N // T
SUB = T // P
CT = C // P
HT = H // P
KT = -(-M // P)
KLAST = M - (KT - 1) * P
NH = 8
DH = C // NH
HALF = C // 2
HALO = T + 2
EDGE = 16
EPS = 1e-5
WS = 32.0
SCALE = float(C) ** -0.5
HEAD = 16
RING = 4
LAG = 3


def build(nc, d):
    with ExitStack() as ctx:
        def sb(name, cols, dt=F32):
            return ctx.enter_context(nc.sbuf_tensor(name, [P, cols], dt))

        heads = []

        def sem(name, owner):
            s = ctx.enter_context(nc.semaphore(name))
            heads.append((owner, s))
            return s

        def start(owner, eng):
            for who, s in heads:
                if who == owner:
                    eng.sem_inc(s, HEAD)

        bank = [ctx.enter_context(nc.psum_tensor(f"bank{i}", [P, 512], F32)) for i in range(8)]

        ident = sb("ident", P)
        ones = sb("ones", P)
        zeros16 = sb("zeros16", 512, F16)
        key_bias = sb("key_bias", KT)
        alpha1 = sb("alpha1", HT)
        b1_col = sb("b1_col", HT)
        alpha2_row = sb("alpha2_row", C)
        attn_row = sb("attn_row", C)
        stats = sb("stats", SUB * 6)
        mv = sb("mv", SUB * 2)
        ve = sb("ve", SUB)
        sd = sb("sd", SUB)
        r0 = sb("r0", SUB)
        r1 = sb("r1", SUB)
        rstd = sb("rstd", SUB)
        stats_v = stats[:, :].rearrange("p (s k) -> p s k", s=SUB)
        mv_v = mv[:, :].rearrange("p (s k) -> p s k", s=SUB)

        ARENA = 51260
        arena = sb("arena", ARENA)

        class Carve:
            def __init__(self, at=0):
                self.at = at

            def f32(self, *shape):
                n = 1
                for k in shape:
                    n *= k
                v = arena[:, self.at:self.at + n]
                self.at += n
                assert self.at <= ARENA, self.at
                return self.shaped(v, shape)

            def f16(self, *shape):
                n = 1
                for k in shape:
                    n *= k
                v = arena[:, self.at:self.at + (n + 1) // 2].bitcast(F16)[:, 0:n]
                self.at += (n + 1) // 2
                assert self.at <= ARENA, self.at
                return self.shaped(v, shape)

            @staticmethod
            def shaped(v, shape):
                if len(shape) == 2:
                    return v.rearrange("p (a b) -> p a b", a=shape[0])
                if len(shape) == 3:
                    return v.rearrange("p (a b c) -> p a b c", a=shape[0], b=shape[1])
                return v

        def blocks(ap):
            return ap.rearrange("(b s p) c -> b p s c", s=SUB, p=P)

        def one(view, n):
            return view[bass.ds(n, 1)].rearrange("b p s c -> (b p) s c")

        x_v, x1_v, x2_v, out_v = blocks(d["x"]), blocks(d["x1"]), blocks(d["x2"]), blocks(d["out"])
        cos_v, sin_v = blocks(d["cos"]), blocks(d["sin"])
        xT_v = [d[k].rearrange("(j p) n -> p j n", p=P) for k in ("xT_hi", "xT_lo")]
        cosT_v, sinT_v = (d[k].rearrange("(j p) n -> p j n", p=P) for k in ("cosT", "sinT"))

        def rows(name):
            return d[name].rearrange("(j p) n -> p j n", p=P)

        def row_of(name):
            return d[name].rearrange("(a n) -> a n", a=1).to_broadcast([P, C])

        def mm3(pe, out, w, x, first, last):
            pe.matmul(out, w[0], x[0], start=first, stop=False)
            pe.matmul(out, w[0], x[1], start=False, stop=False)
            return pe.matmul(out, w[1], x[0], start=False, stop=last)

        class Norm:
            def __init__(self, name, x, xn, xT, loaded):
                self.x, self.xn, self.xT, self.loaded = x, xn, xT, loaded
                self.step = sem(name + "_ln_step", "dve")
                self.sd = sem(name + "_ln_sd", "act")
                self.xn_ready = sem(name + "_xn_ready", "dve")
                self.turned = sem(name + "_turned", "pe")
                self.hi = sem(name + "_xT_hi", "act")
                self.lo = sem(name + "_xT_lo", "dve")

            def vector_stats(self, dve, n, par, i):
                s0 = n * 8
                dve.wait_ge(self.loaded[par], 16 * i + 16)
                for s in range(SUB):
                    last = nc.vector.bn_stats(stats_v[:, s, :], self.x[par][:, s, :])
                last.then_inc(self.step, 1)
                dve.wait_ge(self.step, HEAD + s0 + 1)
                nc.vector.memset(ve[:, :], EPS)
                for s in range(SUB):
                    last = nc.vector.bn_aggr(mv_v[:, s, :], stats_v[:, s, :])
                last.then_inc(self.step, 1)
                dve.wait_ge(self.step, HEAD + s0 + 2)
                nc.vector.tensor_tensor(ve[:, :], mv_v[:, :, 1], ve[:, :], ALU.add).then_inc(self.step, 1)
                dve.wait_ge(self.sd, HEAD + n + 1)
                nc.vector.reciprocal(r0[:, :], sd[:, :]).then_inc(self.step, 1)
                dve.wait_ge(self.step, HEAD + s0 + 4)
                nc.vector.tensor_tensor(r1[:, :], r0[:, :], r0[:, :], ALU.mult).then_inc(self.step, 1)
                dve.wait_ge(self.step, HEAD + s0 + 5)
                nc.vector.tensor_tensor(r1[:, :], r1[:, :], ve[:, :], ALU.mult).then_inc(self.step, 1)
                dve.wait_ge(self.step, HEAD + s0 + 6)
                nc.vector.tensor_scalar(r1[:, :], r1[:, :], -0.5, 1.5, ALU.mult, ALU.add).then_inc(self.step, 1)
                dve.wait_ge(self.step, HEAD + s0 + 7)
                nc.vector.tensor_tensor(rstd[:, :], r0[:, :], r1[:, :], ALU.mult).then_inc(self.step, 1)
                dve.wait_ge(self.step, HEAD + s0 + 8)

            def vector_xn(self, par):
                for s in range(SUB):
                    nc.vector.tensor_scalar(self.xn[par][:, s, :], self.x[par][:, s, :], mv_v[:, s, 0:1],
                                            rstd[:, s:s + 1], ALU.subtract, ALU.mult).then_inc(self.xn_ready, 1)

            def scalar_sd(self, act, n):
                act.wait_ge(self.step, HEAD + n * 8 + 3)
                nc.scalar.activation(sd[:, :], ve[:, :], ACT.Sqrt).then_inc(self.sd, 1)

            def tensor_turn(self, pe, n, par):
                for s in range(SUB):
                    pe.wait_ge(self.xn_ready, HEAD + n * 4 + s + 1)
                    for j in range(CT):
                        last = pe.transpose(bank[4 + j][:, s * P:(s + 1) * P],
                                            self.xn[par][:, s, j * P:(j + 1) * P], ident[:, :])
                last.then_inc(self.turned, 1)

            def scalar_hi(self, act, n, par):
                act.wait_ge(self.turned, HEAD + n + 1)
                for j in range(CT):
                    nc.scalar.activation(self.xT[par][0][:, j, :], bank[4 + j][:, :], ACT.Copy).then_inc(self.hi, 1)

            def vector_lo(self, dve, n, par):
                for j in range(CT):
                    dve.wait_ge(self.hi, HEAD + n * 4 + j + 1)
                    nc.vector.tensor_tensor(self.xT[par][1][:, j, :], bank[4 + j][:, :],
                                            self.xT[par][0][:, j, :], ALU.subtract).then_inc(self.lo, 1)

        a = Carve()
        a_wraw = a.f32(CT, C)
        a_w = (a.f16(CT, C), a.f16(CT, C))
        a_x = [a.f32(SUB, C) for _ in range(2)]
        a_xn = [a.f32(SUB, C) for _ in range(2)]
        a_xT = [(a.f16(CT, T), a.f16(CT, T)) for _ in range(2)]
        a_cos = [a.f32(SUB, HALF) for _ in range(2)]
        a_sin = [a.f32(SUB, HALF) for _ in range(2)]
        a_bias = a.f32(C)
        a_pre = [a.f32(C) for _ in range(2)]
        a_exp = [a.f32(C) for _ in range(2)]
        a_relu = [a.f32(C) for _ in range(2)]
        a_k = [a.f32(C) for _ in range(SUB)]
        a_rc = [a.f32(C) for _ in range(2)]
        a_rs = [a.f32(C) for _ in range(2)]
        a_kr = [a.f32(C) for _ in range(SUB)]
        a_xload = [sem(f"a_xload{u}", None) for u in range(2)]
        a_tabs = [sem(f"a_tabs{u}", None) for u in range(2)]
        a_wload = sem("a_wload", None)
        a_consts = sem("a_consts", "pool")
        a_eye = sem("a_eye", "pool")
        a_whi = sem("a_whi", "act")
        a_wlo = sem("a_wlo", "dve")
        a_store = [sem(f"a_store{u}", "sp") for u in range(2)]
        a_edge = sem("a_edge", None)
        a_kps = sem("a_kps", "pe")
        a_predone = sem("a_predone", "dve")
        a_acts = sem("a_acts", "act")
        a_kdone = sem("a_kdone", "dve")
        a_rot = sem("a_rot", "pool")
        a_krdone = sem("a_krdone", "dve")
        a_kvdone = sem("a_kvdone", "pe")
        A = Norm("a", a_x, a_xn, a_xT, a_xload)

        b = Carve()
        b_wraw = b.f32(CT, C)
        b_lraw = b.f32(3 * CT, C)
        b_w = (b.f16(CT, C), b.f16(CT, C))
        b_lw = (b.f16(3 * CT, C), b.f16(3 * CT, C))
        b_xT = [(b.f16(CT, HALO), b.f16(CT, HALO)) for _ in range(2)]
        b_x = [b.f32(SUB, C) for _ in range(2)]
        b_cos = [b.f32(2, T) for _ in range(2)]
        b_sin = [b.f32(2, T) for _ in range(2)]
        b_exp = [b.f32(T) for _ in range(2)]
        b_relu = [b.f32(T) for _ in range(2)]
        b_q = b.f32(4, T)
        b_ec = b.f32(2, T)
        b_os = b.f32(2, T)
        b_oc = b.f32(2, T)
        b_es = b.f32(2, T)
        b_qr = b.f32(4, T)
        b_kv = b.f32(4, P)
        b_km = b.f32(4, NH)
        b_bq = b.f32(4)
        b_lrow = b.f32(C)
        b_den = b.f32(SUB, NH)
        b_z = b.f32(SUB, NH)
        b_t = [b.f32(C) for _ in range(2)]
        b_wload = sem("b_wload", None)
        b_whi = sem("b_whi", "act")
        b_wlo = sem("b_wlo", "dve")
        b_kvset = sem("b_kvset", "dve")
        b_load = [sem(f"b_load{u}", None) for u in range(2)]
        b_qps = sem("b_qps", "pe")
        b_acts = sem("b_acts", "act")
        b_qdone = sem("b_qdone", "dve")
        b_mdve = sem("b_mdve", "dve")
        b_mpool = sem("b_mpool", "pool")
        b_rope = sem("b_rope", "dve")
        b_zps = sem("b_zps", "pe")
        b_zstep = sem("b_zstep", "dve")
        b_lps = sem("b_lps", "pe")
        b_aps = sem("b_aps", "pe")
        b_xb = sem("b_xb", "pool")
        b_tstep = sem("b_tstep", "dve")
        b_x1 = sem("b_x1", "dve")
        b_store = [sem(f"b_store{u}", "sp") for u in range(2)]

        kvc = Carve()
        kp = (kvc.f16(CT, M), kvc.f16(CT, M))
        vp = (kvc.f16(KT, C), kvc.f16(KT, C))
        s = Carve(kvc.at)
        s_raw = [s.f32(CT, C) for _ in range(4)]
        s_A = (s.f16(CT, C), s.f16(CT, C))
        s_B = (s.f16(CT, C), s.f16(CT, C))
        s_ctx = [s.f32(CT, T) for _ in range(2)]
        s_ctxp = [(s.f16(CT, T), s.f16(CT, T)) for _ in range(2)]
        s_sign = [s.f16(4 * C) for _ in range(2)]
        s_sum2 = s.f32(C)
        s_bq = s.f32(4)
        s_bv = s.f32(4)
        s_bvw = s.f32(4, P)
        s_bo = s.f32(C)
        s_u = (s.f16(4, 2), s.f16(4, 2))
        s_kb = s.f32(4)
        s_wload = sem("s_wload", None)
        s_prod = sem("s_prod", "pe")
        s_hi = sem("s_hi", "act")
        s_lo = sem("s_lo", "dve")
        s_bvw_ok = sem("s_bvw_ok", "dve")
        s_load = [sem(f"s_load{u}", None) for u in range(2)]
        s_chi = sem("s_chi", "act")
        s_clo = sem("s_clo", "dve")
        s_kps = sem("s_kps", "pe")
        s_khi = sem("s_khi", "act")
        s_klo = sem("s_klo", "dve")
        s_vps = sem("s_vps", "pe")
        s_vhi = sem("s_vhi", "act")
        s_vlo = sem("s_vlo", "dve")
        s_bps = sem("s_bps", "pe")
        s_kbs = sem("s_kbs", "dve")
        f_load = [sem(f"f_load{u}", None) for u in range(2)]
        f_sign = sem("f_sign", "act")
        f_abs = sem("f_abs", "act")
        f_add = sem("f_add", "pool")
        f_store = [sem(f"f_store{u}", "act") for u in range(2)]
        f_aps = sem("f_aps", "pe")
        f_alpha = sem("f_alpha", "dve")

        c = Carve(kvc.at)
        c_S = c.f32(KT, T)
        c_xT = [(c.f16(CT, T), c.f16(CT, T))] * 2
        c_x = [c.f32(SUB, C) for _ in range(2)]
        c_xn = [c.f32(SUB, C)] * 2
        c_ph = [c.f16(T) for _ in range(RING)]
        c_diag = Carve(c.at).f32(SUB, P)
        c_pl = [c.f16(T) for _ in range(RING)]
        c_mx = c.f32(T)
        c_mb = c.f32(T)
        c_sum = c.f32(T)
        c_mcol = c.f32(SUB)
        c_rinv = c.f32(SUB)
        c_load = [sem(f"c_load{u}", None) for u in range(2)]
        c_qk = sem("c_qk", "pe")
        c_s = sem("c_s", "act")
        c_max = sem("c_max", "dve")
        c_mt = sem("c_mt", "pe")
        c_mstep = sem("c_mstep", "dve")
        c_mps = sem("c_mps", "pe")
        c_mbd = sem("c_mbd", "dve")
        c_sub = sem("c_sub", "dve")
        c_exp = sem("c_exp", "act")
        c_hi = sem("c_hi", "dve")
        c_lo = sem("c_lo", "dve")
        c_pv = sem("c_pv", "pe")
        c_add = sem("c_add", "pool")
        c_rs = sem("c_rs", "pe")
        c_ri = sem("c_ri", "dve")
        c_xb = sem("c_xb", "pool")
        c_x2 = sem("c_x2", "dve")
        c_store = [sem(f"c_store{u}", "sp") for u in range(2)]
        Cn = Norm("c", c_x, c_xn, c_xT, c_load)

        e = Carve()
        d_w1 = e.f16(CT, H)
        d_w2 = e.f16(HT, C)
        assert e.at <= CT * M
        e = Carve(kvc.at)
        d_x = [e.f32(SUB, C) for _ in range(2)]
        d_xn = [e.f32(SUB, C)] * 2
        d_xT = [(e.f16(CT, T), e.f16(CT, T))] * 2
        d_g = [e.f32(T) for _ in range(2)]
        d_gh = e.f16(HT, T)
        d_gl = e.f16(HT, T)
        d_b2 = e.f32(C)
        d_t = [e.f32(C) for _ in range(2)]
        d_wload = sem("d_wload", None)
        d_load = [sem(f"d_load{u}", None) for u in range(2)]
        d_hps = sem("d_hps", "pe")
        d_gelu = sem("d_gelu", "act")
        d_ghi = sem("d_ghi", "dve")
        d_glo = sem("d_glo", "dve")
        d_f2 = sem("d_f2", "pe")
        d_ops = sem("d_ops", "pe")
        d_xb = sem("d_xb", "pool")
        d_ts = sem("d_ts", "dve")
        d_out = sem("d_out", "dve")
        d_store = [sem(f"d_store{u}", "sp") for u in range(2)]
        Dn = Norm("d", d_x, d_xn, d_xT, d_load)

        def after_a(eng):
            eng.wait_ge(a_kvdone, HEAD + 4 * NB)
            eng.wait_ge(a_krdone, HEAD + 4 * NB)
            for u in range(2):
                eng.wait_ge(a_store[u], HEAD + 16 * NB)

        def after_b(eng):
            eng.wait_ge(b_x1, HEAD + 4 * NB)
            eng.wait_ge(b_lps, HEAD + 4 * NB)
            eng.wait_ge(b_aps, HEAD + 4 * NB)
            for u in range(2):
                eng.wait_ge(b_store[u], HEAD + 16 * NB // 2)

        CH = M // T

        def after_s(eng):
            eng.wait_ge(s_klo, HEAD + 4 * (CH + 1))
            eng.wait_ge(s_vlo, HEAD + KT)
            eng.wait_ge(s_kbs, HEAD + 2 * (CH + 1))
            eng.wait_ge(f_alpha, HEAD + 3)
            for u in range(2):
                eng.wait_ge(f_store[u], HEAD + 64)

        def after_c(eng):
            eng.wait_ge(c_x2, HEAD + 4 * NB)
            eng.wait_ge(c_add, HEAD + (KT - 1) * NB)
            eng.wait_ge(c_rs, HEAD + NB)
            for u in range(2):
                eng.wait_ge(c_store[u], HEAD + 16 * NB // 2)

        block = ctx.enter_context(nc.Block())

        @block.sync
        def _(sp):
            start("sp", sp)

            def pair_loop(body):
                with sp.Fori(0, NB // 2 - 1) as i:
                    body(i, False)
                body(NB // 2 - 1, True)

            def load_a(n, u):
                sp.dma_start(a_x[u], one(x_v, n)).then_inc(a_xload[u], 16)
                sp.dma_start(a_cos[u], one(cos_v, n)).then_inc(a_tabs[u], 16)
                sp.dma_start(a_sin[u], one(sin_v, n)).then_inc(a_tabs[u], 16)

            load_a(0, 0)
            sp.dma_start(a_wraw, rows("wk_rope")).then_inc(a_wload, 16)
            sp.dma_start(a_bias, row_of("bk_rope")).then_inc(a_wload, 16)
            sp.wait_ge(a_consts, HEAD + 1)
            for v in xT_v:
                for col in (0, EDGE + N):
                    sp.dma_start(v[:, :, col:col + EDGE],
                                 zeros16[:, 0:CT * EDGE].rearrange("p (j o) -> p j o", j=CT)).then_inc(a_edge, 16)

            def body_a(i, last):
                for u in range(2):
                    n = 2 * i + u
                    if not (last and u):
                        sp.wait_ge(a_krdone, HEAD + 4 * n)
                        sp.wait_ge(A.xn_ready, HEAD + 4 * n)
                        load_a(n + 1, 1 - u)
                    sp.wait_ge(A.lo, HEAD + 4 * n + 4)
                    for k in range(2):
                        sp.dma_start(xT_v[k][:, :, bass.ds(n * T + EDGE, T)], a_xT[u][k]).then_inc(a_store[u], 16)

            pair_loop(body_a)

            after_a(sp)
            sp.wait_ge(a_edge, 64)
            sp.dma_start(b_wraw, rows("wq_rope")).then_inc(b_wload, 16)
            sp.dma_start(b_bq, d["bq_rope"]).then_inc(b_wload, 16)
            sp.dma_start(b_lrow, row_of("lepe_b")).then_inc(b_wload, 16)

            def load_b(n, u):
                for k in range(2):
                    sp.dma_start(b_xT[u][k], xT_v[k][:, :, bass.ds(n * T + EDGE - 1, HALO)]).then_inc(b_load[u], 16)
                sp.dma_start(b_cos[u], cosT_v[:, :, bass.ds(n * T, T)]).then_inc(b_load[u], 16)
                sp.dma_start(b_sin[u], sinT_v[:, :, bass.ds(n * T, T)]).then_inc(b_load[u], 16)
                sp.dma_start(b_x[u], one(x_v, n)).then_inc(b_load[u], 16)

            load_b(0, 0)
            sp.dma_start(b_lraw, d["lepe_w"].rearrange("(j p) n -> p j n", p=P)).then_inc(b_wload, 16)

            def body_b(i, last):
                for u in range(2):
                    n = 2 * i + u
                    if not (last and u):
                        sp.wait_ge(b_aps, HEAD + 4 * n)
                        sp.wait_ge(b_lps, HEAD + 4 * n)
                        sp.wait_ge(b_store[1 - u], HEAD + 16 * (i + u))
                        load_b(n + 1, 1 - u)
                    sp.wait_ge(b_x1, HEAD + 4 * n + 4)
                    sp.dma_start(one(x1_v, n), b_x[u]).then_inc(b_store[u], 16)

            pair_loop(body_b)

            after_b(sp)
            for k, name in enumerate(("xk", "xq", "xv", "xoT")):
                sp.dma_start(s_raw[k], rows(name)).then_inc(s_wload, 16)
            sp.dma_start(s_bq, d["xbq"]).then_inc(s_wload, 16)
            sp.dma_start(s_bv, d["xbv"]).then_inc(s_wload, 16)
            sp.dma_start(s_bo, row_of("xbo")).then_inc(s_wload, 16)
            ctxT_v = rows("ctxT")

            def load_s(n, u):
                sp.dma_start(s_ctx[u], ctxT_v[:, :, bass.ds(n * T, T)]).then_inc(s_load[u], 16)

            load_s(0, 0)
            with sp.Fori(0, CH // 2 - 1) as i:
                sp.wait_ge(s_clo, HEAD + 8 * i)
                load_s(2 * i + 1, 1)
                sp.wait_ge(s_clo, HEAD + 8 * i + 4)
                load_s(2 * i + 2, 0)
            sp.wait_ge(s_clo, HEAD + 4 * (CH - 2))
            load_s(CH - 1, 1)
            sp.wait_ge(s_clo, HEAD + 4 * (CH - 1))
            sp.dma_start(s_ctx[0][:, :, 0:M - CH * T], ctxT_v[:, :, CH * T:M]).then_inc(s_load[0], 16)

            after_s(sp)

            def load_c(n, u):
                sp.dma_start(c_x[u], one(x1_v, n)).then_inc(c_load[u], 16)

            load_c(0, 0)

            def body_c(i, last):
                for u in range(2):
                    n = 2 * i + u
                    if not (last and u):
                        sp.wait_ge(c_store[1 - u], HEAD + 16 * (i + u))
                        load_c(n + 1, 1 - u)
                    if last and u:
                        sp.wait_ge(c_qk, HEAD + KT * NB)
                        sp.dma_start(d_w1, rows("sign1")).then_inc(d_wload, 16)
                        sp.dma_start(d_w2, rows("sign2")).then_inc(d_wload, 16)
                    sp.wait_ge(c_x2, HEAD + 4 * n + 4)
                    sp.dma_start(one(x2_v, n), c_x[u]).then_inc(c_store[u], 16)

            pair_loop(body_c)

            after_c(sp)

            def load_d(n, u):
                sp.dma_start(d_x[u], one(x2_v, n)).then_inc(d_load[u], 16)

            load_d(0, 0)
            sp.dma_start(d_b2, row_of("b2")).then_inc(d_wload, 16)

            def body_d(i, last):
                for u in range(2):
                    n = 2 * i + u
                    if not (last and u):
                        sp.wait_ge(d_store[1 - u], HEAD + 16 * (i + u))
                        load_d(n + 1, 1 - u)
                    sp.wait_ge(d_out, HEAD + 4 * n + 4)
                    sp.dma_start(one(out_v, n), d_x[u]).then_inc(d_store[u], 16)

            pair_loop(body_d)
            for u in range(2):
                sp.wait_ge(d_store[u], HEAD + 16 * NB // 2)

        @block.gpsimd
        def _(pool):
            nc.gpsimd.memset(zeros16[:, :], 0.0).then_inc(a_consts, 1)
            start("pool", pool)
            nc.gpsimd.memset(ident[:, :], 0.0).then_inc(a_eye, 1)
            nc.gpsimd.memset(ones[:, :], 1.0).then_inc(a_eye, 1)
            pool.wait_ge(a_eye, HEAD + 2)
            nc.gpsimd.affine_select(out=ident[:, :], in_=ident[:, :], compare_op=ALU.not_equal, fill=1.0,
                                    base=0, pattern=[[-1, P]], channel_multiplier=1).then_inc(a_eye, 1)

            def pair_loop(body):
                with pool.Fori(0, NB // 2 - 1) as i:
                    body(i, False)
                body(NB // 2 - 1, True)

            def body_a(i, last):
                for u in range(2):
                    n = 2 * i + u
                    pool.wait_ge(a_tabs[u], 32 * i + 32)
                    for t in range(SUB):
                        pool.wait_ge(a_kdone, HEAD + 4 * n + t + 1)
                        pool.wait_ge(a_krdone, HEAD + 4 * n + t - 1)
                        k2 = a_k[t].rearrange("p (h c) -> p h c", h=2)
                        tab = a_cos[u][:, t, :].rearrange("p (o c) -> p o c", o=1).to_broadcast([P, 2, HALF])
                        nc.gpsimd.tensor_tensor(a_rc[t % 2].rearrange("p (h c) -> p h c", h=2), k2, tab, ALU.mult)
                        nc.gpsimd.tensor_tensor(a_rs[t % 2][:, 0:HALF], a_k[t][:, HALF:C], a_sin[u][:, t, :], ALU.mult)
                        nc.gpsimd.tensor_tensor(a_rs[t % 2][:, HALF:C], a_k[t][:, 0:HALF], a_sin[u][:, t, :],
                                                ALU.mult).then_inc(a_rot, 1)

            pair_loop(body_a)

            after_a(pool)
            pool.wait_ge(b_wload, 48 + 16)

            def body_b(i, last):
                for u in range(2):
                    n = 2 * i + u
                    pool.wait_ge(b_load[u], 80 * i + 80)
                    for t in range(SUB):
                        nc.gpsimd.tensor_tensor(b_x[u][:, t, :], b_x[u][:, t, :], b_lrow, ALU.add).then_inc(b_xb, 1)
                    pool.wait_ge(b_qdone, HEAD + 4 * n + 4)
                    pool.wait_ge(b_rope, HEAD + 2 * n)
                    nc.gpsimd.tensor_tensor(b_oc, b_q[:, 2:4, :], b_cos[u], ALU.mult)
                    nc.gpsimd.tensor_tensor(b_es, b_q[:, 0:2, :], b_sin[u], ALU.mult).then_inc(b_mpool, 1)

            pair_loop(body_b)

            after_b(pool)
            pool.wait_ge(s_prod, HEAD + 10)

            w1v, w2v = rows("w1T"), d["w2T"].rearrange("(g k p) n -> g p k n", k=4, p=P)

            def load_f(g):
                src = w1v[:, g, :].rearrange("p (k n) -> p k n", k=4) if g < 4 else w2v[g - 4]
                pool.dma_start(s_raw[g % 2], src).then_inc(f_load[g % 2], 16)

            load_f(0)
            load_f(1)
            for g in range(8):
                if g:
                    pool.wait_ge(f_abs, HEAD + g + 1)
                    if g < 4:
                        nc.gpsimd.tensor_tensor(s_raw[3], s_raw[3], s_raw[2], ALU.add).then_inc(f_add, 1)
                    else:
                        for k in range(4):
                            if g == 4 and k == 0:
                                nc.gpsimd.tensor_copy(s_sum2, s_raw[2][:, 0, :]).then_inc(f_add, 1)
                            else:
                                pool.wait_ge(f_add, HEAD + 3 + (g - 4) * 4 + k)
                                nc.gpsimd.tensor_tensor(s_sum2, s_sum2, s_raw[2][:, k, :], ALU.add).then_inc(f_add, 1)
                else:
                    pool.wait_ge(f_abs, HEAD + 1)
                if g + 2 < 8:
                    load_f(g + 2)

            after_s(pool)

            def body_c(i, last):
                for u in range(2):
                    n = 2 * i + u
                    pool.wait_ge(Cn.xn_ready, HEAD + 4 * n + 4)
                    for t in range(SUB):
                        nc.gpsimd.tensor_tensor(c_x[u][:, t, :], c_x[u][:, t, :], attn_row[:, :], ALU.add).then_inc(c_xb, 1)
                    pool.wait_ge(c_rs, HEAD + n)
                    for t in range(1, KT):
                        pool.wait_ge(c_exp, HEAD + KT * n + t + 1)
                        k = P if t < KT - 1 else KLAST
                        if t == 1:
                            nc.gpsimd.tensor_tensor(c_sum, c_S[:, 0, :], c_S[:, 1, :], ALU.add).then_inc(c_add, 1)
                        else:
                            pool.wait_ge(c_add, HEAD + (KT - 1) * n + t - 1)
                            nc.gpsimd.tensor_tensor(c_sum[0:k, :], c_sum[0:k, :], c_S[0:k, t, :], ALU.add).then_inc(c_add, 1)

            pair_loop(body_c)

            after_c(pool)
            pool.wait_ge(d_wload, 48)

            def body_d(i, last):
                for u in range(2):
                    n = 2 * i + u
                    pool.wait_ge(Dn.xn_ready, HEAD + 4 * n + 4)
                    for t in range(SUB):
                        nc.gpsimd.tensor_tensor(d_x[u][:, t, :], d_x[u][:, t, :], d_b2, ALU.add).then_inc(d_xb, 1)

            pair_loop(body_d)

        @block.scalar
        def _(act):
            start("act", act)
            act.dma_start(b1_col[:, :], d["b1"]).then_inc(a_wload, 16)

            def pair_loop(body):
                with act.Fori(0, NB // 2 - 1) as i:
                    body(i, False)
                body(NB // 2 - 1, True)

            act.wait_ge(a_wload, 48)
            A.scalar_sd(act, 0)
            for j in range(CT):
                nc.scalar.activation(a_w[0][:, j, :], a_wraw[:, j, :], ACT.Copy, scale=WS).then_inc(a_whi, 1)
            A.scalar_hi(act, 0, 0)

            def body_a(i, last):
                for u in range(2):
                    n = 2 * i + u
                    more = not (last and u)
                    if more:
                        A.scalar_sd(act, n + 1)
                    for t in range(SUB):
                        act.wait_ge(a_predone, HEAD + 4 * n + t + 1)
                        act.wait_ge(a_kdone, HEAD + 4 * n + t - 1)
                        nc.scalar.activation(a_exp[t % 2], a_pre[t % 2], ACT.Exp)
                        nc.scalar.activation(a_relu[t % 2], a_pre[t % 2], ACT.Relu).then_inc(a_acts, 1)
                    if more:
                        act.wait_ge(a_kps, HEAD + 4 * n)
                        act.wait_ge(a_store[1 - u], HEAD + 32 * (i + u))
                        A.scalar_hi(act, n + 1, 1 - u)

            pair_loop(body_a)

            after_a(act)
            act.wait_ge(b_wload, 64)
            for j in range(CT):
                nc.scalar.activation(b_w[0][:, j, :], b_wraw[:, j, :], ACT.Copy, scale=WS).then_inc(b_whi, 1)
            for j in range(3 * CT):
                nc.scalar.activation(b_lw[0][:, j, :], b_lraw[:, j, :], ACT.Copy, scale=WS).then_inc(b_whi, 1)

            def body_b(i, last):
                for u in range(2):
                    n = 2 * i + u
                    for t in range(4):
                        act.wait_ge(b_qps, HEAD + 4 * n + t + 1)
                        act.wait_ge(b_qdone, HEAD + 4 * n + t - 1)
                        nc.scalar.activation(b_exp[t % 2], bank[t % 2][:, :], ACT.Exp, bias=b_bq[:, t:t + 1], scale=1 / WS)
                        nc.scalar.activation(b_relu[t % 2], bank[t % 2][:, :], ACT.Relu, bias=b_bq[:, t:t + 1],
                                             scale=1 / WS).then_inc(b_acts, 1)

            pair_loop(body_b)

            after_b(act)
            for m in range(8):
                act.wait_ge(s_prod, HEAD + m + 1 + (m > 3))
                dst = s_A if m < 4 else s_B
                nc.scalar.activation(dst[0][:, m % 4, :], bank[m % 4][:, :], ACT.Copy, scale=WS).then_inc(s_hi, 1)
                if m == 3:
                    act.wait_ge(s_prod, HEAD + 5)
                    nc.scalar.activation(s_u[0][:, :, 0], bank[6][:, 0:4], ACT.Copy, scale=WS).then_inc(s_hi, 1)

            def ffn_group(g):
                act.wait_ge(f_load[g % 2], 16 * (g // 2) + 16)
                if g >= 2:
                    act.wait_ge(f_store[g % 2], HEAD + 16 * (g // 2))
                flat = s_raw[g % 2].rearrange("p k n -> p (k n)")
                nc.scalar.activation(s_sign[g % 2], flat, ACT.Sign).then_inc(f_sign, 1)
                if g >= 2:
                    act.wait_ge(f_add, HEAD + (g - 1 if g < 5 else 3 + 4 * (g - 4)))
                dst = s_raw[3] if g == 0 else s_raw[2]
                nc.scalar.activation(dst.rearrange("p k n -> p (k n)"), flat, ACT.Abs).then_inc(f_abs, 1)
                act.wait_ge(f_sign, HEAD + g + 1)
                if g < 4:
                    act.dma_start(d["sign1"][g * P:(g + 1) * P, :], s_sign[g % 2]).then_inc(f_store[g % 2], 16)
                else:
                    act.dma_start(d["sign2"].rearrange("(g k p) n -> g p k n", k=4, p=P)[g - 4],
                                  s_sign[g % 2].rearrange("p (k n) -> p k n", k=4)).then_inc(f_store[g % 2], 16)

            def chunk(n, u, i, nk, nt, dyn):
                w = nk
                act.wait_ge(s_load[u], i)
                for j in range(CT):
                    nc.scalar.activation(s_ctxp[u][0][:, j, 0:w], s_ctx[u][:, j, 0:w], ACT.Copy).then_inc(s_chi, 1)
                for j in range(CT):
                    act.wait_ge(s_kps, HEAD + 4 * n + j + 1)
                    nc.scalar.activation(kp[0][:, j, dyn(n, w)], bank[j][:, 0:w], ACT.Copy, scale=1 / WS).then_inc(s_khi, 1)
                for q in range(nt):
                    k = min(P, w - q * P)
                    act.wait_ge(s_vps, HEAD + 4 * n + q + 1)
                    nc.scalar.activation(vp[0][0:k, bass.ds(4 * n + q, 1), :].rearrange("p a c -> p (a c)"),
                                         bank[4 + q % 2][0:k, :], ACT.Copy, scale=1 / WS).then_inc(s_vhi, 1)

            def at(n, w):
                return bass.ds(n * T, w)

            with act.Fori(0, CH // 2) as i:
                for u in range(2):
                    act.wait_ge(s_vps, HEAD + 8 * i + 4 * u - 4)
                    chunk(2 * i + u, u, 16 * i + 16, T, 4, at)
            chunk(CH, 0, 16 * (CH // 2) + 16, M - CH * T, 2, at)
            for g in range(8):
                ffn_group(g)

            after_s(act)
            Cn.scalar_sd(act, 0)
            Cn.scalar_hi(act, 0, 0)

            def body_c(i, last):
                for u in range(2):
                    n = 2 * i + u
                    more = not (last and u)
                    act.wait_ge(c_lo, HEAD + KT * n)
                    act.wait_ge(c_add, HEAD + (KT - 1) * n)
                    for t in range(KT):
                        k = P if t < KT - 1 else KLAST
                        act.wait_ge(c_qk, HEAD + KT * n + t + 1)
                        nc.scalar.activation(c_S[0:k, t, :], bank[4 + t % 3][0:k, :], ACT.Identity,
                                             bias=key_bias[0:k, t:t + 1]).then_inc(c_s, 1)
                    for t in range(KT):
                        k = P if t < KT - 1 else KLAST
                        if more and t == 6:
                            Cn.scalar_sd(act, n + 1)
                        if more and t == 16:
                            Cn.scalar_hi(act, n + 1, 0)
                        act.wait_ge(c_sub, HEAD + KT * n + t + 1)
                        nc.scalar.activation(c_S[0:k, t, :], c_S[0:k, t, :], ACT.Exp, scale=SCALE).then_inc(c_exp, 1)

            pair_loop(body_c)

            after_c(act)
            Dn.scalar_sd(act, 0)
            Dn.scalar_hi(act, 0, 0)

            def body_d(i, last):
                for u in range(2):
                    n = 2 * i + u
                    more = not (last and u)
                    for t in range(HT):
                        if more and t == 8:
                            Dn.scalar_sd(act, n + 1)
                        act.wait_ge(d_hps, HEAD + HT * n + t + 1)
                        act.wait_ge(d_glo, HEAD + HT * n + t - 1)
                        nc.scalar.activation(d_g[t % 2], bank[4 + t % 4][:, :], ACT.Gelu, bias=b1_col[:, t:t + 1],
                                             scale=alpha1[:, t:t + 1]).then_inc(d_gelu, 1)
                    if more:
                        Dn.scalar_hi(act, n + 1, 0)

            pair_loop(body_d)

        @block.vector
        def _(dve):
            start("dve", dve)

            def pair_loop(body):
                with dve.Fori(0, NB // 2 - 1) as i:
                    body(i, False)
                body(NB // 2 - 1, True)

            def lo_part(out, src, hi, scale):
                return nc.vector.scalar_tensor_tensor(out=out, in0=src, scalar=scale, in1=hi,
                                                      op0=ALU.mult, op1=ALU.subtract)

            A.vector_stats(dve, 0, 0, 0)
            A.vector_xn(0)
            dve.wait_ge(a_wload, 48)
            for j in range(CT):
                dve.wait_ge(a_whi, HEAD + j + 1)
                lo_part(a_w[1][:, j, :], a_wraw[:, j, :], a_w[0][:, j, :], WS).then_inc(a_wlo, 1)
            A.vector_lo(dve, 0, 0)

            def elu_a(n, t):
                dve.wait_ge(a_acts, HEAD + 4 * n + t + 1)
                dve.wait_ge(a_kvdone, HEAD + 4 * n + t - 3)
                nc.vector.scalar_tensor_tensor(out=a_k[t], in0=a_exp[t % 2], scalar=1.0, in1=a_relu[t % 2],
                                               op0=ALU.min, op1=ALU.add).then_inc(a_kdone, 1)

            def rope_a(n, t):
                dve.wait_ge(a_rot, HEAD + 4 * n + t + 1)
                nc.vector.tensor_tensor(a_kr[t][:, 0:HALF], a_rc[t % 2][:, 0:HALF], a_rs[t % 2][:, 0:HALF], ALU.subtract)
                nc.vector.tensor_tensor(a_kr[t][:, HALF:C], a_rc[t % 2][:, HALF:C], a_rs[t % 2][:, HALF:C],
                                        ALU.add).then_inc(a_krdone, 1)

            def body_a(i, last):
                for u in range(2):
                    n = 2 * i + u
                    more = not (last and u)
                    if more:
                        A.vector_stats(dve, n + 1, 1 - u, i + u)
                        dve.wait_ge(a_kvdone, HEAD + 4 * n)
                        A.vector_xn(1 - u)
                    for t in range(SUB + 2):
                        if t < SUB:
                            dve.wait_ge(a_kps, HEAD + 4 * n + t + 1)
                            dve.wait_ge(a_acts, HEAD + 4 * n + t - 1)
                            nc.vector.scalar_tensor_tensor(out=a_pre[t % 2], in0=bank[t % 2][:, :], scalar=1 / WS,
                                                           in1=a_bias, op0=ALU.mult, op1=ALU.add).then_inc(a_predone, 1)
                        if 1 <= t <= SUB:
                            elu_a(n, t - 1)
                        if t >= 2:
                            rope_a(n, t - 2)
                    if more:
                        A.vector_lo(dve, n + 1, 1 - u)

            pair_loop(body_a)

            after_a(dve)
            kv_ps = bank[2][:, :].rearrange("p (t c) -> p t c", t=4)
            nc.vector.memset(b_kv, 0.0).then_inc(b_kvset, 1)
            nc.vector.memset(b_km, 0.0).then_inc(b_kvset, 1)
            dve.wait_ge(b_kvset, HEAD + 2)
            for h in range(2):
                o = h * DH
                nc.vector.tensor_scalar(b_kv[o:o + DH, :, o:o + DH], kv_ps[o:o + DH, :, o:o + DH],
                                        float(N) ** -0.5, None, ALU.mult)
            for g in range(4):
                for t in range(4):
                    last = nc.vector.tensor_scalar(b_km[32 * g:32 * g + 32, t, 4 * (t % 2) + g:4 * (t % 2) + g + 1],
                                                   bank[3][32 * g:32 * g + 32, t:t + 1], 1.0 / N, None, ALU.mult)
            last.then_inc(b_kvset, 1)
            dve.wait_ge(b_wload, 64)
            for j in range(4 * CT):
                dve.wait_ge(b_whi, HEAD + j + 1)
                w, r, q = (b_w, b_wraw, j) if j < CT else (b_lw, b_lraw, j - CT)
                lo_part(w[1][:, q, :], r[:, q, :], w[0][:, q, :], WS).then_inc(b_wlo, 1)

            def body_b(i, last):
                for u in range(2):
                    n = 2 * i + u
                    dve.wait_ge(b_load[u], 80 * i + 80)
                    dve.wait_ge(b_zps, HEAD + n)
                    dve.wait_ge(b_mpool, HEAD + n)
                    for t in range(4):
                        dve.wait_ge(b_acts, HEAD + 4 * n + t + 1)
                        nc.vector.scalar_tensor_tensor(out=b_q[:, t, :], in0=b_exp[t % 2], scalar=1.0, in1=b_relu[t % 2],
                                                       op0=ALU.min, op1=ALU.add).then_inc(b_qdone, 1)
                    dve.wait_ge(b_qdone, HEAD + 4 * n + 4)
                    nc.vector.tensor_tensor(b_ec, b_q[:, 0:2, :], b_cos[u], ALU.mult)
                    nc.vector.tensor_tensor(b_os, b_q[:, 2:4, :], b_sin[u], ALU.mult).then_inc(b_mdve, 1)
                    dve.wait_ge(b_mdve, HEAD + n + 1)
                    dve.wait_ge(b_aps, HEAD + 4 * n)
                    nc.vector.tensor_tensor(b_qr[:, 0:2, :], b_ec, b_os, ALU.subtract).then_inc(b_rope, 1)
                    dve.wait_ge(b_mpool, HEAD + n + 1)
                    nc.vector.tensor_tensor(b_qr[:, 2:4, :], b_oc, b_es, ALU.add).then_inc(b_rope, 1)
                    dve.wait_ge(b_zps, HEAD + n + 1)
                    nc.vector.tensor_scalar(b_den, bank[6][:, 0:SUB * NH].rearrange("p (s h) -> p s h", s=SUB), 1e-6,
                                            None, ALU.add).then_inc(b_zstep, 1)
                    dve.wait_ge(b_zstep, HEAD + 2 * n + 1)
                    nc.vector.reciprocal(b_z, b_den).then_inc(b_zstep, 1)
                    dve.wait_ge(b_zstep, HEAD + 2 * n + 2)
                    for t in range(SUB):
                        z = b_z[:, t, :].rearrange("p (h o) -> p h o", o=1).to_broadcast([P, NH, DH])
                        dve.wait_ge(b_aps, HEAD + 4 * n + t + 1)
                        nc.vector.tensor_tensor(b_t[t % 2].rearrange("p (h c) -> p h c", h=NH),
                                                bank[2 + t % 2][:, :].rearrange("p (h c) -> p h c", h=NH),
                                                z, ALU.mult).then_inc(b_tstep, 1)
                        dve.wait_ge(b_tstep, HEAD + 8 * n + 2 * t + 1)
                        dve.wait_ge(b_lps, HEAD + 4 * n + t + 1)
                        nc.vector.scalar_tensor_tensor(out=b_t[t % 2], in0=bank[4 + t % 2][:, :], scalar=1 / WS,
                                                       in1=b_t[t % 2], op0=ALU.mult, op1=ALU.add).then_inc(b_tstep, 1)
                        dve.wait_ge(b_tstep, HEAD + 8 * n + 2 * t + 2)
                        dve.wait_ge(b_xb, HEAD + 4 * n + t + 1)
                        nc.vector.tensor_tensor(b_x[u][:, t, :], b_x[u][:, t, :], b_t[t % 2], ALU.add).then_inc(b_x1, 1)

            pair_loop(body_b)

            after_b(dve)
            dve.wait_ge(s_wload, 7 * 16)
            for j in range(4):
                last = nc.vector.tensor_scalar(s_bvw[:, j, :], ones[:, :], s_bv[:, j:j + 1], None, ALU.mult)
            last.then_inc(s_bvw_ok, 1)
            for m in range(8):
                dve.wait_ge(s_hi, HEAD + m + 1 + (m > 3))
                dst = s_A if m < 4 else s_B
                lo_part(dst[1][:, m % 4, :], bank[m % 4][:, :], dst[0][:, m % 4, :], WS).then_inc(s_lo, 1)
                if m == 3:
                    dve.wait_ge(s_hi, HEAD + 5)
                    lo_part(s_u[0][:, :, 1], bank[6][:, 0:4], s_u[0][:, :, 0], WS).then_inc(s_lo, 1)
            dve.wait_ge(s_prod, HEAD + 10)
            nc.vector.tensor_tensor(attn_row[:, :], bank[7][:, :], s_bo, ALU.add).then_inc(f_alpha, 1)

            def chunk(n, u, nk, nt):
                w = nk
                for j in range(CT):
                    dve.wait_ge(s_chi, HEAD + 4 * n + j + 1)
                    nc.vector.tensor_tensor(s_ctxp[u][1][:, j, 0:w], s_ctx[u][:, j, 0:w], s_ctxp[u][0][:, j, 0:w],
                                            ALU.subtract).then_inc(s_clo, 1)
                for j in range(CT):
                    dve.wait_ge(s_khi, HEAD + 4 * n + j + 1)
                    lo_part(kp[1][:, j, bass.ds(n * T, w)], bank[j][:, 0:w], kp[0][:, j, bass.ds(n * T, w)],
                            1 / WS).then_inc(s_klo, 1)
                for q in range(nt):
                    k = min(P, w - q * P)
                    dve.wait_ge(s_vhi, HEAD + 4 * n + q + 1)
                    tile = bass.ds(4 * n + q, 1)
                    lo_part(vp[1][0:k, tile, :].rearrange("p a c -> p (a c)"), bank[4 + q % 2][0:k, :],
                            vp[0][0:k, tile, :].rearrange("p a c -> p (a c)"), 1 / WS).then_inc(s_vlo, 1)
                dve.wait_ge(s_bps, HEAD + n + 1)
                for q in range(nt):
                    k = min(P, w - q * P)
                    last = nc.vector.tensor_reduce(s_kb[0:k, q:q + 1], bank[6][0:k, 2 * q:2 * q + 2], AX_X, ALU.add)
                last.then_inc(s_kbs, 1)
                dve.wait_ge(s_kbs, HEAD + 2 * n + 1)
                for q in range(nt):
                    k = min(P, w - q * P)
                    last = nc.vector.tensor_scalar(key_bias[0:k, bass.ds(4 * n + q, 1)], s_kb[0:k, q:q + 1], 1 / WS, None,
                                                   ALU.mult)
                last.then_inc(s_kbs, 1)

            with dve.Fori(0, CH // 2) as i:
                for u in range(2):
                    chunk(2 * i + u, u, T, 4)
            chunk(CH, 0, M - CH * T, 2)
            dve.wait_ge(f_aps, HEAD + 1)
            nc.vector.tensor_scalar(alpha1[:, :], bank[5][:, 0:HT], 1.0 / C, None, ALU.mult).then_inc(f_alpha, 1)
            dve.wait_ge(f_aps, HEAD + 2)
            nc.vector.tensor_scalar(alpha2_row[:, :], bank[7][:, :], 1.0 / H, None, ALU.mult).then_inc(f_alpha, 1)

            after_s(dve)
            Cn.vector_stats(dve, 0, 0, 0)
            Cn.vector_xn(0)
            Cn.vector_lo(dve, 0, 0)

            def body_c(i, last):
                for u in range(2):
                    n = 2 * i + u
                    more = not (last and u)
                    for t in range(1, KT):
                        k = P if t < KT - 1 else KLAST
                        dve.wait_ge(c_s, HEAD + KT * n + t + 1)
                        if t == 1:
                            nc.vector.tensor_tensor(c_mx, c_S[:, 0, :], c_S[:, 1, :], ALU.max).then_inc(c_max, 1)
                        else:
                            dve.wait_ge(c_max, HEAD + (KT - 1) * n + t - 1)
                            nc.vector.tensor_tensor(c_mx[0:k, :], c_mx[0:k, :], c_S[0:k, t, :], ALU.max).then_inc(c_max, 1)
                    dve.wait_ge(c_mt, HEAD + n + 1)
                    nc.vector.tensor_reduce(c_mcol, bank[7][:, :].rearrange("p (s k) -> p s k", s=SUB), AX_X,
                                            ALU.max).then_inc(c_mstep, 1)
                    dve.wait_ge(c_mstep, HEAD + 2 * n + 1)
                    for q in range(SUB):
                        last_op = nc.vector.tensor_scalar(c_diag[:, q, :], ident[:, :], c_mcol[:, q:q + 1], None, ALU.mult)
                    last_op.then_inc(c_mstep, 1)
                    dve.wait_ge(c_mps, HEAD + n + 1)
                    nc.vector.tensor_copy(c_mb, bank[7][:, :]).then_inc(c_mbd, 1)
                    dve.wait_ge(c_mbd, HEAD + n + 1)

                    def split(t):
                        k = P if t < KT - 1 else KLAST
                        dve.wait_ge(c_exp, HEAD + KT * n + t + 1)
                        dve.wait_ge(c_pv, HEAD + KT * n + t - RING + 1)
                        nc.vector.tensor_copy(c_ph[t % RING][0:k, :], c_S[0:k, t, :]).then_inc(c_hi, 1)
                        dve.wait_ge(c_hi, HEAD + KT * n + t + 1)
                        nc.vector.tensor_tensor(c_pl[t % RING][0:k, :], c_S[0:k, t, :], c_ph[t % RING][0:k, :],
                                                ALU.subtract).then_inc(c_lo, 1)

                    for t in range(KT + 2):
                        if t < KT:
                            k = P if t < KT - 1 else KLAST
                            nc.vector.tensor_tensor(c_S[0:k, t, :], c_S[0:k, t, :], c_mb[0:k, :], ALU.subtract).then_inc(c_sub, 1)
                        if t >= 2:
                            split(t - 2)
                        if more and t == 6:
                            Cn.vector_stats(dve, n + 1, 1 - u, i + u)
                            Cn.vector_xn(1 - u)
                        if more and t == 20:
                            Cn.vector_lo(dve, n + 1, 0)
                    dve.wait_ge(c_rs, HEAD + n + 1)
                    nc.vector.reciprocal(c_rinv, bank[7][:, 0:SUB]).then_inc(c_ri, 1)
                    dve.wait_ge(c_ri, HEAD + n + 1)
                    dve.wait_ge(c_xb, HEAD + 4 * n + 4)
                    for q in range(SUB):
                        nc.vector.scalar_tensor_tensor(out=c_x[u][:, q, :], in0=bank[q][:, :], scalar=c_rinv[:, q:q + 1],
                                                       in1=c_x[u][:, q, :], op0=ALU.mult, op1=ALU.add).then_inc(c_x2, 1)

            pair_loop(body_c)

            after_c(dve)
            Dn.vector_stats(dve, 0, 0, 0)
            Dn.vector_xn(0)
            Dn.vector_lo(dve, 0, 0)

            def body_d(i, last):
                for u in range(2):
                    n = 2 * i + u
                    more = not (last and u)
                    for t in range(HT):
                        dve.wait_ge(d_gelu, HEAD + HT * n + t + 1)
                        if t < HT - 1:
                            dve.wait_ge(d_f2, HEAD + (HT - 1) * (n - 1) + t + 1)
                        else:
                            dve.wait_ge(d_ops, HEAD + 4 * n)
                        nc.vector.tensor_copy(d_gh[:, t, :], d_g[t % 2]).then_inc(d_ghi, 1)
                        dve.wait_ge(d_ghi, HEAD + HT * n + t + 1)
                        nc.vector.tensor_tensor(d_gl[:, t, :], d_g[t % 2], d_gh[:, t, :], ALU.subtract).then_inc(d_glo, 1)
                        if more and t == 7:
                            Dn.vector_stats(dve, n + 1, 1 - u, i + u)
                            Dn.vector_xn(1 - u)
                    if more:
                        Dn.vector_lo(dve, n + 1, 0)
                    dve.wait_ge(d_xb, HEAD + 4 * n + 4)
                    for q in range(SUB):
                        dve.wait_ge(d_ops, HEAD + 4 * n + q + 1)
                        nc.vector.tensor_tensor(d_t[q % 2], bank[q][:, :], alpha2_row[:, :], ALU.mult).then_inc(d_ts, 1)
                        dve.wait_ge(d_ts, HEAD + 4 * n + q + 1)
                        nc.vector.tensor_tensor(d_x[u][:, q, :], d_t[q % 2], d_x[u][:, q, :], ALU.add).then_inc(d_out, 1)

            pair_loop(body_d)

        @block.tensor
        def _(pe_block):
            pe = nc.tensor
            start("pe", pe_block)

            def pair_loop(body):
                with pe_block.Fori(0, NB // 2 - 1) as i:
                    body(i, False)
                body(NB // 2 - 1, True)

            pe_block.wait_ge(a_consts, HEAD + 1)
            pe_block.wait_ge(a_eye, HEAD + 3)
            for bk in (2, 3):
                pe.matmul(bank[bk][:, :], zeros16[:, 0:P], zeros16[:, :], start=True, stop=True, skip_group_check=True)
            A.tensor_turn(pe_block, 0, 0)
            pe_block.wait_ge(a_wlo, HEAD + CT)

            def k_tile(n, u, t):
                pe_block.wait_ge(a_predone, HEAD + 4 * n + t - 1)
                for j in range(CT):
                    last = mm3(pe, bank[t % 2][:, :],
                               [a_xT[u][h][:, j, t * P:(t + 1) * P] for h in range(2)],
                               [a_w[h][:, j, :] for h in range(2)], j == 0, j == CT - 1)
                last.then_inc(a_kps, 1)

            def kv_tile(n, u, t):
                pe_block.wait_ge(a_krdone, HEAD + 4 * n + t + 1)
                for g in range(4):
                    pe.matmul(bank[2][:, g * P:(g + 1) * P], a_kr[t][:, g * P:(g + 1) * P],
                              a_xn[u][:, t, g * P:(g + 1) * P], start=False, stop=True, skip_group_check=True)
                for g in range(4):
                    last = pe.matmul(bank[3][:, g:g + 1], a_k[t][:, g * P:(g + 1) * P], ones[:, 0:1],
                                     start=False, stop=True, skip_group_check=True)
                last.then_inc(a_kvdone, 1)

            def body_a(i, last):
                for u in range(2):
                    n = 2 * i + u
                    more = not (last and u)
                    pe_block.wait_ge(A.lo, HEAD + 4 * n + 4)
                    k_tile(n, u, 0)
                    k_tile(n, u, 1)
                    k_tile(n, u, 2)
                    if more:
                        A.tensor_turn(pe_block, n + 1, 1 - u)
                    k_tile(n, u, 3)
                    for t in range(SUB):
                        kv_tile(n, u, t)

            pair_loop(body_a)

            after_a(pe_block)
            pe_block.wait_ge(b_wlo, HEAD + CT)
            pe_block.wait_ge(b_kvset, HEAD + 3)

            def lepe(n, u, t):
                pe_block.wait_ge(b_tstep, HEAD + 8 * n + 2 * t - 2)
                for tap in range(3):
                    for j in range(CT):
                        last = mm3(pe, bank[4 + t % 2][:, :],
                                   [b_xT[u][h][:, j, tap + t * P:tap + (t + 1) * P] for h in range(2)],
                                   [b_lw[h][:, tap * CT + j, :] for h in range(2)],
                                   tap == 0 and j == 0, tap == 2 and j == CT - 1)
                last.then_inc(b_lps, 1)

            def att(n, t):
                pe_block.wait_ge(b_rope, HEAD + 2 * n + 2)
                pe_block.wait_ge(b_tstep, HEAD + 8 * n + 2 * t - 3)
                for g in range(4):
                    last = pe.matmul(bank[2 + t % 2][:, g * P:(g + 1) * P], b_qr[:, g, t * P:(t + 1) * P], b_kv[:, g, :],
                                     start=True, stop=True)
                last.then_inc(b_aps, 1)

            def body_b(i, last):
                for u in range(2):
                    n = 2 * i + u
                    pe_block.wait_ge(b_load[u], 80 * i + 80)
                    for t in range(4):
                        pe_block.wait_ge(b_acts, HEAD + 4 * n + t - 1)
                        for j in range(CT):
                            mm = mm3(pe, bank[t % 2][:, :], [b_w[h][:, j, t * P:(t + 1) * P] for h in range(2)],
                                     [b_xT[u][h][:, j, 1:1 + T] for h in range(2)], j == 0, j == CT - 1)
                        mm.then_inc(b_qps, 1)
                    pe_block.wait_ge(b_wlo, HEAD + 4 * CT)
                    lepe(n, u, 0)
                    pe_block.wait_ge(b_qdone, HEAD + 4 * n + 4)
                    for t in range(SUB):
                        for g in range(4):
                            mm = pe.matmul(bank[6][:, t * NH:(t + 1) * NH], b_q[:, g, t * P:(t + 1) * P], b_km[:, g, :],
                                           start=g == 0, stop=g == 3)
                    mm.then_inc(b_zps, 1)
                    lepe(n, u, 1)
                    att(n, 0)
                    att(n, 1)
                    lepe(n, u, 2)
                    att(n, 2)
                    lepe(n, u, 3)
                    att(n, 3)

            pair_loop(body_b)

            after_b(pe_block)
            pe_block.wait_ge(s_wload, 7 * 16)
            for m in range(8):
                w, r = (s_raw[0], s_raw[1]) if m < 4 else (s_raw[2], s_raw[3])
                if m >= 4:
                    pe_block.wait_ge(s_lo, HEAD + m - 3)
                for j in range(CT):
                    mm = pe.matmul(bank[m % 4][:, :], w[:, j, (m % 4) * P:(m % 4 + 1) * P], r[:, j, :],
                                   start=j == 0, stop=j == CT - 1)
                mm.then_inc(s_prod, 1)
                if m == 3:
                    for g in range(4):
                        for j in range(CT):
                            mm = pe.matmul(bank[6][:, g:g + 1], w[:, j, g * P:(g + 1) * P], s_bq[:, j:j + 1],
                                           start=j == 0, stop=j == CT - 1)
                    mm.then_inc(s_prod, 1)
            pe_block.wait_ge(s_bvw_ok, HEAD + 1)
            for j in range(CT):
                mm = pe.matmul(bank[7][:, :], s_bvw[:, j, :], s_raw[3][:, j, :], start=j == 0, stop=j == CT - 1)
            mm.then_inc(s_prod, 1)
            pe_block.wait_ge(s_lo, HEAD + 9)

            def chunk(n, u, w, nt):
                pe_block.wait_ge(s_clo, HEAD + 4 * n + 4)
                for j in range(CT):
                    pe_block.wait_ge(s_klo, HEAD + 4 * n + j - 3)
                    for q in range(CT):
                        mm = mm3(pe, bank[j][:, 0:w], [s_A[h][:, q, j * P:(j + 1) * P] for h in range(2)],
                                 [s_ctxp[u][h][:, q, 0:w] for h in range(2)], q == 0, q == CT - 1)
                    mm.then_inc(s_kps, 1)
                pe_block.wait_ge(s_kbs, HEAD + 2 * n)
                for t in range(nt):
                    k = min(P, w - t * P)
                    for q in range(CT):
                        pe.matmul(bank[6][0:k, 2 * t:2 * t + 2], s_ctxp[u][0][:, q, t * P:t * P + k], s_u[0][:, q, :],
                                  start=q == 0, stop=False)
                        mm = pe.matmul(bank[6][0:k, 2 * t:2 * t + 2], s_ctxp[u][1][:, q, t * P:t * P + k], s_u[0][:, q, :],
                                       start=False, stop=q == CT - 1)
                mm.then_inc(s_bps, 1)
                for t in range(nt):
                    k = min(P, w - t * P)
                    pe_block.wait_ge(s_vlo, HEAD + 4 * n + t - 1)
                    for q in range(CT):
                        mm = mm3(pe, bank[4 + t % 2][0:k, :], [s_ctxp[u][h][:, q, t * P:t * P + k] for h in range(2)],
                                 [s_B[h][:, q, :] for h in range(2)], q == 0, q == CT - 1)
                    mm.then_inc(s_vps, 1)

            with pe_block.Fori(0, CH // 2) as i:
                for u in range(2):
                    chunk(2 * i + u, u, T, 4)
            chunk(CH, 0, M - CH * T, 2)
            pe_block.wait_ge(f_add, HEAD + 3)
            pe_block.wait_ge(s_vlo, HEAD + KT)
            for t in range(HT):
                mm = pe.matmul(bank[5][:, t:t + 1], s_raw[3].rearrange("p k n -> p (k n)")[:, t * P:(t + 1) * P],
                               ones[:, 0:1], start=True, stop=True)
            mm.then_inc(f_aps, 1)
            pe_block.wait_ge(f_add, HEAD + 3 + 16)
            pe.matmul(bank[7][:, :], ones[:, :], s_sum2, start=True, stop=True).then_inc(f_aps, 1)

            after_s(pe_block)
            Cn.tensor_turn(pe_block, 0, 0)

            def body_c(i, last):
                for u in range(2):
                    n = 2 * i + u
                    more = not (last and u)
                    pe_block.wait_ge(Cn.lo, HEAD + 4 * n + 4)
                    for t in range(KT):
                        k = P if t < KT - 1 else KLAST
                        if t >= 3:
                            pe_block.wait_ge(c_s, HEAD + KT * n + t - 2)
                        for j in range(CT):
                            mm = mm3(pe, bank[4 + t % 3][0:k, :], [kp[h][:, j, t * P:t * P + k] for h in range(2)],
                                     [c_xT[0][h][:, j, :] for h in range(2)], j == 0, j == CT - 1)
                        mm.then_inc(c_qk, 1)
                    pe_block.wait_ge(c_max, HEAD + (KT - 1) * n + KT - 1)
                    for q in range(SUB):
                        mm = pe.transpose(bank[7][:, q * P:(q + 1) * P], c_mx[:, q * P:(q + 1) * P], ident[:, :])
                    mm.then_inc(c_mt, 1)
                    pe_block.wait_ge(c_mstep, HEAD + 2 * n + 2)
                    for q in range(SUB):
                        mm = pe.matmul(bank[7][:, q * P:(q + 1) * P], ones[:, :], c_diag[:, q, :], start=True, stop=True)
                    mm.then_inc(c_mps, 1)
                    pe_block.wait_ge(c_x2, HEAD + 4 * n)
                    for t in range(KT):
                        k = P if t < KT - 1 else KLAST
                        if more and t == 16:
                            pe_block.wait_ge(c_s, HEAD + KT * n + KT)
                            Cn.tensor_turn(pe_block, n + 1, 0)
                        pe_block.wait_ge(c_lo, HEAD + KT * n + t + 1)
                        for q in range(SUB):
                            mm = mm3(pe, bank[q][:, :],
                                     [r[t % RING][0:k, q * P:(q + 1) * P] for r in (c_ph, c_pl)],
                                     [vp[h][0:k, t, :] for h in range(2)], t == 0, t == KT - 1)
                        mm.then_inc(c_pv, 1)
                    if more:
                        pe_block.wait_ge(Cn.lo, HEAD + 4 * n + 8)
                    pe_block.wait_ge(c_add, HEAD + (KT - 1) * (n + 1))
                    for q in range(SUB):
                        mm = pe.matmul(bank[7][:, q:q + 1], c_sum[:, q * P:(q + 1) * P], ones[:, 0:1], start=True, stop=True)
                    mm.then_inc(c_rs, 1)

            pair_loop(body_c)

            after_c(pe_block)
            Dn.tensor_turn(pe_block, 0, 0)
            pe_block.wait_ge(d_wload, 48)

            def body_d(i, last):
                for u in range(2):
                    n = 2 * i + u
                    more = not (last and u)

                    def ffn2(t):
                        pe_block.wait_ge(d_glo, HEAD + HT * n + t + 1)
                        if t == 0:
                            pe_block.wait_ge(d_out, HEAD + 4 * n)
                        for q in range(SUB):
                            for h, g in enumerate((d_gh, d_gl)):
                                mm = pe.matmul(bank[q][:, :], g[:, t, q * P:(q + 1) * P], d_w2[:, t, :],
                                               start=t == 0 and h == 0, stop=t == HT - 1 and h == 1)
                            if t == HT - 1:
                                mm.then_inc(d_ops, 1)
                        if t < HT - 1:
                            mm.then_inc(d_f2, 1)

                    pe_block.wait_ge(Dn.lo, HEAD + 4 * n + 4)
                    for t in range(HT + LAG):
                        if t < HT:
                            if t >= 4:
                                pe_block.wait_ge(d_gelu, HEAD + HT * n + t - 3)
                            for j in range(CT):
                                for h in range(2):
                                    mm = pe.matmul(bank[4 + t % 4][:, :], d_w1[:, j, t * P:(t + 1) * P], d_xT[0][h][:, j, :],
                                                   start=j == 0 and h == 0, stop=j == CT - 1 and h == 1)
                            mm.then_inc(d_hps, 1)
                        if more and t == HT + 1:
                            pe_block.wait_ge(d_gelu, HEAD + HT * n + HT)
                            Dn.tensor_turn(pe_block, n + 1, 0)
                        if t >= LAG:
                            ffn2(t - LAG)

            pair_loop(body_d)


def kernel(x, ctx_1024, L0_attn_qk_w, L0_attn_qk_b, L0_attn_lepe_w, L0_attn_lepe_b, L0_xattn_Wk, L0_xattn_Wv,
           L0_xattn_bv, L0_xattn_Wq, L0_xattn_bq, L0_xattn_Wo, L0_xattn_bo, L0_ffn_w1, L0_ffn_b1, L0_ffn_w2,
           L0_ffn_b2):
    import numpy as np
    import concourse.bacc as bacc
    from concourse.bass_utils import run_bass_kernel_spmd as run

    theta = np.float32(1.0) / (10000.0 ** (np.arange(HALF) / HALF)).astype(np.float32)
    angles = np.arange(N, dtype=np.float32)[:, None] * theta
    cos, sin = np.cos(angles), np.sin(angles)

    def cont(v):
        return np.ascontiguousarray(v)

    def column(v):
        return cont(np.reshape(v, (-1, P)).T)

    qk_w, qk_b = np.asarray(L0_attn_qk_w), np.asarray(L0_attn_qk_b)

    def halves(v):
        return np.concatenate([v[..., 0::2], v[..., 1::2]], axis=-1)

    arrays = {
        "x": cont(np.asarray(x)[0]),
        "ctxT": cont(np.asarray(ctx_1024)[0].T),
        "wq_rope": cont(halves(qk_w[:, :C])), "wk_rope": cont(halves(qk_w[:, C:])),
        "bq_rope": column(halves(qk_b[:C])), "bk_rope": cont(halves(qk_b[C:])),
        "lepe_w": cont(np.reshape(L0_attn_lepe_w, (3 * C, C))), "lepe_b": cont(L0_attn_lepe_b),
        "xk": cont(L0_xattn_Wk), "xq": cont(L0_xattn_Wq), "xv": cont(L0_xattn_Wv),
        "xoT": cont(np.asarray(L0_xattn_Wo).T),
        "xbq": column(L0_xattn_bq), "xbv": column(L0_xattn_bv), "xbo": cont(L0_xattn_bo),
        "w1T": cont(np.asarray(L0_ffn_w1).T), "w2T": cont(np.asarray(L0_ffn_w2).T),
        "b1": column(L0_ffn_b1), "b2": cont(L0_ffn_b2),
        "cos": cont(cos), "sin": cont(sin), "cosT": cont(cos.T), "sinT": cont(sin.T),
    }
    nc = bacc.Bacc("TRN2", target_bir_lowering=False, num_devices=1)
    d = {k: nc.dram_tensor(k, v.shape, mybir.dt.from_np(v.dtype), kind="ExternalInput").ap() for k, v in arrays.items()}
    for name, shape, dt in (("x1", (N, C), F32), ("x2", (N, C), F32), ("xT_hi", (C, N + 2 * EDGE), F16), ("xT_lo", (C, N + 2 * EDGE), F16),
                            ("sign1", (C, H), F16), ("sign2", (H, C), F16)):
        d[name] = nc.dram_tensor(name, shape, dt, kind="Internal").ap()
    d["out"] = nc.dram_tensor("out", (N, C), F32, kind="ExternalOutput").ap()
    build(nc, d)
    r = run(nc, [arrays], core_ids=[0])
    return np.reshape(r.results[0]["out"], (1, N, C))
```

```python
from contextlib import ExitStack

import concourse.bass as bass
from concourse import mybir

F32 = mybir.dt.float32
F16 = mybir.dt.float16
ALU = mybir.AluOpType
ACT = mybir.ActivationFunctionType
AX_X = mybir.AxisListType.X

P = 128
N, C, M, H = 4096, 512, 3202, 2048
T = 512
NB = N // T
SUB = T // P
CT = C // P
HT = H // P
KT = M // P
KX = M - KT * P
NH = 8
DH = C // NH
HALF = C // 2
HALO = T + 2
EDGE = 16
EPS = 1e-5
WS = 32.0
SCALE = float(C) ** -0.5
HEAD = 32
RING = 5
HELD = 4
LAG = 3


def build(nc, d):
    with ExitStack() as ctx:
        def sb(name, cols, dt=F32):
            return ctx.enter_context(nc.sbuf_tensor(name, [P, cols], dt))

        heads = []

        def sem(name, owner):
            s = ctx.enter_context(nc.semaphore(name))
            heads.append((owner, s))
            return s

        def start(owner, eng):
            for who, s in heads:
                if who == owner:
                    eng.sem_inc(s, HEAD)

        bank = [ctx.enter_context(nc.psum_tensor(f"bank{i}", [P, 512], F32)) for i in range(8)]

        ident = sb("ident", P)
        ones = sb("ones", P)
        tail_k = sb("tail_k", CT * 2 * KX, F16)
        tail_v = sb("tail_v", C, F16)
        tail_bias = sb("tail_bias", KX)
        key_bias = sb("key_bias", KT)
        alpha1 = sb("alpha1", HT)
        b1_col = sb("b1_col", HT)
        alpha2_row = sb("alpha2_row", C)
        attn_row = sb("attn_row", C)
        stats = sb("stats", SUB * 6)
        mv = sb("mv", SUB * 2)
        ve = sb("ve", SUB)
        sd = sb("sd", SUB)
        r0 = sb("r0", SUB)
        r1 = sb("r1", SUB)
        rstd = sb("rstd", SUB)
        stats_v = stats[:, :].rearrange("p (s k) -> p s k", s=SUB)
        mv_v = mv[:, :].rearrange("p (s k) -> p s k", s=SUB)

        ARENA = 51240
        arena = sb("arena", ARENA)

        class Carve:
            def __init__(self, at=0):
                self.at = at

            def f32(self, *shape):
                n = 1
                for k in shape:
                    n *= k
                v = arena[:, self.at:self.at + n]
                self.at += n
                assert self.at <= ARENA, self.at
                return self.shaped(v, shape)

            def f16(self, *shape):
                n = 1
                for k in shape:
                    n *= k
                v = arena[:, self.at:self.at + (n + 1) // 2].bitcast(F16)[:, 0:n]
                self.at += (n + 1) // 2
                assert self.at <= ARENA, self.at
                return self.shaped(v, shape)

            @staticmethod
            def shaped(v, shape):
                if len(shape) == 2:
                    return v.rearrange("p (a b) -> p a b", a=shape[0])
                if len(shape) == 3:
                    return v.rearrange("p (a b c) -> p a b c", a=shape[0], b=shape[1])
                return v

        def blocks(ap):
            return ap.rearrange("(b s p) c -> b p s c", s=SUB, p=P)

        def one(view, n):
            return view[bass.ds(n, 1)].rearrange("b p s c -> (b p) s c")

        x_v, x1_v, x2_v, out_v = blocks(d["x"]), blocks(d["x1"]), blocks(d["x2"]), blocks(d["out"])
        cos_v, sin_v = blocks(d["cos"]), blocks(d["sin"])
        xT_v = [d[k].rearrange("(j p) n -> p j n", p=P) for k in ("xT_hi", "xT_lo")]
        cosT_v, sinT_v = (d[k].rearrange("(j p) n -> p j n", p=P) for k in ("cosT", "sinT"))

        def rows(name):
            return d[name].rearrange("(j p) n -> p j n", p=P)

        def tile_of(v, j):
            return v[:, bass.ds(j, 1), :].rearrange("p a c -> p (a c)")

        def row_of(name):
            return d[name].rearrange("(a n) -> a n", a=1).to_broadcast([P, C])

        def mm3(pe, out, w, x, first, last):
            pe.matmul(out, w[0], x[0], start=first, stop=False)
            pe.matmul(out, w[0], x[1], start=False, stop=False)
            return pe.matmul(out, w[1], x[0], start=False, stop=last)

        class Norm:
            def __init__(self, name, x, xn, xT, loaded):
                self.x, self.xn, self.xT, self.loaded = x, xn, xT, loaded
                self.step = sem(name + "_ln_step", "dve")
                self.sd = sem(name + "_ln_sd", "act")
                self.xn_ready = sem(name + "_xn_ready", "dve")
                self.turned = sem(name + "_turned", "pe")
                self.hi = sem(name + "_xT_hi", "act")
                self.lo = sem(name + "_xT_lo", "dve")

            def vector_stats(self, dve, n, par, i):
                self.vector_moments(dve, n, par, i)
                self.vector_rstd(dve, n)

            def vector_moments(self, dve, n, par, i):
                s0 = n * 8
                dve.wait_ge(self.loaded[par], 16 * i + 16)
                for s in range(SUB):
                    last = nc.vector.bn_stats(stats_v[:, s, :], self.x[par][:, s, :])
                last.then_inc(self.step, 1)
                dve.wait_ge(self.step, HEAD + s0 + 1)
                nc.vector.memset(ve[:, :], EPS)
                for s in range(SUB):
                    last = nc.vector.bn_aggr(mv_v[:, s, :], stats_v[:, s, :])
                last.then_inc(self.step, 1)
                dve.wait_ge(self.step, HEAD + s0 + 2)
                nc.vector.tensor_tensor(ve[:, :], mv_v[:, :, 1], ve[:, :], ALU.add).then_inc(self.step, 1)

            def vector_rstd(self, dve, n):
                s0 = n * 8
                dve.wait_ge(self.sd, HEAD + n + 1)
                nc.vector.reciprocal(r0[:, :], sd[:, :]).then_inc(self.step, 1)
                dve.wait_ge(self.step, HEAD + s0 + 4)
                nc.vector.tensor_tensor(r1[:, :], r0[:, :], r0[:, :], ALU.mult).then_inc(self.step, 1)
                dve.wait_ge(self.step, HEAD + s0 + 5)
                nc.vector.tensor_tensor(r1[:, :], r1[:, :], ve[:, :], ALU.mult).then_inc(self.step, 1)
                dve.wait_ge(self.step, HEAD + s0 + 6)
                nc.vector.tensor_scalar(r1[:, :], r1[:, :], -0.5, 1.5, ALU.mult, ALU.add).then_inc(self.step, 1)
                dve.wait_ge(self.step, HEAD + s0 + 7)
                nc.vector.tensor_tensor(rstd[:, :], r0[:, :], r1[:, :], ALU.mult).then_inc(self.step, 1)
                dve.wait_ge(self.step, HEAD + s0 + 8)

            def vector_xn(self, par):
                for s in range(SUB):
                    nc.vector.tensor_scalar(self.xn[par][:, s, :], self.x[par][:, s, :], mv_v[:, s, 0:1],
                                            rstd[:, s:s + 1], ALU.subtract, ALU.mult).then_inc(self.xn_ready, 1)

            def scalar_sd(self, act, n):
                act.wait_ge(self.step, HEAD + n * 8 + 3)
                nc.scalar.activation(sd[:, :], ve[:, :], ACT.Sqrt).then_inc(self.sd, 1)

            def tensor_turn(self, pe, n, par):
                for s in range(SUB):
                    pe.wait_ge(self.xn_ready, HEAD + n * 4 + s + 1)
                    for j in range(CT):
                        last = pe.transpose(bank[4 + j][:, s * P:(s + 1) * P],
                                            self.xn[par][:, s, j * P:(j + 1) * P], ident[:, :])
                last.then_inc(self.turned, 1)

            def scalar_hi(self, act, n, par):
                act.wait_ge(self.turned, HEAD + n + 1)
                for j in range(CT):
                    nc.scalar.activation(self.xT[par][0][:, j, :], bank[4 + j][:, :], ACT.Copy).then_inc(self.hi, 1)

            def vector_lo(self, dve, n, par):
                for j in range(CT):
                    dve.wait_ge(self.hi, HEAD + n * 4 + j + 1)
                    nc.vector.tensor_tensor(self.xT[par][1][:, j, :], bank[4 + j][:, :],
                                            self.xT[par][0][:, j, :], ALU.subtract).then_inc(self.lo, 1)

        a = Carve()
        a_wraw = a.f32(CT, C)
        a_w = (a.f16(CT, C), a.f16(CT, C))
        a_x = [a.f32(SUB, C) for _ in range(2)]
        a_xn = [a.f32(SUB, C) for _ in range(2)]
        a_xT = [(a.f16(CT, T), a.f16(CT, T)) for _ in range(2)]
        a_cos = [a.f32(SUB, HALF) for _ in range(2)]
        a_sin = [a.f32(SUB, HALF) for _ in range(2)]
        a_bias = a.f32(C)
        a_pre = [a.f32(C) for _ in range(2)]
        a_exp = [a.f32(C) for _ in range(2)]
        a_relu = [a.f32(C) for _ in range(2)]
        a_k = [a.f32(C) for _ in range(SUB)]
        a_rc = [a.f32(C) for _ in range(2)]
        a_rs = [a.f32(C) for _ in range(2)]
        a_kr = [a.f32(C) for _ in range(SUB)]
        zeros16 = a.f16(512)
        A_END = 30720
        assert a.at <= A_END
        a_xload = [sem(f"a_xload{u}", None) for u in range(2)]
        a_tabs = [sem(f"a_tabs{u}", None) for u in range(2)]
        a_wload = sem("a_wload", None)
        a_consts = sem("a_consts", "pool")
        a_eye = sem("a_eye", "pool")
        a_whi = sem("a_whi", "act")
        a_wlo = sem("a_wlo", "dve")
        a_store = [sem(f"a_store{u}", "sp") for u in range(2)]
        a_edge = sem("a_edge", None)
        a_kps = sem("a_kps", "pe")
        a_predone = sem("a_predone", "dve")
        a_acts = sem("a_acts", "act")
        a_kdone = sem("a_kdone", "dve")
        a_rot = sem("a_rot", "pool")
        a_krdone = sem("a_krdone", "dve")
        a_kvdone = sem("a_kvdone", "pe")
        A = Norm("a", a_x, a_xn, a_xT, a_xload)

        top = Carve(A_END)
        b_w = (top.f16(CT, C), top.f16(CT, C))
        b_lw = (top.f16(3 * CT, C), top.f16(3 * CT, C))
        raw_at = top.at
        b_wraw = top.f32(CT, C)
        b_lraw = top.f32(3 * CT, C)
        b_xT0 = (top.f16(CT, HALO), top.f16(CT, HALO))
        f_sign0 = top.f16(4 * C)
        s_bo = top.f32(C)
        s_bq = top.f32(4)
        s_bv = top.f32(4)
        b = Carve()
        b_xT = [b_xT0, (b.f16(CT, HALO), b.f16(CT, HALO))]
        b_x = [b.f32(SUB, C) for _ in range(2)]
        b_cos = [b.f32(2, T) for _ in range(2)]
        b_sin = [b.f32(2, T) for _ in range(2)]
        b_exp = [b.f32(T) for _ in range(2)]
        b_relu = [b.f32(T) for _ in range(2)]
        b_q = b.f32(4, T)
        b_qr = b.f32(4, T)
        b_ec, b_oc = b_qr[:, 0:2, :], b_qr[:, 2:4, :]
        b_os = b.f32(2, T)
        b_es = b.f32(2, T)
        b_kv = b.f32(4, P)
        b_km = b.f32(4, NH)
        b_bq = b.f32(4)
        b_lrow = b.f32(C)
        b_den = b.f32(SUB, NH)
        b_z = b.f32(SUB, NH)
        b_t = [b.f32(C) for _ in range(2)]
        f_sum = [b.f32(4 * C) for _ in range(2)]
        f_sum_end = b.at
        f_raw = [b.f32(4 * C) for _ in range(2)]
        f_signs = [f_sign0, b.f16(4 * C)]
        assert b.at <= A_END
        b_qwlo = sem("b_qwlo", "dve")
        b_qwhi = sem("b_qwhi", "act")
        b_qload = sem("b_qload", None)
        b_lowload = sem("b_lowload", None)
        b_xT_load = [sem(f"b_xT_load{u}", None) for u in range(2)]
        d_bload = sem("d_bload", None)
        b_wload = sem("b_wload", None)
        b_whi = sem("b_whi", "act")
        b_wlo = sem("b_wlo", "dve")
        b_kvset = sem("b_kvset", "dve")
        b_load = [sem(f"b_load{u}", None) for u in range(2)]
        b_qps = sem("b_qps", "pe")
        b_acts = sem("b_acts", "act")
        b_qdone = sem("b_qdone", "dve")
        b_mdve = sem("b_mdve", "dve")
        b_mpool = sem("b_mpool", "pool")
        b_rope = sem("b_rope", "dve")
        b_zps = sem("b_zps", "pe")
        b_zstep = sem("b_zstep", "dve")
        b_lps = sem("b_lps", "pe")
        b_aps = sem("b_aps", "pe")
        b_xb = sem("b_xb", "pool")
        b_tstep = sem("b_tstep", "dve")
        b_x1 = sem("b_x1", "dve")
        b_store = [sem(f"b_store{u}", "sp") for u in range(2)]

        kvc = Carve()
        kp = (kvc.f16(CT, KT * P), kvc.f16(CT, KT * P))
        vp = (kvc.f16(KT, C), kvc.f16(KT, C))
        assert f_sum_end <= kvc.at
        s = Carve(kvc.at)
        s_A = (s.f16(CT, C), s.f16(CT, C))
        s_B = (s.f16(CT, C), s.f16(CT, C))
        s_ctxp = [(s.f16(CT, T), s.f16(CT, T)) for _ in range(2)]
        s_ctx0 = s.f32(CT, T)
        s_bvw = s.f32(4, P)
        s_uw = s.f32(4, P)
        s_u = s.f16(4, 2)
        s_kb = s.f32(4)
        s_tv = (s.f16(C), s.f16(C))
        assert s.at <= raw_at
        s_raw = [Carve(raw_at + 2048 * k).f32(CT, C) for k in range(4)]
        s_ctx = [s_ctx0, Carve(raw_at + 8192).f32(CT, T)]
        s_wload = sem("s_wload", None)
        s_prod = sem("s_prod", "pe")
        s_hi = sem("s_hi", "act")
        s_lo = sem("s_lo", "dve")
        s_uwd = sem("s_uwd", "dve")
        s_tps = sem("s_tps", "pe")
        s_thi = sem("s_thi", "act")
        s_tlo = sem("s_tlo", "dve")
        s_tst = sem("s_tst", "sp")
        s_tbias = sem("s_tbias", "dve")
        tail_k_v = tail_k[:, :].rearrange("p (j k) -> p j k", j=CT)
        s_bvw_ok = sem("s_bvw_ok", "dve")
        s_load = [sem(f"s_load{u}", None) for u in range(2)]
        s_chi = sem("s_chi", "act")
        s_clo = sem("s_clo", "dve")
        s_kps = sem("s_kps", "pe")
        s_khi = sem("s_khi", "act")
        s_klo = sem("s_klo", "dve")
        s_vps = sem("s_vps", "pe")
        s_vhi = sem("s_vhi", "act")
        s_vlo = sem("s_vlo", "dve")
        s_bps = sem("s_bps", "pe")
        s_kbs = sem("s_kbs", "dve")
        f_load = [sem(f"f_load{u}", None) for u in range(2)]
        f_sign = sem("f_sign", "act")
        f_abs = sem("f_abs", "act")
        f_add = sem("f_add", "dve")
        f_store = [sem(f"f_store{u}", "act") for u in range(2)]
        f_aps = sem("f_aps", "pe")
        f_alpha = sem("f_alpha", "dve")

        c = Carve(kvc.at)
        c_S = c.f32(KT, T)
        c_xT = [(c.f16(CT, T), c.f16(CT, T))] * 2
        c_x = [c.f32(SUB, C) for _ in range(2)]
        c_xn = [c.f32(SUB, C)] * 2
        c_ph = [c.f16(T) for _ in range(RING)]
        c_diag = Carve(c.at).f32(SUB, P)
        c_pl = [c.f16(T) for _ in range(RING)]
        c_mx = c.f32(T)
        c_mb = c_mx
        c_sum = c.f32(T)
        c_mcol = c.f32(SUB)
        c_mtile = c.f32(SUB)
        c_rinv = c.f32(SUB)
        c_den = c.f32(SUB)
        c_ts = c.f32(SUB, KX)
        c_tmax = c.f32(SUB)
        c_td = c.f32(SUB, KX)
        c_tp = c.f32(SUB, KX)
        c_tsum = c.f32(SUB)
        c_th = c.f16(SUB, KX)
        c_t3 = c.f32(SUB, 3 * KX)
        c_tT = c.f16(T)
        c_tsc = sem("c_tsc", "pe")
        c_tstep = sem("c_tstep", "dve")
        c_texp = sem("c_texp", "act")
        c_ttr = sem("c_ttr", "pe")
        c_tTd = sem("c_tTd", "act")
        c_load = [sem(f"c_load{u}", None) for u in range(2)]
        c_qk = sem("c_qk", "pe")
        c_s = sem("c_s", "act")
        c_max = sem("c_max", "dve")
        c_mt = sem("c_mt", "pe")
        c_mstep = sem("c_mstep", "dve")
        c_mps = sem("c_mps", "pe")
        c_mbd = sem("c_mbd", "dve")
        c_sub = sem("c_sub", "dve")
        c_exp = sem("c_exp", "act")
        c_hi = sem("c_hi", "dve")
        c_lo = sem("c_lo", "dve")
        c_pv = sem("c_pv", "pe")
        c_add = sem("c_add", "pool")
        c_rs = sem("c_rs", "pe")
        c_ri = sem("c_ri", "dve")
        c_xb = sem("c_xb", "pool")
        c_x2 = sem("c_x2", "dve")
        c_store = [sem(f"c_store{u}", "sp") for u in range(2)]
        Cn = Norm("c", c_x, c_xn, c_xT, c_load)

        e = Carve()
        d_w1 = e.f16(CT, H)
        d_w2 = e.f16(HT, C)
        d_x0 = e.f32(SUB, C)
        d_xn = [e.f32(SUB, C)] * 2
        assert e.at <= CT * KT * P
        e = Carve(kvc.at)
        d_xT = [(e.f16(CT, T), e.f16(CT, T))] * 2
        d_gh = e.f16(HT, T)
        d_gl = e.f16(HT, T)
        d_g = [e.f32(T) for _ in range(2)]
        d_t = [e.f32(C) for _ in range(2)]
        d_b2 = e.f32(C)
        assert e.at <= kvc.at + KT * T
        d_x = [d_x0, Carve(kvc.at + KT * T).f32(SUB, C)]
        d_wload = sem("d_wload", None)
        d_load = [sem(f"d_load{u}", None) for u in range(2)]
        d_hps = sem("d_hps", "pe")
        d_gelu = sem("d_gelu", "act")
        d_ghi = sem("d_ghi", "dve")
        d_glo = sem("d_glo", "dve")
        d_f2 = sem("d_f2", "pe")
        d_ops = sem("d_ops", "pe")
        d_xb = sem("d_xb", "pool")
        d_ts = sem("d_ts", "dve")
        d_out = sem("d_out", "dve")
        d_store = [sem(f"d_store{u}", "sp") for u in range(2)]
        Dn = Norm("d", d_x, d_xn, d_xT, d_load)

        def after_a(eng):
            eng.wait_ge(a_kvdone, HEAD + 4 * NB)
            eng.wait_ge(a_krdone, HEAD + 4 * NB)
            for u in range(2):
                eng.wait_ge(a_store[u], HEAD + 16 * NB)

        def after_b(eng):
            eng.wait_ge(b_x1, HEAD + 4 * NB)
            eng.wait_ge(b_lps, HEAD + 4 * NB)
            eng.wait_ge(b_aps, HEAD + 4 * NB)
            for u in range(2):
                eng.wait_ge(b_store[u], HEAD + 16 * NB // 2)
                eng.wait_ge(f_store[u], HEAD + 16 * NB // 2)

        CH = M // T

        def after_s(eng):
            eng.wait_ge(s_klo, HEAD + 4 * (CH + 1))
            eng.wait_ge(s_vlo, HEAD + KT)
            eng.wait_ge(s_kbs, HEAD + 2 * (CH + 1))
            eng.wait_ge(s_tlo, HEAD + 4)
            eng.wait_ge(s_tst, HEAD + 48)
            eng.wait_ge(f_alpha, HEAD + 3)

        def after_scores(eng):
            eng.wait_ge(c_lo, HEAD + KT * NB)
            eng.wait_ge(c_add, HEAD + (KT - 1) * NB)

        block = ctx.enter_context(nc.Block())

        @block.sync
        def _(sp):
            start("sp", sp)

            def pair_loop(body):
                with sp.Fori(0, NB // 2 - 1) as i:
                    body(i, False)
                body(NB // 2 - 1, True)

            def load_tables(n, u):
                sp.dma_start(a_cos[u], one(cos_v, n)).then_inc(a_tabs[u], 16)
                sp.dma_start(a_sin[u], one(sin_v, n)).then_inc(a_tabs[u], 16)

            sp.dma_start(a_x[0], one(x_v, 0)).then_inc(a_xload[0], 16)
            sp.dma_start(a_wraw, rows("wk_rope")).then_inc(a_wload, 16)
            sp.dma_start(a_bias, row_of("bk_rope")).then_inc(a_wload, 16)
            sp.dma_start(a_cos[0], one(cos_v, 0)).then_inc(a_tabs[0], 16)
            sp.dma_start(a_sin[0], one(sin_v, 0)).then_inc(a_tabs[0], 16)
            sp.dma_start(a_x[1], one(x_v, 1)).then_inc(a_xload[1], 16)
            sp.dma_start(b_lraw, d["lepe_w"].rearrange("(j p) n -> p j n", p=P)).then_inc(b_wload, 16)
            sp.wait_ge(a_consts, HEAD + 1)
            for v in xT_v:
                for col in (0, EDGE + N):
                    sp.dma_start(v[:, :, col:col + EDGE],
                                 zeros16[:, 0:CT * EDGE].rearrange("p (j o) -> p j o", j=CT)).then_inc(a_edge, 16)

            sp.dma_start(b_wraw, rows("wq_rope")).then_inc(b_qload, 16)

            def store_xT(n, u):
                sp.wait_ge(A.lo, HEAD + 4 * n + 4)
                for k in range(2):
                    sp.dma_start(xT_v[k][:, :, bass.ds(n * T + EDGE, T)], a_xT[u][k]).then_inc(a_store[u], 16)

            store_xT(0, 0)

            def body_a(i, last):
                for u in range(2):
                    n = 2 * i + u
                    if not last:
                        sp.wait_ge(A.xn_ready, HEAD + 4 * n + 4)
                        sp.dma_start(a_x[u], one(x_v, n + 2)).then_inc(a_xload[u], 16)
                    if not (last and u):
                        sp.wait_ge(a_krdone, HEAD + 4 * n)
                        load_tables(n + 1, 1 - u)
                        store_xT(n + 1, 1 - u)

            pair_loop(body_a)

            sp.wait_ge(a_edge, 64)
            sp.wait_ge(a_store[0], HEAD + 32)
            sp.wait_ge(a_store[1], HEAD + 32)

            def load_b(n, u):
                for k in range(2):
                    sp.dma_start(b_xT[u][k], xT_v[k][:, :, bass.ds(n * T + EDGE - 1, HALO)]).then_inc(b_xT_load[u], 16)
                sp.dma_start(b_cos[u], cosT_v[:, :, bass.ds(n * T, T)]).then_inc(b_load[u], 16)
                sp.dma_start(b_sin[u], sinT_v[:, :, bass.ds(n * T, T)]).then_inc(b_load[u], 16)
                sp.dma_start(b_x[u], one(x_v, n)).then_inc(b_load[u], 16)

            for k in range(2):
                sp.dma_start(b_xT[0][k], xT_v[k][:, :, EDGE - 1:EDGE - 1 + HALO]).then_inc(b_xT_load[0], 16)
            after_a(sp)
            sp.dma_start(b_bq, d["bq_rope"]).then_inc(b_lowload, 16)
            sp.dma_start(b_cos[0], cosT_v[:, :, 0:T]).then_inc(b_load[0], 16)
            sp.dma_start(b_sin[0], sinT_v[:, :, 0:T]).then_inc(b_load[0], 16)
            sp.dma_start(b_x[0], one(x_v, 0)).then_inc(b_load[0], 16)
            sp.dma_start(b_lrow, row_of("lepe_b")).then_inc(b_lowload, 16)

            def body_b(i, last):
                for u in range(2):
                    n = 2 * i + u
                    if not (last and u):
                        sp.wait_ge(b_aps, HEAD + 4 * n)
                        sp.wait_ge(b_lps, HEAD + 4 * n)
                        sp.wait_ge(b_store[1 - u], HEAD + 16 * (i + u))
                        load_b(n + 1, 1 - u)
                    if last and u == 0:
                        for k, name in enumerate(("xk", "xq", "xv", "xoT")):
                            sp.dma_start(s_raw[k], rows(name)).then_inc(s_wload, 16)
                        sp.dma_start(s_bq, d["xbq"]).then_inc(s_wload, 16)
                        sp.dma_start(s_bv, d["xbv"]).then_inc(s_wload, 16)
                        sp.dma_start(s_bo, row_of("xbo")).then_inc(s_wload, 16)
                    sp.wait_ge(b_x1, HEAD + 4 * n + 4)
                    sp.dma_start(one(x1_v, n), b_x[u]).then_inc(b_store[u], 16)

            pair_loop(body_b)

            after_b(sp)
            ctxT_v = rows("ctxT")

            def load_s(n, u):
                sp.dma_start(s_ctx[u], ctxT_v[:, :, bass.ds(n * T, T)]).then_inc(s_load[u], 16)

            load_s(0, 0)
            load_s(1, 1)
            with sp.Fori(0, CH // 2 - 1) as i:
                sp.wait_ge(s_clo, HEAD + 8 * i + 4)
                load_s(2 * i + 2, 0)
                sp.wait_ge(s_clo, HEAD + 8 * i + 8)
                load_s(2 * i + 3, 1)
            sp.wait_ge(s_prod, HEAD + 10)

            def load_c(n, u):
                sp.dma_start(c_x[u], one(x1_v, n)).then_inc(c_load[u], 16)

            load_c(0, 0)
            sp.wait_ge(s_clo, HEAD + 4 * (CH - 1))
            sp.dma_start(s_ctx[0][:, :, 0:M - CH * T], ctxT_v[:, :, CH * T:M]).then_inc(s_load[0], 16)
            sp.wait_ge(s_tlo, HEAD + 4)
            for k, part in enumerate((0, 1, 0)):
                sp.dma_start(tail_v[k * KX:(k + 1) * KX, :], s_tv[part][0:KX, :]).then_inc(s_tst, 16)

            after_s(sp)

            def body_c(i, last):
                for u in range(2):
                    n = 2 * i + u
                    if not (last and u):
                        sp.wait_ge(c_store[1 - u], HEAD + 16 * (i + u))
                        load_c(n + 1, 1 - u)
                    if last and u:
                        sp.wait_ge(c_qk, HEAD + KT * NB)
                        sp.dma_start(d_x[0], one(x2_v, 0)).then_inc(d_load[0], 16)
                        signs = d["signs"].rearrange("(g w) p n -> w p g n", w=2)
                        sp.dma_start(d_w1, signs[0]).then_inc(d_wload, 16)
                        sp.dma_start(d_w2.rearrange("p (g k) n -> p g (k n)", g=4), signs[1]).then_inc(d_wload, 16)
                    sp.wait_ge(c_x2, HEAD + 4 * n + 4)
                    sp.dma_start(one(x2_v, n), c_x[u]).then_inc(c_store[u], 16)

            pair_loop(body_c)

            after_scores(sp)
            sp.dma_start(d_b2, row_of("b2")).then_inc(d_bload, 16)

            def load_d(n, u):
                sp.dma_start(d_x[u], one(x2_v, n)).then_inc(d_load[u], 16)

            def body_d(i, last):
                for u in range(2):
                    n = 2 * i + u
                    if not (last and u):
                        sp.wait_ge(d_store[1 - u], HEAD + 16 * (i + u))
                        load_d(n + 1, 1 - u)
                    sp.wait_ge(d_out, HEAD + 4 * n + 4)
                    sp.dma_start(one(out_v, n), d_x[u]).then_inc(d_store[u], 16)

            for u in range(2):
                sp.wait_ge(c_store[u], HEAD + 16 * NB // 2)
            pair_loop(body_d)
            for u in range(2):
                sp.wait_ge(d_store[u], HEAD + 16 * NB // 2)

        @block.gpsimd
        def _(pool):
            nc.gpsimd.memset(zeros16, 0.0).then_inc(a_consts, 1)
            start("pool", pool)
            nc.gpsimd.memset(ident[:, :], 0.0).then_inc(a_eye, 1)
            nc.gpsimd.memset(ones[:, :], 1.0).then_inc(a_eye, 1)
            pool.wait_ge(a_eye, HEAD + 2)
            nc.gpsimd.affine_select(out=ident[:, :], in_=ident[:, :], compare_op=ALU.not_equal, fill=1.0,
                                    base=0, pattern=[[-1, P]], channel_multiplier=1).then_inc(a_eye, 1)

            def pair_loop(body):
                with pool.Fori(0, NB // 2 - 1) as i:
                    body(i, False)
                body(NB // 2 - 1, True)

            def body_a(i, last):
                for u in range(2):
                    n = 2 * i + u
                    pool.wait_ge(a_tabs[u], 32 * i + 32)
                    for t in range(SUB):
                        pool.wait_ge(a_kdone, HEAD + 4 * n + t + 1)
                        pool.wait_ge(a_krdone, HEAD + 4 * n + t - 1)
                        k2 = a_k[t].rearrange("p (h c) -> p h c", h=2)
                        tab = a_cos[u][:, t, :].rearrange("p (o c) -> p o c", o=1).to_broadcast([P, 2, HALF])
                        nc.gpsimd.tensor_tensor(a_rc[t % 2].rearrange("p (h c) -> p h c", h=2), k2, tab, ALU.mult)
                        nc.gpsimd.tensor_tensor(a_rs[t % 2][:, 0:HALF], a_k[t][:, HALF:C], a_sin[u][:, t, :], ALU.mult)
                        nc.gpsimd.tensor_tensor(a_rs[t % 2][:, HALF:C], a_k[t][:, 0:HALF], a_sin[u][:, t, :],
                                                ALU.mult).then_inc(a_rot, 1)

            pair_loop(body_a)

            after_a(pool)
            pool.wait_ge(b_lowload, 32)

            def body_b(i, last):
                for u in range(2):
                    n = 2 * i + u
                    pool.wait_ge(f_add, HEAD + n - 1)
                    pool.dma_start(f_raw[u], d["ffn_w"][bass.ds(n, 1)].rearrange("g p n -> (g p) n")).then_inc(f_load[u], 16)
                    pool.wait_ge(b_load[u], 48 * i + 48)
                    for t in range(SUB):
                        nc.gpsimd.tensor_tensor(b_x[u][:, t, :], b_x[u][:, t, :], b_lrow, ALU.add).then_inc(b_xb, 1)
                    pool.wait_ge(b_qdone, HEAD + 4 * n + 4)
                    pool.wait_ge(b_rope, HEAD + 2 * n)
                    pool.wait_ge(b_aps, HEAD + 4 * n)
                    nc.gpsimd.tensor_tensor(b_oc, b_q[:, 2:4, :], b_cos[u], ALU.mult)
                    nc.gpsimd.tensor_tensor(b_es, b_q[:, 0:2, :], b_sin[u], ALU.mult).then_inc(b_mpool, 1)

            pair_loop(body_b)

            after_s(pool)

            def body_c(i, last):
                for u in range(2):
                    n = 2 * i + u
                    pool.wait_ge(Cn.xn_ready, HEAD + 4 * n + 4)
                    for t in range(SUB):
                        nc.gpsimd.tensor_tensor(c_x[u][:, t, :], c_x[u][:, t, :], attn_row[:, :], ALU.add).then_inc(c_xb, 1)
                    pool.wait_ge(c_rs, HEAD + n)
                    for t in range(1, KT):
                        pool.wait_ge(c_exp, HEAD + KT * n + t + 1)
                        if t == 1:
                            nc.gpsimd.tensor_tensor(c_sum, c_S[:, 0, :], c_S[:, 1, :], ALU.add).then_inc(c_add, 1)
                        else:
                            pool.wait_ge(c_add, HEAD + (KT - 1) * n + t - 1)
                            nc.gpsimd.tensor_tensor(c_sum, c_sum, c_S[:, t, :], ALU.add).then_inc(c_add, 1)

            pair_loop(body_c)

            pool.wait_ge(d_bload, 16)

            def body_d(i, last):
                for u in range(2):
                    n = 2 * i + u
                    pool.wait_ge(Dn.xn_ready, HEAD + 4 * n + 4)
                    for t in range(SUB):
                        nc.gpsimd.tensor_tensor(d_x[u][:, t, :], d_x[u][:, t, :], d_b2, ALU.add).then_inc(d_xb, 1)

            pair_loop(body_d)

        @block.scalar
        def _(act):
            start("act", act)
            act.dma_start(b1_col[:, :], d["b1"]).then_inc(a_wload, 16)

            def pair_loop(body):
                with act.Fori(0, NB // 2 - 1) as i:
                    body(i, False)
                body(NB // 2 - 1, True)

            A.scalar_sd(act, 0)
            act.wait_ge(a_wload, 48)
            for j in range(CT):
                nc.scalar.activation(a_w[0][:, j, :], a_wraw[:, j, :], ACT.Copy, scale=WS).then_inc(a_whi, 1)
            A.scalar_hi(act, 0, 0)

            A.scalar_sd(act, 1)

            def weights_hi(n, last):
                for k in range(2):
                    if last:
                        j = 2 * (n - (NB - 2)) + k
                        nc.scalar.activation(b_w[0][:, j, :], b_wraw[:, j, :], ACT.Copy, scale=WS).then_inc(b_qwhi, 1)
                    else:
                        nc.scalar.activation(tile_of(b_lw[0], 2 * n + k), tile_of(b_lraw, 2 * n + k), ACT.Copy,
                                             scale=WS).then_inc(b_whi, 1)

            def act_a(n, t):
                act.wait_ge(a_predone, HEAD + 4 * n + t + 1)
                act.wait_ge(a_kdone, HEAD + 4 * n + t - 1)
                nc.scalar.activation(a_exp[t % 2], a_pre[t % 2], ACT.Exp)
                nc.scalar.activation(a_relu[t % 2], a_pre[t % 2], ACT.Relu).then_inc(a_acts, 1)

            act_a(0, 0)
            act_a(0, 1)

            def body_a(i, last):
                if last:
                    act.wait_ge(b_qload, 16)
                else:
                    act.wait_ge(b_wload, 16)
                for u in range(2):
                    n = 2 * i + u
                    more = not (last and u)
                    act_a(n, 2)
                    if more:
                        act.wait_ge(a_kps, HEAD + 4 * n)
                        act.wait_ge(a_store[1 - u], HEAD + 32 * (i + u))
                        A.scalar_hi(act, n + 1, 1 - u)
                    weights_hi(n, last)
                    act_a(n, 3)
                    if not last:
                        A.scalar_sd(act, n + 2)
                    if more:
                        act_a(n + 1, 0)
                        act_a(n + 1, 1)

            pair_loop(body_a)

            after_a(act)
            act.wait_ge(b_lowload, 32)

            def body_b(i, last):
                for u in range(2):
                    n = 2 * i + u
                    for t in range(4):
                        act.wait_ge(b_qps, HEAD + 4 * n + t + 1)
                        act.wait_ge(b_qdone, HEAD + 4 * n + t - 1)
                        nc.scalar.activation(b_exp[t % 2], bank[t % 2][:, :], ACT.Exp, bias=b_bq[:, t:t + 1], scale=1 / WS)
                        nc.scalar.activation(b_relu[t % 2], bank[t % 2][:, :], ACT.Relu, bias=b_bq[:, t:t + 1],
                                             scale=1 / WS).then_inc(b_acts, 1)
                    act.wait_ge(f_store[u], HEAD + 16 * i)
                    act.wait_ge(f_load[u], 16 * i + 16)
                    nc.scalar.activation(f_signs[u], f_raw[u], ACT.Sign).then_inc(f_sign, 1)
                    nc.scalar.activation(f_raw[u], f_raw[u], ACT.Abs).then_inc(f_abs, 1)
                    act.wait_ge(f_sign, HEAD + n + 1)
                    act.dma_start(d["signs"][bass.ds(n, 1)].rearrange("g p n -> (g p) n"), f_signs[u]).then_inc(f_store[u], 16)

            pair_loop(body_b)

            after_b(act)
            for m in range(8):
                act.wait_ge(s_prod, HEAD + m + 1 + (m > 3))
                dst = s_A if m < 4 else s_B
                nc.scalar.activation(dst[0][:, m % 4, :], bank[m % 4][:, :], ACT.Copy, scale=WS).then_inc(s_hi, 1)
                if m == 3:
                    act.wait_ge(s_prod, HEAD + 5)
                    nc.scalar.activation(s_u[:, :, 0], bank[6][:, 0:4], ACT.Copy, scale=WS).then_inc(s_hi, 1)

            def ctx_hi(n, u, i, w):
                act.wait_ge(s_load[u], 16 * i + 16)
                act.wait_ge(s_vps, HEAD + 4 * n - 4)
                for j in range(CT):
                    nc.scalar.activation(s_ctxp[u][0][:, j, 0:w], s_ctx[u][:, j, 0:w], ACT.Copy).then_inc(s_chi, 1)

            def kprime_hi(n, w):
                for j in range(CT):
                    act.wait_ge(s_kps, HEAD + 4 * n + j + 1)
                    if w < T:
                        nc.scalar.activation(tail_k_v[:, j, 0:KX], bank[j][:, w:w + KX], ACT.Copy, scale=1 / WS)
                    nc.scalar.activation(kp[0][:, j, bass.ds(n * T, w)], bank[j][:, 0:w], ACT.Copy, scale=1 / WS).then_inc(s_khi, 1)

            def vprime_hi(n, nt):
                for q in range(nt):
                    act.wait_ge(s_vps, HEAD + 4 * n + q + 1)
                    nc.scalar.activation(vp[0][:, bass.ds(4 * n + q, 1), :].rearrange("p a c -> p (a c)"),
                                         bank[4 + q % 2][:, :], ACT.Copy, scale=1 / WS).then_inc(s_vhi, 1)

            ctx_hi(0, 0, 0, T)

            def body_s(i, last):
                for u in range(2):
                    n = 2 * i + u
                    kprime_hi(n, T)
                    ctx_hi(n + 1, 1 - u, i + u, M - CH * T if last and u else T)
                    vprime_hi(n, 4)

            with act.Fori(0, CH // 2 - 1) as i:
                body_s(i, False)
            body_s(CH // 2 - 1, True)
            kprime_hi(CH, P)
            vprime_hi(CH, 1)
            act.wait_ge(s_tps, HEAD + 1)
            nc.scalar.activation(s_tv[0][0:KX, :], bank[5][0:KX, :], ACT.Copy, scale=1 / WS).then_inc(s_thi, 1)

            Cn.scalar_sd(act, 0)
            Cn.scalar_hi(act, 0, 0)
            after_s(act)

            def evac_scores(n):
                for t in range(KT):
                    act.wait_ge(c_qk, HEAD + KT * n + t + 1)
                    act.wait_ge(c_lo, HEAD + KT * n + t + 1 - KT)
                    act.wait_ge(c_add, HEAD + (KT - 1) * n + t + 1 - KT + (1 if t == 0 else 0))
                    nc.scalar.activation(c_S[:, t, :], bank[4 + t % 3][:, :], ACT.Identity,
                                         bias=key_bias[:, t:t + 1]).then_inc(c_s, 1)

            def exp(n, t):
                act.wait_ge(c_sub, HEAD + KT * n + t + 1)
                nc.scalar.activation(c_S[:, t, :], c_S[:, t, :], ACT.Exp, scale=SCALE).then_inc(c_exp, 1)

            evac_scores(0)
            exp(0, 0)
            exp(0, 1)

            def body_c(i, last):
                for u in range(2):
                    n = 2 * i + u
                    more = not (last and u)
                    nxt, nn = (Cn, n + 1) if more else (Dn, 0)
                    for t in range(2, KT):
                        if t == 4:
                            act.wait_ge(c_tstep, HEAD + 7 * n + 4)
                            nc.scalar.activation(c_tp, c_td, ACT.Exp, scale=SCALE).then_inc(c_texp, 1)
                        if t == 7:
                            nxt.scalar_sd(act, nn)
                        if t == 11:
                            act.wait_ge(c_ttr, HEAD + n + 1)
                            nc.scalar.activation(c_tT[0:3 * KX, :], bank[5][0:3 * KX, :], ACT.Copy).then_inc(c_tTd, 1)
                        if t == 19:
                            if not more:
                                act.wait_ge(c_lo, HEAD + KT * n + 4)
                                act.wait_ge(c_add, HEAD + (KT - 1) * n + 3)
                            nxt.scalar_hi(act, nn, 0)
                        exp(n, t)
                    if more:
                        evac_scores(n + 1)
                        exp(n + 1, 0)
                        exp(n + 1, 1)

            pair_loop(body_c)

            after_scores(act)

            def body_d(i, last):
                for u in range(2):
                    n = 2 * i + u
                    more = not (last and u)
                    for t in range(HT):
                        if more and t == 8:
                            Dn.scalar_sd(act, n + 1)
                        act.wait_ge(d_hps, HEAD + HT * n + t + 1)
                        act.wait_ge(d_glo, HEAD + HT * n + t - 1)
                        nc.scalar.activation(d_g[t % 2], bank[4 + t % 4][:, :], ACT.Gelu, bias=b1_col[:, t:t + 1],
                                             scale=alpha1[:, t:t + 1]).then_inc(d_gelu, 1)
                    if more:
                        Dn.scalar_hi(act, n + 1, 0)

            pair_loop(body_d)

        @block.vector
        def _(dve):
            start("dve", dve)

            def pair_loop(body):
                with dve.Fori(0, NB // 2 - 1) as i:
                    body(i, False)
                body(NB // 2 - 1, True)

            def lo_part(out, src, hi, scale):
                return nc.vector.scalar_tensor_tensor(out=out, in0=src, scalar=scale, in1=hi,
                                                      op0=ALU.mult, op1=ALU.subtract)

            A.vector_stats(dve, 0, 0, 0)
            A.vector_xn(0)
            dve.wait_ge(a_wload, 48)
            for j in range(CT):
                dve.wait_ge(a_whi, HEAD + j + 1)
                lo_part(a_w[1][:, j, :], a_wraw[:, j, :], a_w[0][:, j, :], WS).then_inc(a_wlo, 1)
            A.vector_lo(dve, 0, 0)

            def pre_a(n, t):
                dve.wait_ge(a_kps, HEAD + 4 * n + t + 1)
                dve.wait_ge(a_acts, HEAD + 4 * n + t - 1)
                nc.vector.scalar_tensor_tensor(out=a_pre[t % 2], in0=bank[t % 2][:, :], scalar=1 / WS,
                                               in1=a_bias, op0=ALU.mult, op1=ALU.add).then_inc(a_predone, 1)

            def elu_a(n, t):
                dve.wait_ge(a_acts, HEAD + 4 * n + t + 1)
                dve.wait_ge(a_kvdone, HEAD + 4 * n + t - 3)
                nc.vector.scalar_tensor_tensor(out=a_k[t], in0=a_exp[t % 2], scalar=1.0, in1=a_relu[t % 2],
                                               op0=ALU.min, op1=ALU.add).then_inc(a_kdone, 1)

            def rope_a(n, t):
                dve.wait_ge(a_rot, HEAD + 4 * n + t + 1)
                nc.vector.tensor_tensor(a_kr[t][:, 0:HALF], a_rc[t % 2][:, 0:HALF], a_rs[t % 2][:, 0:HALF], ALU.subtract)
                nc.vector.tensor_tensor(a_kr[t][:, HALF:C], a_rc[t % 2][:, HALF:C], a_rs[t % 2][:, HALF:C],
                                        ALU.add).then_inc(a_krdone, 1)

            def weights_lo(n, last):
                for k in range(2):
                    if last:
                        j = 2 * (n - (NB - 2)) + k
                        dve.wait_ge(b_qwhi, HEAD + j + 1)
                        lo_part(b_w[1][:, j, :], b_wraw[:, j, :], b_w[0][:, j, :], WS).then_inc(b_qwlo, 1)
                    else:
                        dve.wait_ge(b_whi, HEAD + 2 * n + k + 1)
                        lo_part(tile_of(b_lw[1], 2 * n + k), tile_of(b_lraw, 2 * n + k), tile_of(b_lw[0], 2 * n + k),
                                WS).then_inc(b_wlo, 1)

            A.vector_moments(dve, 1, 1, 0)
            pre_a(0, 0)
            A.vector_rstd(dve, 1)
            elu_a(0, 0)
            pre_a(0, 1)

            def body_a(i, last):
                if last:
                    dve.wait_ge(b_qload, 16)
                else:
                    dve.wait_ge(b_wload, 16)
                for u in range(2):
                    n = 2 * i + u
                    more = not (last and u)
                    if more:
                        dve.wait_ge(a_kvdone, HEAD + 4 * n)
                        A.vector_xn(1 - u)
                    rope_a(n, 0)
                    elu_a(n, 1)
                    pre_a(n, 2)
                    if more:
                        A.vector_lo(dve, n + 1, 1 - u)
                    rope_a(n, 1)
                    elu_a(n, 2)
                    pre_a(n, 3)
                    rope_a(n, 2)
                    elu_a(n, 3)
                    if not last:
                        A.vector_moments(dve, n + 2, u, i + 1)
                    if more:
                        pre_a(n + 1, 0)
                    rope_a(n, 3)
                    if not last:
                        A.vector_rstd(dve, n + 2)
                    if more:
                        elu_a(n + 1, 0)
                        pre_a(n + 1, 1)
                    weights_lo(n, last)

            pair_loop(body_a)

            after_a(dve)
            kv_ps = bank[2][:, :].rearrange("p (t c) -> p t c", t=4)
            nc.vector.memset(b_kv, 0.0).then_inc(b_kvset, 1)
            nc.vector.memset(b_km, 0.0).then_inc(b_kvset, 1)
            dve.wait_ge(b_kvset, HEAD + 2)
            for h in range(2):
                o = h * DH
                nc.vector.tensor_scalar(b_kv[o:o + DH, :, o:o + DH], kv_ps[o:o + DH, :, o:o + DH],
                                        float(N) ** -0.5, None, ALU.mult)
            for g in range(4):
                for t in range(4):
                    last = nc.vector.tensor_scalar(b_km[32 * g:32 * g + 32, t, 4 * (t % 2) + g:4 * (t % 2) + g + 1],
                                                   bank[3][32 * g:32 * g + 32, t:t + 1], 1.0 / N, None, ALU.mult)
            last.then_inc(b_kvset, 1)
            for u in range(2):
                nc.vector.memset(f_sum[u], 0.0).then_inc(b_kvset, 1)
            dve.wait_ge(b_kvset, HEAD + 5)

            def body_b(i, last):
                for u in range(2):
                    n = 2 * i + u
                    dve.wait_ge(b_load[u], 48 * i + 48)
                    dve.wait_ge(b_zps, HEAD + n)
                    dve.wait_ge(b_mpool, HEAD + n)
                    for t in range(4):
                        dve.wait_ge(b_acts, HEAD + 4 * n + t + 1)
                        nc.vector.scalar_tensor_tensor(out=b_q[:, t, :], in0=b_exp[t % 2], scalar=1.0, in1=b_relu[t % 2],
                                                       op0=ALU.min, op1=ALU.add).then_inc(b_qdone, 1)
                    dve.wait_ge(b_qdone, HEAD + 4 * n + 4)
                    dve.wait_ge(b_aps, HEAD + 4 * n)
                    nc.vector.tensor_tensor(b_ec, b_q[:, 0:2, :], b_cos[u], ALU.mult)
                    nc.vector.tensor_tensor(b_os, b_q[:, 2:4, :], b_sin[u], ALU.mult).then_inc(b_mdve, 1)
                    dve.wait_ge(b_mdve, HEAD + n + 1)
                    nc.vector.tensor_tensor(b_qr[:, 0:2, :], b_ec, b_os, ALU.subtract).then_inc(b_rope, 1)
                    dve.wait_ge(b_mpool, HEAD + n + 1)
                    nc.vector.tensor_tensor(b_qr[:, 2:4, :], b_oc, b_es, ALU.add).then_inc(b_rope, 1)
                    dve.wait_ge(b_zps, HEAD + n + 1)
                    nc.vector.tensor_scalar(b_den, bank[6][:, 0:SUB * NH].rearrange("p (s h) -> p s h", s=SUB), 1e-6,
                                            None, ALU.add).then_inc(b_zstep, 1)
                    dve.wait_ge(b_zstep, HEAD + 2 * n + 1)
                    nc.vector.reciprocal(b_z, b_den).then_inc(b_zstep, 1)
                    dve.wait_ge(b_zstep, HEAD + 2 * n + 2)
                    for t in range(SUB):
                        z = b_z[:, t, :].rearrange("p (h o) -> p h o", o=1).to_broadcast([P, NH, DH])
                        dve.wait_ge(b_aps, HEAD + 4 * n + t + 1)
                        nc.vector.tensor_tensor(b_t[t % 2].rearrange("p (h c) -> p h c", h=NH),
                                                bank[2 + t % 2][:, :].rearrange("p (h c) -> p h c", h=NH),
                                                z, ALU.mult).then_inc(b_tstep, 1)
                        dve.wait_ge(b_tstep, HEAD + 8 * n + 2 * t + 1)
                        dve.wait_ge(b_lps, HEAD + 4 * n + t + 1)
                        nc.vector.scalar_tensor_tensor(out=b_t[t % 2], in0=bank[4 + t % 2][:, :], scalar=1 / WS,
                                                       in1=b_t[t % 2], op0=ALU.mult, op1=ALU.add).then_inc(b_tstep, 1)
                        dve.wait_ge(b_tstep, HEAD + 8 * n + 2 * t + 2)
                        dve.wait_ge(b_xb, HEAD + 4 * n + t + 1)
                        nc.vector.tensor_tensor(b_x[u][:, t, :], b_x[u][:, t, :], b_t[t % 2], ALU.add).then_inc(b_x1, 1)
                        if t == 1:
                            dve.wait_ge(f_abs, HEAD + n + 1)
                            dve.wait_ge(f_add, HEAD + n - 1)
                            nc.vector.tensor_tensor(f_sum[u], f_sum[u], f_raw[u], ALU.add).then_inc(f_add, 1)

            pair_loop(body_b)

            dve.wait_ge(s_wload, 7 * 16)
            after_b(dve)
            for j in range(4):
                last = nc.vector.tensor_scalar(s_bvw[:, j, :], ones[:, :], s_bv[:, j:j + 1], None, ALU.mult)
            last.then_inc(s_bvw_ok, 1)
            for m in range(8):
                dve.wait_ge(s_hi, HEAD + m + 1 + (m > 3))
                dst = s_A if m < 4 else s_B
                lo_part(dst[1][:, m % 4, :], bank[m % 4][:, :], dst[0][:, m % 4, :], WS).then_inc(s_lo, 1)
                if m == 3:
                    dve.wait_ge(s_hi, HEAD + 5)
                    lo_part(s_u[:, :, 1], bank[6][:, 0:4], s_u[:, :, 0], WS).then_inc(s_lo, 1)
                    for j in range(4):
                        last = nc.vector.tensor_scalar(s_uw[:, j, :], ones[:, :], bank[6][:, j:j + 1], None, ALU.mult)
                    last.then_inc(s_uwd, 1)
            dve.wait_ge(f_aps, HEAD + 1)
            nc.vector.tensor_scalar(alpha1[:, :], bank[5][:, 0:HT], 1.0 / C, None, ALU.mult).then_inc(f_alpha, 1)
            dve.wait_ge(f_aps, HEAD + 2)
            nc.vector.tensor_scalar(alpha2_row[:, :], bank[4][:, :], 1.0 / H, None, ALU.mult).then_inc(f_alpha, 1)
            dve.wait_ge(s_prod, HEAD + 10)
            nc.vector.tensor_tensor(attn_row[:, :], bank[7][:, :], s_bo, ALU.add).then_inc(f_alpha, 1)

            def ctx_lo(n, u, w):
                for j in range(CT):
                    dve.wait_ge(s_chi, HEAD + 4 * n + j + 1)
                    nc.vector.tensor_tensor(s_ctxp[u][1][:, j, 0:w], s_ctx[u][:, j, 0:w], s_ctxp[u][0][:, j, 0:w],
                                            ALU.subtract).then_inc(s_clo, 1)

            def kprime_lo(n, w):
                for j in range(CT):
                    dve.wait_ge(s_khi, HEAD + 4 * n + j + 1)
                    if w < T:
                        lo_part(tail_k_v[:, j, KX:2 * KX], bank[j][:, w:w + KX], tail_k_v[:, j, 0:KX], 1 / WS)
                    lo_part(kp[1][:, j, bass.ds(n * T, w)], bank[j][:, 0:w], kp[0][:, j, bass.ds(n * T, w)],
                            1 / WS).then_inc(s_klo, 1)

            def vprime_lo(n, nt):
                for q in range(nt):
                    dve.wait_ge(s_vhi, HEAD + 4 * n + q + 1)
                    tile = bass.ds(4 * n + q, 1)
                    lo_part(vp[1][:, tile, :].rearrange("p a c -> p (a c)"), bank[4 + q % 2][:, :],
                            vp[0][:, tile, :].rearrange("p a c -> p (a c)"), 1 / WS).then_inc(s_vlo, 1)

            def bias(n, nt):
                dve.wait_ge(s_bps, HEAD + n + 1)
                for q in range(nt):
                    last = nc.vector.tensor_reduce(s_kb[:, q:q + 1], bank[6][:, 2 * q:2 * q + 2], AX_X, ALU.add)
                last.then_inc(s_kbs, 1)
                dve.wait_ge(s_kbs, HEAD + 2 * n + 1)
                for q in range(nt):
                    last = nc.vector.tensor_scalar(key_bias[:, bass.ds(4 * n + q, 1)], s_kb[:, q:q + 1], 1 / WS, None,
                                                   ALU.mult)
                last.then_inc(s_kbs, 1)

            ctx_lo(0, 0, T)

            def body_s(i, last):
                for u in range(2):
                    n = 2 * i + u
                    kprime_lo(n, T)
                    ctx_lo(n + 1, 1 - u, M - CH * T if last and u else T)
                    bias(n, 4)
                    vprime_lo(n, 4)

            with dve.Fori(0, CH // 2 - 1) as i:
                body_s(i, False)
            body_s(CH // 2 - 1, True)
            Cn.vector_moments(dve, 0, 0, 0)
            kprime_lo(CH, P)
            bias(CH, 1)
            vprime_lo(CH, 1)
            dve.wait_ge(s_thi, HEAD + 1)
            lo_part(s_tv[1][0:KX, :], bank[5][0:KX, :], s_tv[0][0:KX, :], 1 / WS).then_inc(s_tlo, 4)
            dve.wait_ge(s_tps, HEAD + 2)
            nc.vector.tensor_copy(tail_bias[:, :], bank[6][:, 0:KX]).then_inc(s_tbias, 1)

            Cn.vector_rstd(dve, 0)
            Cn.vector_xn(0)
            Cn.vector_lo(dve, 0, 0)
            after_s(dve)

            def maximum(n):
                for t in range(1, KT):
                    dve.wait_ge(c_s, HEAD + KT * n + t + 1)
                    if t == 1:
                        nc.vector.tensor_tensor(c_mx, c_S[:, 0, :], c_S[:, 1, :], ALU.max).then_inc(c_max, 1)
                    else:
                        dve.wait_ge(c_max, HEAD + (KT - 1) * n + t - 1)
                        nc.vector.tensor_tensor(c_mx, c_mx, c_S[:, t, :], ALU.max).then_inc(c_max, 1)
                dve.wait_ge(c_tsc, HEAD + n + 1)
                nc.vector.tensor_reduce(c_ts, bank[5][:, 0:SUB * 2 * KX].rearrange("p (s h k) -> p s k h", s=SUB, h=2),
                                        AX_X, ALU.add).then_inc(c_tstep, 1)
                dve.wait_ge(c_tstep, HEAD + 7 * n + 1)
                nc.vector.tensor_tensor(c_ts, c_ts,
                                        tail_bias[:, :].rearrange("p (o k) -> p o k", o=1).to_broadcast([P, SUB, KX]),
                                        ALU.add).then_inc(c_tstep, 1)
                dve.wait_ge(c_tstep, HEAD + 7 * n + 2)
                nc.vector.tensor_reduce(c_tmax, c_ts, AX_X, ALU.max).then_inc(c_tstep, 1)
                dve.wait_ge(c_mt, HEAD + n + 1)
                nc.vector.tensor_reduce(c_mtile, bank[7][:, :].rearrange("p (s k) -> p s k", s=SUB), AX_X,
                                        ALU.max).then_inc(c_mstep, 1)
                dve.wait_ge(c_mstep, HEAD + 3 * n + 1)
                dve.wait_ge(c_tstep, HEAD + 7 * n + 3)
                nc.vector.tensor_tensor(c_mcol, c_mtile, c_tmax, ALU.max).then_inc(c_mstep, 1)
                dve.wait_ge(c_mstep, HEAD + 3 * n + 2)
                for q in range(SUB):
                    last_op = nc.vector.tensor_scalar(c_diag[:, q, :], ident[:, :], c_mcol[:, q:q + 1], None, ALU.mult)
                last_op.then_inc(c_mstep, 1)
                nc.vector.tensor_tensor(c_td, c_ts,
                                        c_mcol.rearrange("p (s o) -> p s o", o=1).to_broadcast([P, SUB, KX]),
                                        ALU.subtract).then_inc(c_tstep, 1)
                dve.wait_ge(c_mps, HEAD + n + 1)
                nc.vector.tensor_copy(c_mb, bank[7][:, :]).then_inc(c_mbd, 1)
                dve.wait_ge(c_mbd, HEAD + n + 1)

            def sub(t):
                nc.vector.tensor_tensor(c_S[:, t, :], c_S[:, t, :], c_mb, ALU.subtract).then_inc(c_sub, 1)

            def split(n, t):
                dve.wait_ge(c_exp, HEAD + KT * n + t + 1)
                dve.wait_ge(c_pv, HEAD + KT * n + t - RING + 1)
                nc.vector.tensor_copy(c_ph[t % RING], c_S[:, t, :]).then_inc(c_hi, 1)
                dve.wait_ge(c_hi, HEAD + KT * n + t + 1)
                nc.vector.tensor_tensor(c_pl[t % RING], c_S[:, t, :], c_ph[t % RING], ALU.subtract).then_inc(c_lo, 1)

            def first(n):
                sub(0)
                sub(1)
                split(n, 0)

            def tail(n):
                dve.wait_ge(c_texp, HEAD + n + 1)
                nc.vector.tensor_copy(c_th, c_tp).then_inc(c_tstep, 1)
                dve.wait_ge(c_tstep, HEAD + 7 * n + 5)
                nc.vector.tensor_copy(c_t3[:, :, 0:KX], c_th)
                nc.vector.tensor_copy(c_t3[:, :, KX:2 * KX], c_th)
                nc.vector.tensor_tensor(c_t3[:, :, 2 * KX:3 * KX], c_tp, c_th, ALU.subtract).then_inc(c_tstep, 1)
                nc.vector.tensor_reduce(c_tsum, c_tp, AX_X, ALU.add).then_inc(c_tstep, 1)

            def finish(n, u):
                dve.wait_ge(c_rs, HEAD + n + 1)
                dve.wait_ge(c_tstep, HEAD + 7 * n + 7)
                nc.vector.tensor_tensor(c_den, bank[6][:, 0:SUB], c_tsum, ALU.add).then_inc(c_ri, 1)
                dve.wait_ge(c_ri, HEAD + 2 * n + 1)
                nc.vector.reciprocal(c_rinv, c_den).then_inc(c_ri, 1)
                dve.wait_ge(c_ri, HEAD + 2 * n + 2)
                dve.wait_ge(c_xb, HEAD + 4 * n + 4)
                for q in range(SUB):
                    nc.vector.scalar_tensor_tensor(out=c_x[u][:, q, :], in0=bank[q][:, :], scalar=c_rinv[:, q:q + 1],
                                                   in1=c_x[u][:, q, :], op0=ALU.mult, op1=ALU.add).then_inc(c_x2, 1)

            maximum(0)
            first(0)

            def body_c(i, last):
                for u in range(2):
                    n = 2 * i + u
                    more = not (last and u)
                    nxt, nn, npar, ni = (Cn, n + 1, 1 - u, i + u) if more else (Dn, 0, 0, 0)
                    for t in range(2, KT + 1):
                        if t < KT:
                            sub(t)
                        split(n, t - 1)
                        if t == 5:
                            tail(n)
                        if t == 7:
                            nxt.vector_stats(dve, nn, npar, ni)
                            nxt.vector_xn(npar)
                        if t == 21:
                            nxt.vector_lo(dve, nn, 0)
                    if more:
                        maximum(n + 1)
                        first(n + 1)
                    finish(n, u)

            pair_loop(body_c)

            after_scores(dve)

            def body_d(i, last):
                for u in range(2):
                    n = 2 * i + u
                    more = not (last and u)
                    for t in range(HT):
                        dve.wait_ge(d_gelu, HEAD + HT * n + t + 1)
                        if t < HT - 1:
                            dve.wait_ge(d_f2, HEAD + (HT - 1) * (n - 1) + t + 1)
                        else:
                            dve.wait_ge(d_ops, HEAD + 4 * n)
                        nc.vector.tensor_copy(d_gh[:, t, :], d_g[t % 2]).then_inc(d_ghi, 1)
                        dve.wait_ge(d_ghi, HEAD + HT * n + t + 1)
                        nc.vector.tensor_tensor(d_gl[:, t, :], d_g[t % 2], d_gh[:, t, :], ALU.subtract).then_inc(d_glo, 1)
                        if more and t == 7:
                            Dn.vector_stats(dve, n + 1, 1 - u, i + u)
                            Dn.vector_xn(1 - u)
                    if more:
                        Dn.vector_lo(dve, n + 1, 0)
                    dve.wait_ge(d_xb, HEAD + 4 * n + 4)
                    for q in range(SUB):
                        dve.wait_ge(d_ops, HEAD + 4 * n + q + 1)
                        nc.vector.tensor_tensor(d_t[q % 2], bank[q][:, :], alpha2_row[:, :], ALU.mult).then_inc(d_ts, 1)
                        dve.wait_ge(d_ts, HEAD + 4 * n + q + 1)
                        nc.vector.tensor_tensor(d_x[u][:, q, :], d_t[q % 2], d_x[u][:, q, :], ALU.add).then_inc(d_out, 1)

            pair_loop(body_d)

        @block.tensor
        def _(pe_block):
            pe = nc.tensor
            start("pe", pe_block)

            def pair_loop(body):
                with pe_block.Fori(0, NB // 2 - 1) as i:
                    body(i, False)
                body(NB // 2 - 1, True)

            pe_block.wait_ge(a_consts, HEAD + 1)
            pe_block.wait_ge(a_eye, HEAD + 3)
            for bk in (2, 3):
                pe.matmul(bank[bk][:, :], zeros16[:, 0:P], zeros16, start=True, stop=True, skip_group_check=True)
            A.tensor_turn(pe_block, 0, 0)
            pe_block.wait_ge(a_wlo, HEAD + CT)

            def k_tile(n, u, t):
                pe_block.wait_ge(a_predone, HEAD + 4 * n + t - 1)
                for j in range(CT):
                    last = mm3(pe, bank[t % 2][:, :],
                               [a_xT[u][h][:, j, t * P:(t + 1) * P] for h in range(2)],
                               [a_w[h][:, j, :] for h in range(2)], j == 0, j == CT - 1)
                last.then_inc(a_kps, 1)

            def kv_tile(n, u, t):
                pe_block.wait_ge(a_krdone, HEAD + 4 * n + t + 1)
                for g in range(4):
                    pe.matmul(bank[2][:, g * P:(g + 1) * P], a_kr[t][:, g * P:(g + 1) * P],
                              a_xn[u][:, t, g * P:(g + 1) * P], start=False, stop=True, skip_group_check=True)
                for g in range(4):
                    last = pe.matmul(bank[3][:, g:g + 1], a_k[t][:, g * P:(g + 1) * P], ones[:, 0:1],
                                     start=False, stop=True, skip_group_check=True)
                last.then_inc(a_kvdone, 1)

            pe_block.wait_ge(A.lo, HEAD + 4)
            k_tile(0, 0, 0)
            k_tile(0, 0, 1)

            def body_a(i, last):
                for u in range(2):
                    n = 2 * i + u
                    more = not (last and u)
                    k_tile(n, u, 2)
                    if more:
                        A.tensor_turn(pe_block, n + 1, 1 - u)
                    kv_tile(n, u, 0)
                    k_tile(n, u, 3)
                    kv_tile(n, u, 1)
                    if more:
                        pe_block.wait_ge(A.lo, HEAD + 4 * n + 8)
                        k_tile(n + 1, 1 - u, 0)
                    kv_tile(n, u, 2)
                    if more:
                        k_tile(n + 1, 1 - u, 1)
                    kv_tile(n, u, 3)

            pair_loop(body_a)

            def lepe(n, u, t):
                pe_block.wait_ge(b_tstep, HEAD + 8 * n + 2 * t - 2)
                for tap in range(3):
                    for j in range(CT):
                        last = mm3(pe, bank[4 + t % 2][:, :],
                                   [b_xT[u][h][:, j, tap + t * P:tap + (t + 1) * P] for h in range(2)],
                                   [b_lw[h][:, tap * CT + j, :] for h in range(2)],
                                   tap == 0 and j == 0, tap == 2 and j == CT - 1)
                last.then_inc(b_lps, 1)

            def att(n, t):
                pe_block.wait_ge(b_rope, HEAD + 2 * n + 2)
                pe_block.wait_ge(b_tstep, HEAD + 8 * n + 2 * t - 3)
                for g in range(4):
                    last = pe.matmul(bank[2 + t % 2][:, g * P:(g + 1) * P], b_qr[:, g, t * P:(t + 1) * P], b_kv[:, g, :],
                                     start=True, stop=True)
                last.then_inc(b_aps, 1)

            pe_block.wait_ge(b_qwlo, HEAD + CT)
            pe_block.wait_ge(a_predone, HEAD + 4 * NB)

            def body_b(i, last):
                for u in range(2):
                    n = 2 * i + u
                    pe_block.wait_ge(b_xT_load[u], 32 * i + 32)
                    for t in range(4):
                        pe_block.wait_ge(b_acts, HEAD + 4 * n + t - 1)
                        for j in range(CT):
                            mm = mm3(pe, bank[t % 2][:, :], [b_w[h][:, j, t * P:(t + 1) * P] for h in range(2)],
                                     [b_xT[u][h][:, j, 1:1 + T] for h in range(2)], j == 0, j == CT - 1)
                        mm.then_inc(b_qps, 1)
                    pe_block.wait_ge(b_wlo, HEAD + 3 * CT)
                    lepe(n, u, 0)
                    pe_block.wait_ge(b_kvset, HEAD + 3)
                    pe_block.wait_ge(b_qdone, HEAD + 4 * n + 4)
                    for t in range(SUB):
                        for g in range(4):
                            mm = pe.matmul(bank[6][:, t * NH:(t + 1) * NH], b_q[:, g, t * P:(t + 1) * P], b_km[:, g, :],
                                           start=g == 0, stop=g == 3)
                    mm.then_inc(b_zps, 1)
                    lepe(n, u, 1)
                    att(n, 0)
                    att(n, 1)
                    lepe(n, u, 2)
                    att(n, 2)
                    lepe(n, u, 3)
                    att(n, 3)

            pair_loop(body_b)

            pe_block.wait_ge(s_wload, 7 * 16)
            pe_block.wait_ge(b_tstep, HEAD + 8 * NB)
            for m in range(8):
                w, r = (s_raw[0], s_raw[1]) if m < 4 else (s_raw[2], s_raw[3])
                if m >= 4:
                    pe_block.wait_ge(s_lo, HEAD + m - 3)
                for j in range(CT):
                    mm = pe.matmul(bank[m % 4][:, :], w[:, j, (m % 4) * P:(m % 4 + 1) * P], r[:, j, :],
                                   start=j == 0, stop=j == CT - 1)
                mm.then_inc(s_prod, 1)
                if m == 3:
                    for g in range(4):
                        for j in range(CT):
                            mm = pe.matmul(bank[6][:, g:g + 1], w[:, j, g * P:(g + 1) * P], s_bq[:, j:j + 1],
                                           start=j == 0, stop=j == CT - 1)
                    mm.then_inc(s_prod, 1)
            pe_block.wait_ge(s_bvw_ok, HEAD + 1)
            for j in range(CT):
                mm = pe.matmul(bank[7][:, :], s_bvw[:, j, :], s_raw[3][:, j, :], start=j == 0, stop=j == CT - 1)
            mm.then_inc(s_prod, 1)
            pe_block.wait_ge(f_add, HEAD + NB)
            for t in range(HT):
                mm = pe.matmul(bank[5][:, t:t + 1], f_sum[0][:, t * P:(t + 1) * P], ones[:, 0:1], start=True, stop=True)
            mm.then_inc(f_aps, 1)
            for k in range(4):
                mm = pe.matmul(bank[4][:, :], ones[:, :], f_sum[1][:, k * C:(k + 1) * C], start=k == 0, stop=k == 3)
            mm.then_inc(f_aps, 1)
            pe_block.wait_ge(s_lo, HEAD + 9)

            def k_chunk(n, u, w):
                pe_block.wait_ge(s_clo, HEAD + 4 * n + 4)
                for j in range(CT):
                    pe_block.wait_ge(s_klo, HEAD + 4 * n + j - 3)
                    for q in range(CT):
                        mm = mm3(pe, bank[j][:, 0:w], [s_A[h][:, q, j * P:(j + 1) * P] for h in range(2)],
                                 [s_ctxp[u][h][:, q, 0:w] for h in range(2)], q == 0, q == CT - 1)
                    mm.then_inc(s_kps, 1)

            def v_chunk(n, u, nt):
                pe_block.wait_ge(s_kbs, HEAD + 2 * n)
                for t in range(nt):
                    for q in range(CT):
                        pe.matmul(bank[6][:, 2 * t:2 * t + 2], s_ctxp[u][0][:, q, t * P:(t + 1) * P], s_u[:, q, :],
                                  start=q == 0, stop=False)
                        mm = pe.matmul(bank[6][:, 2 * t:2 * t + 2], s_ctxp[u][1][:, q, t * P:(t + 1) * P], s_u[:, q, :],
                                       start=False, stop=q == CT - 1)
                mm.then_inc(s_bps, 1)
                for t in range(nt):
                    pe_block.wait_ge(s_vlo, HEAD + 4 * n + t - 1)
                    for q in range(CT):
                        mm = mm3(pe, bank[4 + t % 2][:, :], [s_ctxp[u][h][:, q, t * P:(t + 1) * P] for h in range(2)],
                                 [s_B[h][:, q, :] for h in range(2)], q == 0, q == CT - 1)
                    mm.then_inc(s_vps, 1)

            pe_block.wait_ge(f_alpha, HEAD + 3)
            with pe_block.Fori(0, CH // 2) as i:
                for u in range(2):
                    k_chunk(2 * i + u, u, T)
                    v_chunk(2 * i + u, u, 4)
            k_chunk(CH, 0, P + KX)
            v_chunk(CH, 0, 1)
            pe_block.wait_ge(s_vlo, HEAD + KT - 1)
            for q in range(CT):
                mm = mm3(pe, bank[5][0:KX, :], [s_ctxp[0][h][:, q, P:P + KX] for h in range(2)],
                         [s_B[h][:, q, :] for h in range(2)], q == 0, q == CT - 1)
            mm.then_inc(s_tps, 1)
            pe_block.wait_ge(s_uwd, HEAD + 1)
            pe_block.wait_ge(s_kbs, HEAD + 2 * CH + 2)
            for q in range(CT):
                mm = pe.matmul(bank[6][:, 0:KX], s_uw[:, q, :], s_ctx[0][:, q, P:P + KX], start=q == 0, stop=q == CT - 1)
            mm.then_inc(s_tps, 1)

            pe_block.wait_ge(s_vlo, HEAD + KT)
            pe_block.wait_ge(s_tlo, HEAD + 4)
            pe_block.wait_ge(s_tbias, HEAD + 1)
            Cn.tensor_turn(pe_block, 0, 0)
            after_s(pe_block)

            def scores(n):
                pe_block.wait_ge(Cn.lo, HEAD + 4 * n + 4)
                for t in range(KT):
                    if t >= 3:
                        pe_block.wait_ge(c_s, HEAD + KT * n + t - 2)
                    for j in range(CT):
                        mm = mm3(pe, bank[4 + t % 3][:, :], [kp[h][:, j, t * P:(t + 1) * P] for h in range(2)],
                                 [c_xT[0][h][:, j, :] for h in range(2)], j == 0, j == CT - 1)
                    mm.then_inc(c_qk, 1)
                pe_block.wait_ge(c_s, HEAD + KT * n + KT - 2)
                for q in range(SUB):
                    o = q * 2 * KX
                    for j in range(CT):
                        if j == CT - 1:
                            for k in range(CT):
                                pe.matmul(bank[5][:, o:o + KX], c_xT[0][1][:, k, q * P:(q + 1) * P],
                                          tail_k_v[:, k, 0:KX], start=False, stop=False)
                        mm = pe.matmul(bank[5][:, o:o + 2 * KX], c_xT[0][0][:, j, q * P:(q + 1) * P],
                                       tail_k_v[:, j, :], start=j == 0, stop=j == CT - 1)
                mm.then_inc(c_tsc, 1)

            def turn_max(n):
                pe_block.wait_ge(c_max, HEAD + (KT - 1) * (n + 1))
                for q in range(SUB):
                    mm = pe.transpose(bank[7][:, q * P:(q + 1) * P], c_mx[:, q * P:(q + 1) * P], ident[:, :])
                mm.then_inc(c_mt, 1)

            def spread_max(n):
                pe_block.wait_ge(c_mstep, HEAD + 3 * n + 3)
                for q in range(SUB):
                    mm = pe.matmul(bank[7][:, q * P:(q + 1) * P], ones[:, :], c_diag[:, q, :], start=True, stop=True)
                mm.then_inc(c_mps, 1)

            def pv(n, t):
                pe_block.wait_ge(c_lo, HEAD + KT * n + t + 1)
                for q in range(SUB):
                    if t == 0:
                        pe_block.wait_ge(c_x2, HEAD + 4 * n + q - 3)
                    mm = mm3(pe, bank[q][:, :], [r[t % RING][:, q * P:(q + 1) * P] for r in (c_ph, c_pl)],
                             [vp[h][:, t, :] for h in range(2)], t == 0, t == KT - 1)
                mm.then_inc(c_pv, 1)

            def sums(n):
                pe_block.wait_ge(c_add, HEAD + (KT - 1) * (n + 1))
                for q in range(SUB):
                    mm = pe.matmul(bank[6][:, q:q + 1], c_sum[:, q * P:(q + 1) * P], ones[:, 0:1], start=True, stop=True)
                mm.then_inc(c_rs, 1)

            scores(0)
            turn_max(0)
            spread_max(0)

            def body_c(i, last):
                for u in range(2):
                    n = 2 * i + u
                    more = not (last and u)
                    for t in range(KT - HELD):
                        if t == 5:
                            pe_block.wait_ge(c_tstep, HEAD + 7 * n + 6)
                            for q in range(SUB):
                                mm = pe.transpose(bank[5][0:3 * KX, q * P:(q + 1) * P], c_t3[:, q, :], ident[:, :])
                            mm.then_inc(c_ttr, 1)
                        if t == 12:
                            if more:
                                Cn.tensor_turn(pe_block, n + 1, 0)
                            else:
                                Dn.tensor_turn(pe_block, 0, 0)
                        pv(n, t)
                        if t == 11:
                            pe_block.wait_ge(c_tTd, HEAD + n + 1)
                            for q in range(SUB):
                                pe.matmul(bank[q][:, :], c_tT[0:3 * KX, q * P:(q + 1) * P], tail_v[0:3 * KX, :],
                                          start=False, stop=False)
                    if more:
                        scores(n + 1)
                    pv(n, KT - 4)
                    pv(n, KT - 3)
                    if more:
                        turn_max(n + 1)
                    pv(n, KT - 2)
                    if more:
                        spread_max(n + 1)
                    pv(n, KT - 1)
                    pe_block.wait_ge(c_s, HEAD + KT * n + KT + (KT if more else 0))
                    if not more:
                        pe_block.wait_ge(Dn.lo, HEAD + 4)
                    sums(n)

            pair_loop(body_c)

            pe_block.wait_ge(d_wload, 32)
            pe_block.wait_ge(c_ri, HEAD + 2 * NB)

            def body_d(i, last):
                for u in range(2):
                    n = 2 * i + u
                    more = not (last and u)

                    def ffn2(t):
                        pe_block.wait_ge(d_glo, HEAD + HT * n + t + 1)
                        if t == 0:
                            pe_block.wait_ge(c_x2, HEAD + 4 * NB)
                            pe_block.wait_ge(d_out, HEAD + 4 * n)
                        for q in range(SUB):
                            for h, g in enumerate((d_gh, d_gl)):
                                mm = pe.matmul(bank[q][:, :], g[:, t, q * P:(q + 1) * P], d_w2[:, t, :],
                                               start=t == 0 and h == 0, stop=t == HT - 1 and h == 1)
                            if t == HT - 1:
                                mm.then_inc(d_ops, 1)
                        if t < HT - 1:
                            mm.then_inc(d_f2, 1)

                    pe_block.wait_ge(Dn.lo, HEAD + 4 * n + 4)
                    for t in range(HT + LAG):
                        if t < HT:
                            if t >= 4:
                                pe_block.wait_ge(d_gelu, HEAD + HT * n + t - 3)
                            for j in range(CT):
                                for h in range(2):
                                    mm = pe.matmul(bank[4 + t % 4][:, :], d_w1[:, j, t * P:(t + 1) * P], d_xT[0][h][:, j, :],
                                                   start=j == 0 and h == 0, stop=j == CT - 1 and h == 1)
                            mm.then_inc(d_hps, 1)
                        if more and t == HT + 1:
                            pe_block.wait_ge(d_gelu, HEAD + HT * n + HT)
                            Dn.tensor_turn(pe_block, n + 1, 0)
                        if t >= LAG:
                            ffn2(t - LAG)

            pair_loop(body_d)


def kernel(x, ctx_1024, L0_attn_qk_w, L0_attn_qk_b, L0_attn_lepe_w, L0_attn_lepe_b, L0_xattn_Wk, L0_xattn_Wv,
           L0_xattn_bv, L0_xattn_Wq, L0_xattn_bq, L0_xattn_Wo, L0_xattn_bo, L0_ffn_w1, L0_ffn_b1, L0_ffn_w2,
           L0_ffn_b2):
    import numpy as np
    import concourse.bacc as bacc
    from concourse.bass_utils import run_bass_kernel_spmd as run

    theta = np.float32(1.0) / (10000.0 ** (np.arange(HALF) / HALF)).astype(np.float32)
    angles = np.arange(N, dtype=np.float32)[:, None] * theta
    cos, sin = np.cos(angles), np.sin(angles)

    def cont(v):
        return np.ascontiguousarray(v)

    def column(v):
        return cont(np.reshape(v, (-1, P)).T)

    w1_groups = np.reshape(np.asarray(L0_ffn_w1).T, (4, P, H))
    w2_groups = np.reshape(np.transpose(np.reshape(np.asarray(L0_ffn_w2).T, (4, 4, P, C)), (0, 2, 1, 3)), (4, P, 4 * C))
    ffn_w = cont(np.stack([w1_groups, w2_groups], axis=1).reshape(8, P, 4 * C))
    qk_w, qk_b = np.asarray(L0_attn_qk_w), np.asarray(L0_attn_qk_b)

    def halves(v):
        return np.concatenate([v[..., 0::2], v[..., 1::2]], axis=-1)

    arrays = {
        "x": cont(np.asarray(x)[0]),
        "ctxT": cont(np.asarray(ctx_1024)[0].T),
        "wq_rope": cont(halves(qk_w[:, :C])), "wk_rope": cont(halves(qk_w[:, C:])),
        "bq_rope": column(halves(qk_b[:C])), "bk_rope": cont(halves(qk_b[C:])),
        "lepe_w": cont(np.reshape(L0_attn_lepe_w, (3 * C, C))), "lepe_b": cont(L0_attn_lepe_b),
        "xk": cont(L0_xattn_Wk), "xq": cont(L0_xattn_Wq), "xv": cont(L0_xattn_Wv),
        "xoT": cont(np.asarray(L0_xattn_Wo).T),
        "xbq": column(L0_xattn_bq), "xbv": column(L0_xattn_bv), "xbo": cont(L0_xattn_bo),
        "ffn_w": ffn_w,
        "b1": column(L0_ffn_b1), "b2": cont(L0_ffn_b2),
        "cos": cont(cos), "sin": cont(sin), "cosT": cont(cos.T), "sinT": cont(sin.T),
    }
    nc = bacc.Bacc("TRN2", target_bir_lowering=False, num_devices=1)
    d = {k: nc.dram_tensor(k, v.shape, mybir.dt.from_np(v.dtype), kind="ExternalInput").ap() for k, v in arrays.items()}
    for name, shape, dt in (("x1", (N, C), F32), ("x2", (N, C), F32), ("xT_hi", (C, N + 2 * EDGE), F16), ("xT_lo", (C, N + 2 * EDGE), F16),
                            ("signs", (8, P, 4 * C), F16)):
        d[name] = nc.dram_tensor(name, shape, dt, kind="Internal").ap()
    d["out"] = nc.dram_tensor("out", (N, C), F32, kind="ExternalOutput").ap()
    build(nc, d)
    r = run(nc, [arrays], core_ids=[0])
    return np.reshape(r.results[0]["out"], (1, N, C))
```

```python
from contextlib import ExitStack

import concourse.bass as bass
from concourse import mybir

F32 = mybir.dt.float32
F16 = mybir.dt.float16
ALU = mybir.AluOpType
ACT = mybir.ActivationFunctionType
AX_X = mybir.AxisListType.X

P = 128
N, C, M, H = 4096, 512, 3202, 2048
T = 512
NB = N // T
SUB = T // P
CT = C // P
HT = H // P
KT = M // P
KX = M - KT * P
NH = 8
DH = C // NH
HALF = C // 2
PAIRS = T // 2
HALO = T + 2
EDGE = 16
EPS = 1e-5
WS = 32.0
SCALE = float(C) ** -0.5
HEAD = 32
RING = 5
HELD = 4
LAG = 3


def build(nc, d):
    with ExitStack() as ctx:
        def sb(name, cols, dt=F32):
            return ctx.enter_context(nc.sbuf_tensor(name, [P, cols], dt))

        heads = []

        def sem(name, owner):
            s = ctx.enter_context(nc.semaphore(name))
            heads.append((owner, s))
            return s

        def start(owner, eng):
            for who, s in heads:
                if who == owner:
                    eng.sem_inc(s, HEAD)

        bank = [ctx.enter_context(nc.psum_tensor(f"bank{i}", [P, 512], F32)) for i in range(8)]

        ident = sb("ident", P)
        ones = sb("ones", P)
        tail_k = sb("tail_k", CT * 2 * KX, F16)
        tail_v = sb("tail_v", C, F16)
        tail_bias = sb("tail_bias", KX)
        key_bias = sb("key_bias", KT)
        alpha1 = sb("alpha1", HT)
        b1_col = sb("b1_col", HT)
        alpha2_row = sb("alpha2_row", C)
        attn_row = sb("attn_row", C)
        s_bq = sb("s_bq", CT)
        s_bv = sb("s_bv", CT)
        stats = sb("stats", SUB * 6)
        mv = sb("mv", SUB * 2)
        ve = sb("ve", SUB)
        sd = sb("sd", SUB)
        r0 = sb("r0", SUB)
        r1 = sb("r1", SUB)
        rstd = sb("rstd", SUB)
        stats_v = stats[:, :].rearrange("p (s k) -> p s k", s=SUB)
        mv_v = mv[:, :].rearrange("p (s k) -> p s k", s=SUB)

        ARENA = 51240
        arena = sb("arena", ARENA)

        class Carve:
            def __init__(self, at=0):
                self.at = at

            def f32(self, *shape):
                n = 1
                for k in shape:
                    n *= k
                v = arena[:, self.at:self.at + n]
                self.at += n
                assert self.at <= ARENA, self.at
                return self.shaped(v, shape)

            def f16(self, *shape):
                n = 1
                for k in shape:
                    n *= k
                v = arena[:, self.at:self.at + (n + 1) // 2].bitcast(F16)[:, 0:n]
                self.at += (n + 1) // 2
                assert self.at <= ARENA, self.at
                return self.shaped(v, shape)

            @staticmethod
            def shaped(v, shape):
                if len(shape) == 2:
                    return v.rearrange("p (a b) -> p a b", a=shape[0])
                if len(shape) == 3:
                    return v.rearrange("p (a b c) -> p a b c", a=shape[0], b=shape[1])
                return v

        def blocks(ap):
            return ap.rearrange("(b s p) c -> b p s c", s=SUB, p=P)

        def one(view, n):
            return view[bass.ds(n, 1)].rearrange("b p s c -> (b p) s c")

        x_v, x1_v, x2_v, out_v = blocks(d["x"]), blocks(d["x1"]), blocks(d["x2"]), blocks(d["out"])
        xp_v, x1p_v = (d[k].rearrange("(b h p e) c -> b p h (e c)", h=2, p=P, e=2) for k in ("x", "x1"))
        cos_v, sin_v = blocks(d["cos"]), blocks(d["sin"])
        xT_v = [d[k].rearrange("(j p) n -> p j n", p=P) for k in ("xT_hi", "xT_lo")]
        cosT_v, sinT_v = (d[k].rearrange("(j p) n -> p j n", p=P) for k in ("cosT", "sinT"))

        def rows(name):
            return d[name].rearrange("(j p) n -> p j n", p=P)

        def tile_of(v, j):
            return v[:, bass.ds(j, 1), :].rearrange("p a c -> p (a c)")

        def row_of(name):
            return d[name].rearrange("(a n) -> a n", a=1).to_broadcast([P, C])

        def mm3(pe, out, w, x, first, last):
            pe.matmul(out, w[0], x[0], start=first, stop=False)
            pe.matmul(out, w[0], x[1], start=False, stop=False)
            return pe.matmul(out, w[1], x[0], start=False, stop=last)

        class Norm:
            def __init__(self, name, x, xn, xT, loaded):
                self.x, self.xn, self.xT, self.loaded = x, xn, xT, loaded
                self.step = sem(name + "_ln_step", "dve")
                self.sd = sem(name + "_ln_sd", "act")
                self.xn_ready = sem(name + "_xn_ready", "dve")
                self.turned = sem(name + "_turned", "pe")
                self.hi = sem(name + "_xT_hi", "act")
                self.lo = sem(name + "_xT_lo", "dve")

            def vector_stats(self, dve, n, par, i):
                self.vector_moments(dve, n, par, i)
                self.vector_rstd(dve, n)

            def vector_moments(self, dve, n, par, i):
                s0 = n * 8
                dve.wait_ge(self.loaded[par], 16 * i + 16)
                for s in range(SUB):
                    last = nc.vector.bn_stats(stats_v[:, s, :], self.x[par][:, s, :])
                last.then_inc(self.step, 1)
                dve.wait_ge(self.step, HEAD + s0 + 1)
                nc.vector.memset(ve[:, :], EPS)
                for s in range(SUB):
                    last = nc.vector.bn_aggr(mv_v[:, s, :], stats_v[:, s, :])
                last.then_inc(self.step, 1)
                dve.wait_ge(self.step, HEAD + s0 + 2)
                nc.vector.tensor_tensor(ve[:, :], mv_v[:, :, 1], ve[:, :], ALU.add).then_inc(self.step, 1)

            def vector_rstd(self, dve, n):
                s0 = n * 8
                dve.wait_ge(self.sd, HEAD + n + 1)
                nc.vector.reciprocal(r0[:, :], sd[:, :]).then_inc(self.step, 1)
                dve.wait_ge(self.step, HEAD + s0 + 4)
                nc.vector.tensor_tensor(r1[:, :], r0[:, :], r0[:, :], ALU.mult).then_inc(self.step, 1)
                dve.wait_ge(self.step, HEAD + s0 + 5)
                nc.vector.tensor_tensor(r1[:, :], r1[:, :], ve[:, :], ALU.mult).then_inc(self.step, 1)
                dve.wait_ge(self.step, HEAD + s0 + 6)
                nc.vector.tensor_scalar(r1[:, :], r1[:, :], -0.5, 1.5, ALU.mult, ALU.add).then_inc(self.step, 1)
                dve.wait_ge(self.step, HEAD + s0 + 7)
                nc.vector.tensor_tensor(rstd[:, :], r0[:, :], r1[:, :], ALU.mult).then_inc(self.step, 1)
                dve.wait_ge(self.step, HEAD + s0 + 8)

            def vector_xn(self, par):
                for s in range(SUB):
                    nc.vector.tensor_scalar(self.xn[par][:, s, :], self.x[par][:, s, :], mv_v[:, s, 0:1],
                                            rstd[:, s:s + 1], ALU.subtract, ALU.mult).then_inc(self.xn_ready, 1)

            def scalar_sd(self, act, n):
                act.wait_ge(self.step, HEAD + n * 8 + 3)
                nc.scalar.activation(sd[:, :], ve[:, :], ACT.Sqrt).then_inc(self.sd, 1)

            def tensor_turn(self, pe, n, par):
                for s in range(SUB):
                    pe.wait_ge(self.xn_ready, HEAD + n * 4 + s + 1)
                    for j in range(CT):
                        last = pe.transpose(bank[4 + j][:, s * P:(s + 1) * P],
                                            self.xn[par][:, s, j * P:(j + 1) * P], ident[:, :])
                last.then_inc(self.turned, 1)

            def scalar_hi(self, act, n, par):
                act.wait_ge(self.turned, HEAD + n + 1)
                for j in range(CT):
                    nc.scalar.activation(self.xT[par][0][:, j, :], bank[4 + j][:, :], ACT.Copy).then_inc(self.hi, 1)

            def vector_lo(self, dve, n, par):
                for j in range(CT):
                    dve.wait_ge(self.hi, HEAD + n * 4 + j + 1)
                    nc.vector.tensor_tensor(self.xT[par][1][:, j, :], bank[4 + j][:, :],
                                            self.xT[par][0][:, j, :], ALU.subtract).then_inc(self.lo, 1)

        a = Carve()
        a_wraw = a.f32(CT, C)
        a_w = (a.f16(CT, C), a.f16(CT, C))
        a_x = [a.f32(SUB, C) for _ in range(2)]
        a_xn = [a.f32(SUB, C) for _ in range(2)]
        a_xT = [(a.f16(CT, T), a.f16(CT, T)) for _ in range(2)]
        a_cos = [a.f32(SUB, HALF) for _ in range(2)]
        a_sin = [a.f32(SUB, HALF) for _ in range(2)]
        a_bias = a.f32(C)
        a_b16 = (a.f16(C), a.f16(C))
        a_sel = a.f16(P)
        a_ksum = a.f32(C)
        a_exp = [a.f32(C) for _ in range(2)]
        a_relu = [a.f32(C) for _ in range(2)]
        a_k = [a.f32(C) for _ in range(SUB)]
        a_rc = [a.f32(C) for _ in range(2)]
        a_rs = [a.f32(C) for _ in range(2)]
        a_kr = [a.f32(C) for _ in range(SUB)]
        zeros16 = a.f16(512)
        A_END = 30720
        assert a.at <= A_END
        a_xload = [sem(f"a_xload{u}", None) for u in range(2)]
        a_tabs = [sem(f"a_tabs{u}", None) for u in range(2)]
        a_wload = sem("a_wload", None)
        a_consts = sem("a_consts", "pool")
        a_eye = sem("a_eye", "pool")
        a_whi = sem("a_whi", "act")
        a_wlo = sem("a_wlo", "dve")
        a_store = [sem(f"a_store{u}", "sp") for u in range(2)]
        a_edge = sem("a_edge", None)
        a_kps = sem("a_kps", "pe")
        a_selset = sem("a_selset", "pool")
        a_kadd = sem("a_kadd", "pool")
        a_sumdone = sem("a_sumdone", "pe")
        a_acts = sem("a_acts", "act")
        a_kdone = sem("a_kdone", "dve")
        a_rot = sem("a_rot", "pool")
        a_krdone = sem("a_krdone", "dve")
        a_kvdone = sem("a_kvdone", "pe")
        A = Norm("a", a_x, a_xn, a_xT, a_xload)

        top = Carve(A_END)
        b_w = (top.f16(CT, C), top.f16(CT, C))
        b_lw = (top.f16(4 * CT, C), top.f16(4 * CT, C))
        raw_at = top.at
        b_lraw = top.f32(3 * CT, C)
        b_xT = (top.f16(CT, HALO), top.f16(CT, HALO))
        b_mix = Carve(top.at).f32(2, C)
        b_V = [None] * 4
        for k in (2, 3):
            b_V[k] = (top.f16(CT, PAIRS), top.f16(CT, PAIRS))
        under = Carve(raw_at + 2 * CT * C)
        for k in (0, 1):
            b_V[k] = (under.f16(CT, PAIRS), under.f16(CT, PAIRS))
        assert under.at <= raw_at + 3 * CT * C
        CONV_BANKS = (4, 5, 7, 4, 5, 7, 4, 5)
        b_wraw = a_wraw
        b = Carve()
        f_sum = [b.f32(4 * C) for _ in range(2)]
        b_x32 = b.f32(CT, HALO)
        b_v32 = [b.f32(CT, PAIRS) for _ in range(2)]
        b_x = [b.f32(SUB, C) for _ in range(2)]
        even, odd = (b_x32.rearrange("p j (i e) -> p j i e", e=2)[:, :, :, e] for e in range(2))
        d0, d1 = even[:, :, 0:PAIRS], odd[:, :, 0:PAIRS]
        d2, d3 = even[:, :, 1:PAIRS + 1], odd[:, :, 1:PAIRS + 1]
        b_cos = [b.f32(2, T) for _ in range(2)]
        b_sin = [b.f32(2, T) for _ in range(2)]
        b_exp = [b.f32(T) for _ in range(2)]
        b_relu = [b.f32(T) for _ in range(2)]
        b_q = b.f32(4, T)
        b_qr = b.f32(4, T)
        b_ec, b_oc = b_qr[:, 0:2, :], b_qr[:, 2:4, :]
        under = Carve(b.at)
        b_os = b.f32(2, T)
        b_es = b.f32(2, T)
        b_q16 = (under.f16(4, T), under.f16(4, T))
        assert under.at == b.at
        b_kv = b.f32(4, P)
        b_km = b.f32(4, NH)
        b_km16 = (b.f16(4, NH), b.f16(4, NH))
        b_bq = b.f32(4)
        b_lrow = b.f32(C)
        b_den = b.f32(SUB, NH)
        b_z = b.f32(SUB, NH)
        b_t = [b.f32(C) for _ in range(2)]
        f_raw = b.f32(4 * C)
        f_signs = b.f16(4 * C)
        assert b.at <= A_END
        b_qwlo = sem("b_qwlo", "dve")
        b_qwhi = sem("b_qwhi", "act")
        b_qload = sem("b_qload", None)
        b_lowload = sem("b_lowload", None)
        b_xT_load = sem("b_xT_load", None)
        b_mixed = sem("b_mixed", "dve")
        b_x32_ready = sem("b_x32_ready", "pool")
        b_v_dve = sem("b_v_dve", "dve")
        b_v_pool = sem("b_v_pool", "pool")
        b_vhi = sem("b_vhi", "act")
        b_vlo = sem("b_vlo", "dve")
        b_convps = sem("b_convps", "pe")
        b_gathered = sem("b_gathered", "dve")
        d_b2load = sem("d_b2load", None)
        b_wload = sem("b_wload", None)
        b_whi = sem("b_whi", "act")
        b_wlo = sem("b_wlo", "dve")
        b_kvset = sem("b_kvset", "dve")
        b_load = [sem(f"b_load{u}", None) for u in range(2)]
        b_qps = sem("b_qps", "pe")
        b_acts = sem("b_acts", "act")
        b_qdone = sem("b_qdone", "dve")
        b_mdve = sem("b_mdve", "dve")
        b_mpool = sem("b_mpool", "pool")
        b_rope = sem("b_rope", "dve")
        b_qhi = sem("b_qhi", "act")
        b_qlo = sem("b_qlo", "dve")
        b_zps = sem("b_zps", "pe")
        b_zstep = sem("b_zstep", "dve")
        b_aps = sem("b_aps", "pe")
        b_xb = sem("b_xb", "pool")
        b_tstep = sem("b_tstep", "dve")
        b_att_added = sem("b_att_added", "dve")
        b_store = [sem(f"b_store{u}", "sp") for u in range(2)]

        kvc = Carve()
        kp = (kvc.f16(CT, KT * P), kvc.f16(CT, KT * P))
        vp = (kvc.f16(KT, C), kvc.f16(KT, C))
        s = Carve(kvc.at)
        s_A = (s.f16(CT, C), s.f16(CT, C))
        s_B = (s.f16(CT, C), s.f16(CT, C))
        s_ctxp = [(s.f16(CT, T), s.f16(CT, T)) for _ in range(2)]
        s_ctx0 = s.f32(CT, T)
        s_bvw = s.f32(4, P)
        s_uw = s.f32(4, P)
        s_u = s.f16(4, 2)
        s_kb = s.f32(4)
        assert s.at <= raw_at
        s_raw = [Carve(raw_at + 2048 * k).f32(CT, C) for k in range(4)]
        s_ctx = [s_ctx0, Carve(raw_at + 8192).f32(CT, T)]
        s_wload = sem("s_wload", None)
        s_vload = sem("s_vload", None)
        s_prod = sem("s_prod", "pe")
        s_hi = sem("s_hi", "act")
        s_lo = sem("s_lo", "dve")
        s_uw_ready = sem("s_uw_ready", "dve")
        s_tailps = sem("s_tailps", "pe")
        s_tailhi = sem("s_tailhi", "act")
        s_taillo = sem("s_taillo", "dve")
        s_tailstore = sem("s_tailstore", "sp")
        s_tbias = sem("s_tbias", "dve")
        tail_k_v = tail_k[:, :].rearrange("p (j k) -> p j k", j=CT)
        s_bvw_ready = sem("s_bvw_ready", "dve")
        s_load = [sem(f"s_load{u}", None) for u in range(2)]
        s_chi = sem("s_chi", "act")
        s_clo = sem("s_clo", "dve")
        s_kps = sem("s_kps", "pe")
        s_khi = sem("s_khi", "act")
        s_klo = sem("s_klo", "dve")
        s_vps = sem("s_vps", "pe")
        s_vhi = sem("s_vhi", "act")
        s_vlo = sem("s_vlo", "dve")
        s_bps = sem("s_bps", "pe")
        s_kbs = sem("s_kbs", "dve")
        f_load = sem("f_load", None)
        f_sign = sem("f_sign", "act")
        f_abs = sem("f_abs", "act")
        f_zero = sem("f_zero", "pool")
        f_add = sem("f_add", "dve")
        f_store = sem("f_store", "act")
        f_fold = sem("f_fold", "dve")
        f_aps = sem("f_aps", "pe")
        f_alpha = sem("f_alpha", "dve")

        c = Carve(kvc.at)
        c_S = c.f32(KT, T)
        c_xT = [(c.f16(CT, T), c.f16(CT, T))] * 2
        c_x = [c.f32(SUB, C) for _ in range(2)]
        c_xn = [c.f32(SUB, C)] * 2
        c_ph = [c.f16(T) for _ in range(RING)]
        s_tv = [ph[:, 0:C] for ph in c_ph[0:2]]
        c_diag = Carve(c.at).f32(SUB, P)
        c_pl = [c.f16(T) for _ in range(RING)]
        c_mx = c.f32(T)
        c_mb = c_mx
        c_sum = c.f32(T)
        c_mcol = c.f32(SUB)
        c_mtile = c.f32(SUB)
        c_rinv = c.f32(SUB)
        c_den = c.f32(SUB)
        c_ts = c.f32(SUB, KX)
        c_tmax = c.f32(SUB)
        c_td = c.f32(SUB, KX)
        c_tp = c.f32(SUB, KX)
        c_tsum = c.f32(SUB)
        c_th = c.f16(SUB, KX)
        c_t3 = c.f32(SUB, 3 * KX)
        c_tT = c.f16(T)
        c_tailps = sem("c_tailps", "pe")
        c_tstep = sem("c_tstep", "dve")
        c_tailexp = sem("c_tailexp", "act")
        c_tail_turned = sem("c_tail_turned", "pe")
        c_tail_rows = sem("c_tail_rows", "act")
        c_load = [sem(f"c_load{u}", None) for u in range(2)]
        c_scoreps = sem("c_scoreps", "pe")
        c_score = sem("c_score", "act")
        c_max = sem("c_max", "dve")
        c_max_turned = sem("c_max_turned", "pe")
        c_mstep = sem("c_mstep", "dve")
        c_mps = sem("c_mps", "pe")
        c_mb_ready = sem("c_mb_ready", "dve")
        c_sub = sem("c_sub", "dve")
        c_exp = sem("c_exp", "act")
        c_hi = sem("c_hi", "dve")
        c_lo = sem("c_lo", "dve")
        c_pv = sem("c_pv", "pe")
        c_out = sem("c_out", "pe")
        c_add = sem("c_add", "pool")
        c_sumps = sem("c_sumps", "pe")
        c_rinvstep = sem("c_rinvstep", "dve")
        c_xb = sem("c_xb", "pool")
        c_x2 = sem("c_x2", "dve")
        c_store = [sem(f"c_store{u}", "sp") for u in range(2)]
        Cn = Norm("c", c_x, c_xn, c_xT, c_load)

        e = Carve()
        d_w1 = e.f16(CT, H)
        d_w2 = e.f16(HT, C)
        d_x0 = e.f32(SUB, C)
        d_xn = [e.f32(SUB, C)] * 2
        assert e.at <= CT * KT * P
        e = Carve(kvc.at)
        d_xT = [(e.f16(CT, T), e.f16(CT, T))] * 2
        d_gh = e.f16(HT, T)
        d_gl = e.f16(HT, T)
        d_g = [e.f32(T) for _ in range(2)]
        d_t = [e.f32(C) for _ in range(2)]
        d_b2 = e.f32(C)
        assert e.at <= kvc.at + KT * T
        d_x = [d_x0, Carve(kvc.at + KT * T).f32(SUB, C)]
        d_wload = sem("d_wload", None)
        d_load = [sem(f"d_load{u}", None) for u in range(2)]
        d_hps = sem("d_hps", "pe")
        d_gelu = sem("d_gelu", "act")
        d_ghi = sem("d_ghi", "dve")
        d_glo = sem("d_glo", "dve")
        d_f2 = sem("d_f2", "pe")
        d_ops = sem("d_ops", "pe")
        d_xb = sem("d_xb", "pool")
        d_ts = sem("d_ts", "dve")
        d_out = sem("d_out", "dve")
        d_store = [sem(f"d_store{u}", "sp") for u in range(2)]
        Dn = Norm("d", d_x, d_xn, d_xT, d_load)

        def after_a(eng):
            eng.wait_ge(a_kvdone, HEAD + 4 * NB)
            eng.wait_ge(a_krdone, HEAD + 4 * NB)
            eng.wait_ge(a_sumdone, HEAD + 1)
            for u in range(2):
                eng.wait_ge(a_store[u], HEAD + 16 * NB)

        def after_b(eng):
            eng.wait_ge(b_gathered, HEAD + 8 * NB)
            eng.wait_ge(b_aps, HEAD + 4 * NB)
            eng.wait_ge(f_store, HEAD + 16 * NB)
            for u in range(2):
                eng.wait_ge(b_store[u], HEAD + 16 * NB // 2)

        CH = M // T

        def after_s(eng):
            eng.wait_ge(s_klo, HEAD + 4 * (CH + 1))
            eng.wait_ge(s_vlo, HEAD + KT)
            eng.wait_ge(s_kbs, HEAD + 2 * (CH + 1))
            eng.wait_ge(s_taillo, HEAD + 4)
            eng.wait_ge(s_tbias, HEAD + 1)
            eng.wait_ge(f_alpha, HEAD + 3)

        def after_scores(eng):
            eng.wait_ge(c_lo, HEAD + KT * NB)
            eng.wait_ge(c_add, HEAD + (KT - 1) * NB)

        block = ctx.enter_context(nc.Block())

        @block.sync
        def _(sp):
            start("sp", sp)

            def pair_loop(body):
                with sp.Fori(0, NB // 2 - 1) as i:
                    body(i, False)
                body(NB // 2 - 1, True)

            def load_tables(n, u):
                sp.dma_start(a_cos[u], one(cos_v, n)).then_inc(a_tabs[u], 16)
                sp.dma_start(a_sin[u], one(sin_v, n)).then_inc(a_tabs[u], 16)

            sp.dma_start(a_x[0], one(x_v, 0)).then_inc(a_xload[0], 16)
            sp.dma_start(a_wraw, rows("wk_rope")).then_inc(a_wload, 16)
            sp.dma_start(a_bias, row_of("bk_rope")).then_inc(a_wload, 16)
            sp.dma_start(a_cos[0], one(cos_v, 0)).then_inc(a_tabs[0], 16)
            sp.dma_start(a_sin[0], one(sin_v, 0)).then_inc(a_tabs[0], 16)
            sp.dma_start(a_x[1], one(x_v, 1)).then_inc(a_xload[1], 16)
            sp.dma_start(b_lraw, d["lepe_w"].rearrange("(j p) n -> p j n", p=P)).then_inc(b_wload, 16)
            sp.wait_ge(a_consts, HEAD + 1)
            for v in xT_v:
                for col in (0, EDGE + N):
                    sp.dma_start(v[:, :, col:col + EDGE],
                                 zeros16[:, 0:CT * EDGE].rearrange("p (j o) -> p j o", j=CT)).then_inc(a_edge, 16)

            def store_xT(n, u):
                sp.wait_ge(A.lo, HEAD + 4 * n + 4)
                for k in range(2):
                    sp.dma_start(xT_v[k][:, :, bass.ds(n * T + EDGE, T)], a_xT[u][k]).then_inc(a_store[u], 16)

            store_xT(0, 0)
            sp.wait_ge(a_wlo, HEAD + CT)
            sp.dma_start(b_wraw, rows("wq_rope")).then_inc(b_qload, 16)

            def body_a(i, last):
                for u in range(2):
                    n = 2 * i + u
                    if not last:
                        sp.wait_ge(A.xn_ready, HEAD + 4 * n + 4)
                        sp.dma_start(a_x[u], one(x_v, n + 2)).then_inc(a_xload[u], 16)
                    if not (last and u):
                        sp.wait_ge(a_krdone, HEAD + 4 * n)
                        load_tables(n + 1, 1 - u)
                        store_xT(n + 1, 1 - u)

            pair_loop(body_a)

            sp.wait_ge(a_edge, 64)
            sp.wait_ge(a_store[0], HEAD + 32)
            sp.wait_ge(a_store[1], HEAD + 32)

            def load_xT(n):
                for k in range(2):
                    sp.dma_start(b_xT[k], xT_v[k][:, :, bass.ds(n * T + EDGE - 1, HALO)]).then_inc(b_xT_load, 16)

            def pairs(v, n):
                return v[bass.ds(n, 1)].rearrange("b p h f -> (b p) h f")

            def load_b(n, u):
                sp.dma_start(b_cos[u], cosT_v[:, :, bass.ds(n * T, T)]).then_inc(b_load[u], 16)
                sp.dma_start(b_sin[u], sinT_v[:, :, bass.ds(n * T, T)]).then_inc(b_load[u], 16)
                sp.dma_start(b_x[u].rearrange("p (h e) c -> p h (e c)", h=2), pairs(xp_v, n)).then_inc(b_load[u], 16)

            load_xT(0)
            after_a(sp)
            sp.dma_start(b_bq, d["bq_rope"]).then_inc(b_lowload, 16)
            sp.dma_start(b_lrow, row_of("lepe_b")).then_inc(b_lowload, 16)
            load_b(0, 0)

            def body_b(i, last):
                for u in range(2):
                    n = 2 * i + u
                    if last and u == 0:
                        sp.wait_ge(b_wlo, HEAD + 4 * CT)
                        for k, name in enumerate(("xk", "xq")):
                            sp.dma_start(s_raw[k], rows(name)).then_inc(s_wload, 16)
                        sp.dma_start(s_bq[:, :], d["xbq"]).then_inc(s_wload, 16)
                        sp.dma_start(s_bv[:, :], d["xbv"]).then_inc(s_wload, 16)
                        sp.dma_start(attn_row[:, :], row_of("xbo")).then_inc(s_wload, 16)
                    if not (last and u):
                        sp.wait_ge(b_rope, HEAD + 2 * n)
                        sp.wait_ge(b_store[1 - u], HEAD + 16 * (i + u))
                        load_b(n + 1, 1 - u)
                        sp.wait_ge(b_qps, HEAD + 4 * n + 4)
                        sp.wait_ge(b_x32_ready, HEAD + 4 * n + 4)
                        load_xT(n + 1)
                    sp.wait_ge(b_gathered, HEAD + 8 * n + 8)
                    sp.dma_start(pairs(x1p_v, n), b_x[u].rearrange("p (h e) c -> p h (e c)", h=2)).then_inc(b_store[u], 16)

            pair_loop(body_b)

            after_b(sp)
            for k, name in ((2, "xv"), (3, "xoT")):
                sp.dma_start(s_raw[k], rows(name)).then_inc(s_vload, 16)
            ctxT_v = rows("ctxT")

            def load_s(n, u):
                sp.dma_start(s_ctx[u], ctxT_v[:, :, bass.ds(n * T, T)]).then_inc(s_load[u], 16)

            load_s(0, 0)
            load_s(1, 1)
            with sp.Fori(0, CH // 2 - 1) as i:
                sp.wait_ge(s_clo, HEAD + 8 * i + 4)
                load_s(2 * i + 2, 0)
                sp.wait_ge(s_clo, HEAD + 8 * i + 8)
                load_s(2 * i + 3, 1)
            sp.wait_ge(s_prod, HEAD + 10)

            def load_c(n, u):
                sp.dma_start(c_x[u], one(x1_v, n)).then_inc(c_load[u], 16)

            load_c(0, 0)
            sp.wait_ge(s_clo, HEAD + 4 * (CH - 1))
            sp.dma_start(s_ctx[0][:, :, 0:M - CH * T], ctxT_v[:, :, CH * T:M]).then_inc(s_load[0], 16)
            sp.wait_ge(s_taillo, HEAD + 4)
            for k, part in enumerate((0, 1, 0)):
                sp.dma_start(tail_v[k * KX:(k + 1) * KX, :], s_tv[part][0:KX, :]).then_inc(s_tailstore, 16)

            after_s(sp)
            sp.wait_ge(s_tailstore, HEAD + 48)

            def body_c(i, last):
                for u in range(2):
                    n = 2 * i + u
                    if not (last and u):
                        sp.wait_ge(c_store[1 - u], HEAD + 16 * (i + u))
                        load_c(n + 1, 1 - u)
                    if last and u:
                        sp.wait_ge(c_scoreps, HEAD + KT * NB)
                        sp.dma_start(d_x[0], one(x2_v, 0)).then_inc(d_load[0], 16)
                        signs = d["signs"].rearrange("(g w) p n -> w p g n", w=2)
                        sp.dma_start(d_w1, signs[0]).then_inc(d_wload, 16)
                        sp.dma_start(d_w2.rearrange("p (g k) n -> p g (k n)", g=4), signs[1]).then_inc(d_wload, 16)
                    sp.wait_ge(c_x2, HEAD + 4 * n + 4)
                    sp.dma_start(one(x2_v, n), c_x[u]).then_inc(c_store[u], 16)

            pair_loop(body_c)

            after_scores(sp)
            sp.dma_start(d_b2, row_of("b2")).then_inc(d_b2load, 16)

            def load_d(n, u):
                sp.dma_start(d_x[u], one(x2_v, n)).then_inc(d_load[u], 16)

            def body_d(i, last):
                for u in range(2):
                    n = 2 * i + u
                    if not (last and u):
                        sp.wait_ge(d_store[1 - u], HEAD + 16 * (i + u))
                        load_d(n + 1, 1 - u)
                    sp.wait_ge(d_out, HEAD + 4 * n + 4)
                    sp.dma_start(one(out_v, n), d_x[u]).then_inc(d_store[u], 16)

            for u in range(2):
                sp.wait_ge(c_store[u], HEAD + 16 * NB // 2)
            pair_loop(body_d)
            for u in range(2):
                sp.wait_ge(d_store[u], HEAD + 16 * NB // 2)

        @block.gpsimd
        def _(pool):
            nc.gpsimd.memset(zeros16, 0.0).then_inc(a_consts, 1)
            start("pool", pool)
            nc.gpsimd.memset(a_sel, 0.0).then_inc(a_selset, 1)
            pool.wait_ge(a_selset, HEAD + 1)
            nc.gpsimd.memset(a_sel[0:2, :], 1.0).then_inc(a_selset, 1)
            nc.gpsimd.memset(a_ksum, 0.0).then_inc(a_kadd, 1)
            nc.gpsimd.memset(ident[:, :], 0.0).then_inc(a_eye, 1)
            nc.gpsimd.memset(ones[:, :], 1.0).then_inc(a_eye, 1)
            pool.wait_ge(a_eye, HEAD + 2)
            nc.gpsimd.affine_select(out=ident[:, :], in_=ident[:, :], compare_op=ALU.not_equal, fill=1.0,
                                    base=0, pattern=[[-1, P]], channel_multiplier=1).then_inc(a_eye, 1)

            def pair_loop(body):
                with pool.Fori(0, NB // 2 - 1) as i:
                    body(i, False)
                body(NB // 2 - 1, True)

            def body_a(i, last):
                for u in range(2):
                    n = 2 * i + u
                    pool.wait_ge(a_tabs[u], 32 * i + 32)
                    for t in range(SUB):
                        pool.wait_ge(a_kdone, HEAD + 4 * n + t + 1)
                        pool.wait_ge(a_krdone, HEAD + 4 * n + t - 1)
                        k2 = a_k[t].rearrange("p (h c) -> p h c", h=2)
                        tab = a_cos[u][:, t, :].rearrange("p (o c) -> p o c", o=1).to_broadcast([P, 2, HALF])
                        nc.gpsimd.tensor_tensor(a_rc[t % 2].rearrange("p (h c) -> p h c", h=2), k2, tab, ALU.mult)
                        nc.gpsimd.tensor_tensor(a_rs[t % 2][:, 0:HALF], a_k[t][:, HALF:C], a_sin[u][:, t, :], ALU.mult)
                        nc.gpsimd.tensor_tensor(a_rs[t % 2][:, HALF:C], a_k[t][:, 0:HALF], a_sin[u][:, t, :],
                                                ALU.mult).then_inc(a_rot, 1)
                        if t < SUB - 1:
                            pool.wait_ge(a_kadd, HEAD + (SUB - 1) * n + t + 1)
                            nc.gpsimd.tensor_tensor(a_ksum, a_ksum, a_k[t], ALU.add).then_inc(a_kadd, 1)

            pair_loop(body_a)

            after_a(pool)

            def add_xT(n):
                pool.wait_ge(b_xT_load, 32 * n + 32)
                pool.wait_ge(b_v_dve, HEAD + 2 * n)
                pool.wait_ge(b_v_pool, HEAD + 2 * n)
                nc.gpsimd.tensor_tensor(b_x32, b_xT[0], b_xT[1], ALU.add).then_inc(b_x32_ready, 4)

            def transform(n, k):
                pool.wait_ge(b_x32_ready, HEAD + 4 * n + 4)
                pool.wait_ge(b_vlo, HEAD + 4 * n + k - 1)
                left, right = ((d0, d2), (d3, d1))[k - 2]
                nc.gpsimd.tensor_tensor(b_v32[k % 2], left, right, ALU.subtract).then_inc(b_v_pool, 1)

            add_xT(0)
            pool.wait_ge(b_qwlo, HEAD + CT)
            for u in range(2):
                nc.gpsimd.memset(f_sum[u], 0.0).then_inc(f_zero, 1)
            pool.wait_ge(b_lowload, 32)

            def body_b(i, last):
                for u in range(2):
                    n = 2 * i + u
                    pool.wait_ge(f_add, HEAD + n)
                    pool.dma_start(f_raw, d["ffn_w"][bass.ds(n, 1)].rearrange("g p n -> (g p) n")).then_inc(f_load, 16)
                    transform(n, 2)
                    pool.wait_ge(b_load[u], 48 * i + 48)
                    for t in range(SUB):
                        nc.gpsimd.tensor_tensor(b_x[u][:, t, :], b_x[u][:, t, :], b_lrow, ALU.add).then_inc(b_xb, 1)
                    pool.wait_ge(b_qdone, HEAD + 4 * n + 4)
                    pool.wait_ge(b_rope, HEAD + 2 * n)
                    pool.wait_ge(b_aps, HEAD + 4 * n)
                    nc.gpsimd.tensor_tensor(b_oc, b_q[:, 2:4, :], b_cos[u], ALU.mult)
                    nc.gpsimd.tensor_tensor(b_es, b_q[:, 0:2, :], b_sin[u], ALU.mult).then_inc(b_mpool, 1)
                    transform(n, 3)
                    if not (last and u):
                        add_xT(n + 1)

            pair_loop(body_b)

            after_s(pool)

            def body_c(i, last):
                for u in range(2):
                    n = 2 * i + u
                    pool.wait_ge(Cn.xn_ready, HEAD + 4 * n + 4)
                    for t in range(SUB):
                        nc.gpsimd.tensor_tensor(c_x[u][:, t, :], c_x[u][:, t, :], attn_row[:, :], ALU.add).then_inc(c_xb, 1)
                    pool.wait_ge(c_sumps, HEAD + n)
                    for t in range(1, KT):
                        pool.wait_ge(c_exp, HEAD + KT * n + t + 1)
                        if t == 1:
                            nc.gpsimd.tensor_tensor(c_sum, c_S[:, 0, :], c_S[:, 1, :], ALU.add).then_inc(c_add, 1)
                        else:
                            pool.wait_ge(c_add, HEAD + (KT - 1) * n + t - 1)
                            nc.gpsimd.tensor_tensor(c_sum, c_sum, c_S[:, t, :], ALU.add).then_inc(c_add, 1)

            pair_loop(body_c)

            pool.wait_ge(d_b2load, 16)

            def body_d(i, last):
                for u in range(2):
                    n = 2 * i + u
                    pool.wait_ge(Dn.xn_ready, HEAD + 4 * n + 4)
                    for t in range(SUB):
                        nc.gpsimd.tensor_tensor(d_x[u][:, t, :], d_x[u][:, t, :], d_b2, ALU.add).then_inc(d_xb, 1)

            pair_loop(body_d)

        @block.scalar
        def _(act):
            start("act", act)
            act.dma_start(b1_col[:, :], d["b1"]).then_inc(a_wload, 16)

            def pair_loop(body):
                with act.Fori(0, NB // 2 - 1) as i:
                    body(i, False)
                body(NB // 2 - 1, True)

            A.scalar_sd(act, 0)
            act.wait_ge(a_wload, 48)
            for j in range(CT):
                nc.scalar.activation(a_w[0][:, j, :], a_wraw[:, j, :], ACT.Copy, scale=WS).then_inc(a_whi, 1)
            nc.scalar.activation(a_b16[0], a_bias, ACT.Copy, scale=WS).then_inc(a_whi, 1)
            A.scalar_hi(act, 0, 0)

            A.scalar_sd(act, 1)

            def hi_of(out, src, scale, signal):
                nc.scalar.activation(out, src, ACT.Copy, scale=scale).then_inc(signal, 1)

            def taps_hi(j, k):
                act.wait_ge(b_wload, 16)
                if k < 2:
                    act.wait_ge(b_mixed, HEAD + 2 * j + 2)
                src = (tile_of(b_lraw, CT + j), b_mix[:, 1, :], tile_of(b_lraw, j), tile_of(b_lraw, 2 * CT + j))[k]
                hi_of(tile_of(b_lw[0], k * CT + j), src, WS / 2 if k < 2 else WS, b_whi)

            def act_a(n, t):
                act.wait_ge(a_kps, HEAD + 4 * n + t + 1)
                act.wait_ge(a_kdone, HEAD + 4 * n + t - 1)
                nc.scalar.activation(a_exp[t % 2], bank[t % 2][:, :], ACT.Exp, scale=1 / WS)
                nc.scalar.activation(a_relu[t % 2], bank[t % 2][:, :], ACT.Relu, scale=1 / WS).then_inc(a_acts, 1)

            act_a(0, 0)
            act_a(0, 1)

            def body_a(i, last):
                for u in range(2):
                    n = 2 * i + u
                    more = not (last and u)
                    act_a(n, 2)
                    if more:
                        act.wait_ge(a_kps, HEAD + 4 * n)
                        act.wait_ge(a_store[1 - u], HEAD + 32 * (i + u))
                        A.scalar_hi(act, n + 1, 1 - u)
                    for k in ((2, 3), (0, 1))[u]:
                        taps_hi(i, k)
                    if last and u:
                        act.wait_ge(b_qload, 16)
                        for j in range(CT):
                            hi_of(b_w[0][:, j, :], b_wraw[:, j, :], WS, b_qwhi)
                    act_a(n, 3)
                    if not last:
                        A.scalar_sd(act, n + 2)
                    if more:
                        act_a(n + 1, 0)
                        act_a(n + 1, 1)

            pair_loop(body_a)

            after_a(act)
            act.wait_ge(b_lowload, 32)

            def v_hi(n, k):
                if k < 2:
                    act.wait_ge(b_v_dve, HEAD + 2 * n + k + 1)
                else:
                    act.wait_ge(b_v_pool, HEAD + 2 * n + k - 1)
                act.wait_ge(b_convps, HEAD + 8 * n + 2 * k - 6)
                nc.scalar.activation(b_V[k][0], b_v32[k % 2], ACT.Copy).then_inc(b_vhi, 1)

            v_hi(0, 0)
            v_hi(0, 1)

            def body_b(i, last):
                for u in range(2):
                    n = 2 * i + u
                    for t in range(4):
                        if t == 2:
                            v_hi(n, 2)
                        act.wait_ge(b_qps, HEAD + 4 * n + t + 1)
                        act.wait_ge(b_qdone, HEAD + 4 * n + t - 1)
                        nc.scalar.activation(b_exp[t % 2], bank[t % 2][:, :], ACT.Exp, bias=b_bq[:, t:t + 1], scale=1 / WS)
                        nc.scalar.activation(b_relu[t % 2], bank[t % 2][:, :], ACT.Relu, bias=b_bq[:, t:t + 1],
                                             scale=1 / WS).then_inc(b_acts, 1)
                    act.wait_ge(b_qdone, HEAD + 4 * n + 4)
                    act.wait_ge(b_rope, HEAD + 2 * n + 2)
                    nc.scalar.activation(b_q16[0], b_q, ACT.Copy).then_inc(b_qhi, 1)
                    act.wait_ge(f_store, HEAD + 16 * n)
                    act.wait_ge(f_load, 16 * n + 16)
                    nc.scalar.activation(f_signs, f_raw, ACT.Sign).then_inc(f_sign, 1)
                    nc.scalar.activation(f_raw, f_raw, ACT.Abs).then_inc(f_abs, 1)
                    act.wait_ge(f_sign, HEAD + n + 1)
                    act.dma_start(d["signs"][bass.ds(n, 1)].rearrange("g p n -> (g p) n"), f_signs).then_inc(f_store, 16)
                    v_hi(n, 3)
                    if not (last and u):
                        v_hi(n + 1, 0)
                        v_hi(n + 1, 1)

            pair_loop(body_b)

            after_b(act)
            for m in range(8):
                act.wait_ge(s_prod, HEAD + m + 1 + (m > 3))
                dst = s_A if m < 4 else s_B
                nc.scalar.activation(dst[0][:, m % 4, :], bank[m % 4][:, :], ACT.Copy, scale=WS).then_inc(s_hi, 1)
                if m == 3:
                    act.wait_ge(s_prod, HEAD + 5)
                    nc.scalar.activation(s_u[:, :, 0], bank[6][:, 0:4], ACT.Copy, scale=WS).then_inc(s_hi, 1)

            def ctx_hi(n, u, i, w):
                act.wait_ge(s_load[u], 16 * i + 16)
                act.wait_ge(s_vps, HEAD + 4 * n - 4)
                for j in range(CT):
                    nc.scalar.activation(s_ctxp[u][0][:, j, 0:w], s_ctx[u][:, j, 0:w], ACT.Copy).then_inc(s_chi, 1)

            def kprime_hi(n, w):
                for j in range(CT):
                    act.wait_ge(s_kps, HEAD + 4 * n + j + 1)
                    if w < T:
                        nc.scalar.activation(tail_k_v[:, j, 0:KX], bank[j][:, w:w + KX], ACT.Copy, scale=1 / WS)
                    nc.scalar.activation(kp[0][:, j, bass.ds(n * T, w)], bank[j][:, 0:w], ACT.Copy,
                                         scale=1 / WS).then_inc(s_khi, 1)

            def vprime_hi(n, nt):
                for q in range(nt):
                    act.wait_ge(s_vps, HEAD + 4 * n + q + 1)
                    nc.scalar.activation(vp[0][:, bass.ds(4 * n + q, 1), :].rearrange("p a c -> p (a c)"),
                                         bank[4 + q % 2][:, :], ACT.Copy, scale=1 / WS).then_inc(s_vhi, 1)

            ctx_hi(0, 0, 0, T)

            def body_s(i, last):
                for u in range(2):
                    n = 2 * i + u
                    if last and u:
                        Cn.scalar_sd(act, 0)
                    kprime_hi(n, T)
                    ctx_hi(n + 1, 1 - u, i + u, M - CH * T if last and u else T)
                    vprime_hi(n, 4)

            with act.Fori(0, CH // 2 - 1) as i:
                body_s(i, False)
            body_s(CH // 2 - 1, True)
            kprime_hi(CH, P)
            Cn.scalar_hi(act, 0, 0)
            act.wait_ge(s_vps, HEAD + KT)
            nc.scalar.activation(vp[0][:, KT - 1, :], bank[0][:, :], ACT.Copy, scale=1 / WS).then_inc(s_vhi, 1)
            act.wait_ge(s_tailps, HEAD + 1)
            nc.scalar.activation(s_tv[0][0:KX, :], bank[2][0:KX, :], ACT.Copy, scale=1 / WS).then_inc(s_tailhi, 1)

            after_s(act)

            def evac_scores(n):
                for t in range(KT):
                    act.wait_ge(c_scoreps, HEAD + KT * n + t + 1)
                    act.wait_ge(c_lo, HEAD + KT * n + t + 1 - KT)
                    act.wait_ge(c_add, HEAD + (KT - 1) * n + t + 1 - KT + (1 if t == 0 else 0))
                    nc.scalar.activation(c_S[:, t, :], bank[4 + t % 3][:, :], ACT.Identity,
                                         bias=key_bias[:, t:t + 1]).then_inc(c_score, 1)

            def exp(n, t):
                act.wait_ge(c_sub, HEAD + KT * n + t + 1)
                nc.scalar.activation(c_S[:, t, :], c_S[:, t, :], ACT.Exp, scale=SCALE).then_inc(c_exp, 1)

            evac_scores(0)
            exp(0, 0)
            exp(0, 1)

            def body_c(i, last):
                for u in range(2):
                    n = 2 * i + u
                    more = not (last and u)
                    nxt, nn = (Cn, n + 1) if more else (Dn, 0)
                    for t in range(2, KT):
                        if t == 4:
                            act.wait_ge(c_tstep, HEAD + 7 * n + 4)
                            nc.scalar.activation(c_tp, c_td, ACT.Exp, scale=SCALE).then_inc(c_tailexp, 1)
                        if t == 9:
                            nxt.scalar_sd(act, nn)
                        if t == 11:
                            act.wait_ge(c_tail_turned, HEAD + n + 1)
                            nc.scalar.activation(c_tT[0:3 * KX, :], bank[5][0:3 * KX, :], ACT.Copy).then_inc(c_tail_rows, 1)
                        if t == 19:
                            if not more:
                                act.wait_ge(c_lo, HEAD + KT * n + 4)
                                act.wait_ge(c_add, HEAD + (KT - 1) * n + 3)
                            nxt.scalar_hi(act, nn, 0)
                        exp(n, t)
                    if more:
                        evac_scores(n + 1)
                        exp(n + 1, 0)
                        exp(n + 1, 1)

            pair_loop(body_c)

            after_scores(act)

            def body_d(i, last):
                for u in range(2):
                    n = 2 * i + u
                    more = not (last and u)
                    for t in range(HT):
                        if more and t == 8:
                            Dn.scalar_sd(act, n + 1)
                        act.wait_ge(d_hps, HEAD + HT * n + t + 1)
                        act.wait_ge(d_glo, HEAD + HT * n + t - 1)
                        nc.scalar.activation(d_g[t % 2], bank[4 + t % 4][:, :], ACT.Gelu, bias=b1_col[:, t:t + 1],
                                             scale=alpha1[:, t:t + 1]).then_inc(d_gelu, 1)
                    if more:
                        Dn.scalar_hi(act, n + 1, 0)

            pair_loop(body_d)

        @block.vector
        def _(dve):
            start("dve", dve)

            def pair_loop(body):
                with dve.Fori(0, NB // 2 - 1) as i:
                    body(i, False)
                body(NB // 2 - 1, True)

            def lo_part(out, src, hi, scale):
                return nc.vector.scalar_tensor_tensor(out=out, in0=src, scalar=scale, in1=hi,
                                                      op0=ALU.mult, op1=ALU.subtract)

            A.vector_stats(dve, 0, 0, 0)
            A.vector_xn(0)
            dve.wait_ge(a_wload, 48)
            for j in range(CT):
                dve.wait_ge(a_whi, HEAD + j + 1)
                lo_part(a_w[1][:, j, :], a_wraw[:, j, :], a_w[0][:, j, :], WS).then_inc(a_wlo, 1)
            dve.wait_ge(a_whi, HEAD + CT + 1)
            lo_part(a_b16[1], a_bias, a_b16[0], WS).then_inc(a_wlo, 1)
            dve.wait_ge(a_wlo, HEAD + CT + 1)
            nc.vector.tensor_copy(a_b16[1][0:1, :], a_b16[0][0:1, :]).then_inc(a_wlo, 1)
            A.vector_lo(dve, 0, 0)

            def elu_a(n, t):
                dve.wait_ge(a_acts, HEAD + 4 * n + t + 1)
                if t < SUB - 1:
                    dve.wait_ge(a_kadd, HEAD + (SUB - 1) * (n - 1) + t + 2)
                else:
                    dve.wait_ge(a_kvdone, HEAD + 4 * n + t - 3)
                nc.vector.scalar_tensor_tensor(out=a_k[t], in0=a_exp[t % 2], scalar=1.0, in1=a_relu[t % 2],
                                               op0=ALU.min, op1=ALU.add).then_inc(a_kdone, 1)

            def rope_a(n, t):
                dve.wait_ge(a_rot, HEAD + 4 * n + t + 1)
                nc.vector.tensor_tensor(a_kr[t][:, 0:HALF], a_rc[t % 2][:, 0:HALF], a_rs[t % 2][:, 0:HALF], ALU.subtract)
                nc.vector.tensor_tensor(a_kr[t][:, HALF:C], a_rc[t % 2][:, HALF:C], a_rs[t % 2][:, HALF:C],
                                        ALU.add).then_inc(a_krdone, 1)

            def taps_lo(j, k):
                dve.wait_ge(b_whi, HEAD + 4 * j + (k + 2) % 4 + 1)
                src = (tile_of(b_lraw, CT + j), b_mix[:, 1, :], tile_of(b_lraw, j), tile_of(b_lraw, 2 * CT + j))[k]
                lo_part(tile_of(b_lw[1], k * CT + j), src, tile_of(b_lw[0], k * CT + j),
                        WS / 2 if k < 2 else WS).then_inc(b_wlo, 1)

            def mix_taps(j):
                g = [tile_of(b_lraw, tap * CT + j) for tap in range(3)]
                dve.wait_ge(b_wload, 16)
                dve.wait_ge(b_wlo, HEAD + 4 * j)
                nc.vector.tensor_tensor(b_mix[:, 0, :], g[0], g[2], ALU.add).then_inc(b_mixed, 1)
                dve.wait_ge(b_mixed, HEAD + 2 * j + 1)
                nc.vector.tensor_tensor(b_mix[:, 1, :], b_mix[:, 0, :], g[1], ALU.subtract)
                nc.vector.tensor_tensor(g[1], b_mix[:, 0, :], g[1], ALU.add).then_inc(b_mixed, 1)

            A.vector_moments(dve, 1, 1, 0)
            A.vector_rstd(dve, 1)
            elu_a(0, 0)

            def body_a(i, last):
                for u in range(2):
                    n = 2 * i + u
                    more = not (last and u)
                    if more:
                        dve.wait_ge(a_kvdone, HEAD + 4 * n)
                        A.vector_xn(1 - u)
                    rope_a(n, 0)
                    elu_a(n, 1)
                    if more:
                        A.vector_lo(dve, n + 1, 1 - u)
                    rope_a(n, 1)
                    elu_a(n, 2)
                    if u == 0:
                        mix_taps(i)
                    rope_a(n, 2)
                    elu_a(n, 3)
                    if not last:
                        A.vector_moments(dve, n + 2, u, i + 1)
                    rope_a(n, 3)
                    if not last:
                        A.vector_rstd(dve, n + 2)
                    if more:
                        elu_a(n + 1, 0)
                    for k in ((2, 3), (0, 1))[u]:
                        taps_lo(i, k)
                    if last and u:
                        dve.wait_ge(b_qload, 16)
                        for j in range(CT):
                            dve.wait_ge(b_qwhi, HEAD + j + 1)
                            lo_part(b_w[1][:, j, :], b_wraw[:, j, :], b_w[0][:, j, :], WS).then_inc(b_qwlo, 1)

            pair_loop(body_a)

            after_a(dve)
            kv_ps = bank[2][:, :].rearrange("p (t c) -> p t c", t=4)
            nc.vector.memset(b_kv, 0.0).then_inc(b_kvset, 1)
            nc.vector.memset(b_km, 0.0).then_inc(b_kvset, 1)
            dve.wait_ge(b_kvset, HEAD + 2)
            for h in range(2):
                o = h * DH
                nc.vector.tensor_scalar(b_kv[o:o + DH, :, o:o + DH], kv_ps[o:o + DH, :, o:o + DH],
                                        float(N) ** -0.5, None, ALU.mult)
            for g in range(4):
                for t in range(4):
                    last = nc.vector.tensor_scalar(b_km[32 * g:32 * g + 32, t, 4 * (t % 2) + g:4 * (t % 2) + g + 1],
                                                   bank[3][32 * g:32 * g + 32, t:t + 1], 1.0 / N, None, ALU.mult)
            last.then_inc(b_kvset, 1)
            dve.wait_ge(b_kvset, HEAD + 3)
            nc.vector.tensor_copy(b_km16[0], b_km).then_inc(b_kvset, 1)
            dve.wait_ge(b_kvset, HEAD + 4)
            nc.vector.tensor_tensor(b_km16[1], b_km, b_km16[0], ALU.subtract).then_inc(b_kvset, 1)
            def transform(n, k):
                dve.wait_ge(b_x32_ready, HEAD + 4 * n + 4)
                nc.vector.tensor_tensor(b_v32[k], d2, d1, (ALU.add, ALU.subtract)[k]).then_inc(b_v_dve, 1)

            def v_lo(n, k):
                dve.wait_ge(b_vhi, HEAD + 4 * n + k + 1)
                nc.vector.tensor_tensor(b_V[k][1], b_v32[k % 2], b_V[k][0], ALU.subtract).then_inc(b_vlo, 1)

            def transforms(n):
                transform(n, 0)
                transform(n, 1)
                v_lo(n, 0)
                v_lo(n, 1)

            def gather(n, u, k):
                dve.wait_ge(b_convps, HEAD + 8 * n + k + 1)
                if k < 2:
                    dve.wait_ge(b_xb, HEAD + 4 * n + 4)
                else:
                    dve.wait_ge(b_gathered, HEAD + 8 * n + k - 1)
                if k in (4, 5):
                    dve.wait_ge(b_att_added, HEAD + 4 * n + 2 * (k - 3))
                signs = ((1, 1), (1, -1), (1, 0), (0, 1))[k // 2]
                for e in range(2):
                    if signs[e]:
                        tile = b_x[u][:, 2 * (k % 2) + e, :]
                        last_op = nc.vector.scalar_tensor_tensor(out=tile, in0=bank[CONV_BANKS[k]][:, :],
                                                                 scalar=signs[e] / WS, in1=tile, op0=ALU.mult,
                                                                 op1=ALU.add)
                last_op.then_inc(b_gathered, 1)

            transforms(0)
            dve.wait_ge(f_zero, HEAD + 2)

            def body_b(i, last):
                for u in range(2):
                    n = 2 * i + u
                    dve.wait_ge(b_load[u], 48 * i + 48)
                    dve.wait_ge(b_zps, HEAD + n)
                    dve.wait_ge(b_mpool, HEAD + n)
                    for t in range(4):
                        if t == 2:
                            v_lo(n, 2)
                        dve.wait_ge(b_acts, HEAD + 4 * n + t + 1)
                        nc.vector.scalar_tensor_tensor(out=b_q[:, t, :], in0=b_exp[t % 2], scalar=1.0, in1=b_relu[t % 2],
                                                       op0=ALU.min, op1=ALU.add).then_inc(b_qdone, 1)
                    dve.wait_ge(b_qdone, HEAD + 4 * n + 4)
                    dve.wait_ge(b_aps, HEAD + 4 * n)
                    nc.vector.tensor_tensor(b_ec, b_q[:, 0:2, :], b_cos[u], ALU.mult)
                    nc.vector.tensor_tensor(b_os, b_q[:, 2:4, :], b_sin[u], ALU.mult).then_inc(b_mdve, 1)
                    dve.wait_ge(b_mdve, HEAD + n + 1)
                    nc.vector.tensor_tensor(b_qr[:, 0:2, :], b_ec, b_os, ALU.subtract).then_inc(b_rope, 1)
                    gather(n, u, 0)
                    dve.wait_ge(b_mpool, HEAD + n + 1)
                    nc.vector.tensor_tensor(b_qr[:, 2:4, :], b_oc, b_es, ALU.add).then_inc(b_rope, 1)
                    gather(n, u, 1)
                    dve.wait_ge(b_qhi, HEAD + n + 1)
                    nc.vector.tensor_tensor(b_q16[1], b_q, b_q16[0], ALU.subtract).then_inc(b_qlo, 1)
                    gather(n, u, 2)
                    gather(n, u, 3)
                    v_lo(n, 3)
                    dve.wait_ge(b_zps, HEAD + n + 1)
                    nc.vector.tensor_scalar(b_den, bank[6][:, 0:SUB * NH].rearrange("p (s h) -> p s h", s=SUB), 1e-6,
                                            None, ALU.add).then_inc(b_zstep, 1)
                    dve.wait_ge(b_zstep, HEAD + 2 * n + 1)
                    nc.vector.reciprocal(b_z, b_den).then_inc(b_zstep, 1)
                    dve.wait_ge(b_zstep, HEAD + 2 * n + 2)
                    dve.wait_ge(b_gathered, HEAD + 8 * n + 4)
                    for t in range(SUB):
                        z = b_z[:, t, :].rearrange("p (h o) -> p h o", o=1).to_broadcast([P, NH, DH])
                        dve.wait_ge(b_aps, HEAD + 4 * n + t + 1)
                        nc.vector.tensor_tensor(b_t[t % 2].rearrange("p (h c) -> p h c", h=NH),
                                                bank[2 + t % 2][:, :].rearrange("p (h c) -> p h c", h=NH),
                                                z, ALU.mult).then_inc(b_tstep, 1)
                        if t == 1:
                            dve.wait_ge(f_abs, HEAD + n + 1)
                            dve.wait_ge(f_add, HEAD + n - 1)
                            nc.vector.tensor_tensor(f_sum[u], f_sum[u], f_raw, ALU.add).then_inc(f_add, 1)
                        dve.wait_ge(b_tstep, HEAD + 4 * n + t + 1)
                        nc.vector.tensor_tensor(b_x[u][:, t, :], b_x[u][:, t, :], b_t[t % 2], ALU.add).then_inc(b_att_added, 1)
                        if t == 1:
                            gather(n, u, 4)
                    gather(n, u, 5)
                    if not (last and u):
                        transforms(n + 1)
                    gather(n, u, 6)
                    gather(n, u, 7)

            pair_loop(body_b)

            dve.wait_ge(s_wload, 5 * 16)
            after_b(dve)
            dve.wait_ge(f_add, HEAD + NB)
            nc.vector.tensor_tensor(f_sum[1][:, 0:2 * C], f_sum[1][:, 0:2 * C], f_sum[1][:, 2 * C:4 * C],
                                    ALU.add).then_inc(f_fold, 1)
            dve.wait_ge(f_fold, HEAD + 1)
            nc.vector.tensor_tensor(f_sum[1][:, 0:C], f_sum[1][:, 0:C], f_sum[1][:, C:2 * C], ALU.add).then_inc(f_fold, 1)
            for j in range(4):
                last = nc.vector.tensor_scalar(s_bvw[:, j, :], ones[:, :], s_bv[:, j:j + 1], None, ALU.mult)
            last.then_inc(s_bvw_ready, 1)
            def ctx_lo(n, u, w):
                for j in range(CT):
                    dve.wait_ge(s_chi, HEAD + 4 * n + j + 1)
                    nc.vector.tensor_tensor(s_ctxp[u][1][:, j, 0:w], s_ctx[u][:, j, 0:w], s_ctxp[u][0][:, j, 0:w],
                                            ALU.subtract).then_inc(s_clo, 1)

            for m in range(8):
                dve.wait_ge(s_hi, HEAD + m + 1 + (m > 3))
                dst = s_A if m < 4 else s_B
                lo_part(dst[1][:, m % 4, :], bank[m % 4][:, :], dst[0][:, m % 4, :], WS).then_inc(s_lo, 1)
                if m == 3:
                    dve.wait_ge(s_hi, HEAD + 5)
                    lo_part(s_u[:, :, 1], bank[6][:, 0:4], s_u[:, :, 0], WS).then_inc(s_lo, 1)
                    for j in range(4):
                        last = nc.vector.tensor_scalar(s_uw[:, j, :], ones[:, :], bank[6][:, j:j + 1], None, ALU.mult)
                    last.then_inc(s_uw_ready, 1)
            ctx_lo(0, 0, T)
            dve.wait_ge(f_aps, HEAD + 1)
            nc.vector.tensor_scalar(alpha1[:, :], bank[5][:, 0:HT], 1.0 / C, None, ALU.mult).then_inc(f_alpha, 1)
            dve.wait_ge(f_aps, HEAD + 2)
            nc.vector.tensor_scalar(alpha2_row[:, :], bank[4][:, :], 1.0 / H, None, ALU.mult).then_inc(f_alpha, 1)
            dve.wait_ge(s_prod, HEAD + 10)
            nc.vector.tensor_tensor(attn_row[:, :], bank[7][:, :], attn_row[:, :], ALU.add).then_inc(f_alpha, 1)

            def kprime_lo(n, w):
                for j in range(CT):
                    dve.wait_ge(s_khi, HEAD + 4 * n + j + 1)
                    if w < T:
                        lo_part(tail_k_v[:, j, KX:2 * KX], bank[j][:, w:w + KX], tail_k_v[:, j, 0:KX], 1 / WS)
                    lo_part(kp[1][:, j, bass.ds(n * T, w)], bank[j][:, 0:w], kp[0][:, j, bass.ds(n * T, w)],
                            1 / WS).then_inc(s_klo, 1)

            def vprime_lo(n, nt):
                for q in range(nt):
                    dve.wait_ge(s_vhi, HEAD + 4 * n + q + 1)
                    tile = bass.ds(4 * n + q, 1)
                    lo_part(vp[1][:, tile, :].rearrange("p a c -> p (a c)"), bank[4 + q % 2][:, :],
                            vp[0][:, tile, :].rearrange("p a c -> p (a c)"), 1 / WS).then_inc(s_vlo, 1)

            def bias(n, nt, sums=bank[6]):
                dve.wait_ge(s_bps, HEAD + n + 1)
                for q in range(nt):
                    last = nc.vector.tensor_reduce(s_kb[:, q:q + 1], sums[:, 2 * q:2 * q + 2], AX_X, ALU.add)
                last.then_inc(s_kbs, 1)
                dve.wait_ge(s_kbs, HEAD + 2 * n + 1)
                for q in range(nt):
                    last = nc.vector.tensor_scalar(key_bias[:, bass.ds(4 * n + q, 1)], s_kb[:, q:q + 1], 1 / WS, None,
                                                   ALU.mult)
                last.then_inc(s_kbs, 1)

            def body_s(i, last):
                for u in range(2):
                    n = 2 * i + u
                    if last and u:
                        Cn.vector_stats(dve, 0, 0, 0)
                        Cn.vector_xn(0)
                    kprime_lo(n, T)
                    ctx_lo(n + 1, 1 - u, M - CH * T if last and u else T)
                    bias(n, 4)
                    vprime_lo(n, 4)

            with dve.Fori(0, CH // 2 - 1) as i:
                body_s(i, False)
            body_s(CH // 2 - 1, True)
            kprime_lo(CH, P)
            Cn.vector_lo(dve, 0, 0)
            dve.wait_ge(s_vhi, HEAD + KT)
            lo_part(vp[1][:, KT - 1, :], bank[0][:, :], vp[0][:, KT - 1, :], 1 / WS).then_inc(s_vlo, 1)
            bias(CH, 1, bank[1])
            dve.wait_ge(s_tailhi, HEAD + 1)
            lo_part(s_tv[1][0:KX, :], bank[2][0:KX, :], s_tv[0][0:KX, :], 1 / WS).then_inc(s_taillo, 4)
            dve.wait_ge(s_tailps, HEAD + 2)
            nc.vector.tensor_copy(tail_bias[:, :], bank[3][:, 0:KX]).then_inc(s_tbias, 1)

            after_s(dve)

            def maximum(n):
                for t in range(1, KT):
                    dve.wait_ge(c_score, HEAD + KT * n + t + 1)
                    if t == 1:
                        nc.vector.tensor_tensor(c_mx, c_S[:, 0, :], c_S[:, 1, :], ALU.max).then_inc(c_max, 1)
                    else:
                        dve.wait_ge(c_max, HEAD + (KT - 1) * n + t - 1)
                        nc.vector.tensor_tensor(c_mx, c_mx, c_S[:, t, :], ALU.max).then_inc(c_max, 1)
                dve.wait_ge(c_tailps, HEAD + n + 1)
                nc.vector.tensor_reduce(c_ts, bank[5][:, 0:SUB * 2 * KX].rearrange("p (s h k) -> p s k h", s=SUB, h=2),
                                        AX_X, ALU.add).then_inc(c_tstep, 1)
                dve.wait_ge(c_tstep, HEAD + 7 * n + 1)
                nc.vector.tensor_tensor(c_ts, c_ts,
                                        tail_bias[:, :].rearrange("p (o k) -> p o k", o=1).to_broadcast([P, SUB, KX]),
                                        ALU.add).then_inc(c_tstep, 1)
                dve.wait_ge(c_tstep, HEAD + 7 * n + 2)
                nc.vector.tensor_reduce(c_tmax, c_ts, AX_X, ALU.max).then_inc(c_tstep, 1)
                dve.wait_ge(c_max_turned, HEAD + n + 1)
                nc.vector.tensor_reduce(c_mtile, bank[7][:, :].rearrange("p (s k) -> p s k", s=SUB), AX_X,
                                        ALU.max).then_inc(c_mstep, 1)
                dve.wait_ge(c_mstep, HEAD + 3 * n + 1)
                dve.wait_ge(c_tstep, HEAD + 7 * n + 3)
                nc.vector.tensor_tensor(c_mcol, c_mtile, c_tmax, ALU.max).then_inc(c_mstep, 1)
                dve.wait_ge(c_mstep, HEAD + 3 * n + 2)
                for q in range(SUB):
                    last_op = nc.vector.tensor_scalar(c_diag[:, q, :], ident[:, :], c_mcol[:, q:q + 1], None, ALU.mult)
                last_op.then_inc(c_mstep, 1)
                nc.vector.tensor_tensor(c_td, c_ts,
                                        c_mcol.rearrange("p (s o) -> p s o", o=1).to_broadcast([P, SUB, KX]),
                                        ALU.subtract).then_inc(c_tstep, 1)
                dve.wait_ge(c_mps, HEAD + n + 1)
                nc.vector.tensor_copy(c_mb, bank[7][:, :]).then_inc(c_mb_ready, 1)
                dve.wait_ge(c_mb_ready, HEAD + n + 1)

            def sub(t):
                nc.vector.tensor_tensor(c_S[:, t, :], c_S[:, t, :], c_mb, ALU.subtract).then_inc(c_sub, 1)

            def split(n, t):
                dve.wait_ge(c_exp, HEAD + KT * n + t + 1)
                dve.wait_ge(c_pv, HEAD + KT * n + t - RING + 1)
                nc.vector.tensor_copy(c_ph[t % RING], c_S[:, t, :]).then_inc(c_hi, 1)
                dve.wait_ge(c_hi, HEAD + KT * n + t + 1)
                nc.vector.tensor_tensor(c_pl[t % RING], c_S[:, t, :], c_ph[t % RING], ALU.subtract).then_inc(c_lo, 1)

            def first(n):
                sub(0)
                sub(1)
                split(n, 0)

            def tail(n):
                dve.wait_ge(c_tailexp, HEAD + n + 1)
                nc.vector.tensor_copy(c_th, c_tp).then_inc(c_tstep, 1)
                dve.wait_ge(c_tstep, HEAD + 7 * n + 5)
                nc.vector.tensor_copy(c_t3[:, :, 0:KX], c_th)
                nc.vector.tensor_copy(c_t3[:, :, KX:2 * KX], c_th)
                nc.vector.tensor_tensor(c_t3[:, :, 2 * KX:3 * KX], c_tp, c_th, ALU.subtract).then_inc(c_tstep, 1)
                nc.vector.tensor_reduce(c_tsum, c_tp, AX_X, ALU.add).then_inc(c_tstep, 1)

            def finish(n, u):
                dve.wait_ge(c_sumps, HEAD + n + 1)
                dve.wait_ge(c_tstep, HEAD + 7 * n + 7)
                nc.vector.tensor_tensor(c_den, bank[6][:, 0:SUB], c_tsum, ALU.add).then_inc(c_rinvstep, 1)
                dve.wait_ge(c_rinvstep, HEAD + 2 * n + 1)
                nc.vector.reciprocal(c_rinv, c_den).then_inc(c_rinvstep, 1)
                dve.wait_ge(c_rinvstep, HEAD + 2 * n + 2)
                dve.wait_ge(c_xb, HEAD + 4 * n + 4)
                for q in range(SUB):
                    if q < SUB - 1:
                        dve.wait_ge(c_out, HEAD + (SUB - 1) * n + q + 1)
                    else:
                        dve.wait_ge(c_pv, HEAD + KT * n + KT)
                    nc.vector.scalar_tensor_tensor(out=c_x[u][:, q, :], in0=bank[q][:, :], scalar=c_rinv[:, q:q + 1],
                                                   in1=c_x[u][:, q, :], op0=ALU.mult, op1=ALU.add).then_inc(c_x2, 1)

            maximum(0)
            dve.wait_ge(s_tailstore, HEAD + 48)
            first(0)

            def body_c(i, last):
                for u in range(2):
                    n = 2 * i + u
                    more = not (last and u)
                    nxt, nn, npar, ni = (Cn, n + 1, 1 - u, i + u) if more else (Dn, 0, 0, 0)
                    for t in range(2, KT + 1):
                        if t < KT:
                            sub(t)
                        split(n, t - 1)
                        if t == 5:
                            tail(n)
                        if t == 8:
                            nxt.vector_moments(dve, nn, npar, ni)
                        if t == 11:
                            nxt.vector_rstd(dve, nn)
                            nxt.vector_xn(npar)
                        if t == 21:
                            nxt.vector_lo(dve, nn, 0)
                    if more:
                        maximum(n + 1)
                        first(n + 1)
                    finish(n, u)

            pair_loop(body_c)

            after_scores(dve)

            def body_d(i, last):
                for u in range(2):
                    n = 2 * i + u
                    more = not (last and u)
                    for t in range(HT):
                        dve.wait_ge(d_gelu, HEAD + HT * n + t + 1)
                        if t < HT - 1:
                            dve.wait_ge(d_f2, HEAD + (HT - 1) * (n - 1) + t + 1)
                        else:
                            dve.wait_ge(d_ops, HEAD + 4 * n)
                        nc.vector.tensor_copy(d_gh[:, t, :], d_g[t % 2]).then_inc(d_ghi, 1)
                        dve.wait_ge(d_ghi, HEAD + HT * n + t + 1)
                        nc.vector.tensor_tensor(d_gl[:, t, :], d_g[t % 2], d_gh[:, t, :], ALU.subtract).then_inc(d_glo, 1)
                        if more and t == 7:
                            Dn.vector_stats(dve, n + 1, 1 - u, i + u)
                            Dn.vector_xn(1 - u)
                    if more:
                        Dn.vector_lo(dve, n + 1, 0)
                    dve.wait_ge(d_xb, HEAD + 4 * n + 4)
                    for q in range(SUB):
                        dve.wait_ge(d_ops, HEAD + 4 * n + q + 1)
                        nc.vector.tensor_tensor(d_t[q % 2], bank[q][:, :], alpha2_row[:, :], ALU.mult).then_inc(d_ts, 1)
                        dve.wait_ge(d_ts, HEAD + 4 * n + q + 1)
                        nc.vector.tensor_tensor(d_x[u][:, q, :], d_t[q % 2], d_x[u][:, q, :], ALU.add).then_inc(d_out, 1)

            pair_loop(body_d)

        @block.tensor
        def _(pe_block):
            pe = nc.tensor
            start("pe", pe_block)

            def pair_loop(body):
                with pe_block.Fori(0, NB // 2 - 1) as i:
                    body(i, False)
                body(NB // 2 - 1, True)

            pe_block.wait_ge(a_consts, HEAD + 1)
            pe_block.wait_ge(a_eye, HEAD + 3)
            for bk in (2, 3):
                pe.matmul(bank[bk][:, :], zeros16[:, 0:P], zeros16, start=True, stop=True, skip_group_check=True)
            A.tensor_turn(pe_block, 0, 0)
            pe_block.wait_ge(a_wlo, HEAD + CT + 2)
            pe_block.wait_ge(a_selset, HEAD + 2)

            def k_tile(n, u, t):
                pe_block.wait_ge(a_acts, HEAD + 4 * n + t - 1)
                pe.matmul(bank[t % 2][:, :], a_sel, a_b16[1], start=True, stop=False)
                for j in range(CT):
                    last = mm3(pe, bank[t % 2][:, :],
                               [a_xT[u][h][:, j, t * P:(t + 1) * P] for h in range(2)],
                               [a_w[h][:, j, :] for h in range(2)], False, j == CT - 1)
                last.then_inc(a_kps, 1)

            def sum_k(tile):
                for g in range(4):
                    mm = pe.matmul(bank[3][:, g:g + 1], tile[:, g * P:(g + 1) * P], ones[:, 0:1],
                                   start=False, stop=True, skip_group_check=True)
                return mm

            def kv_tile(n, u, t):
                pe_block.wait_ge(a_krdone, HEAD + 4 * n + t + 1)
                for g in range(4):
                    mm = pe.matmul(bank[2][:, g * P:(g + 1) * P], a_kr[t][:, g * P:(g + 1) * P],
                              a_xn[u][:, t, g * P:(g + 1) * P], start=False, stop=True, skip_group_check=True)
                if t == SUB - 1:
                    mm = sum_k(a_k[t])
                mm.then_inc(a_kvdone, 1)

            pe_block.wait_ge(A.lo, HEAD + 4)
            k_tile(0, 0, 0)
            k_tile(0, 0, 1)

            def body_a(i, last):
                for u in range(2):
                    n = 2 * i + u
                    more = not (last and u)
                    k_tile(n, u, 2)
                    if more:
                        A.tensor_turn(pe_block, n + 1, 1 - u)
                    kv_tile(n, u, 0)
                    k_tile(n, u, 3)
                    kv_tile(n, u, 1)
                    if more:
                        pe_block.wait_ge(A.lo, HEAD + 4 * n + 8)
                        k_tile(n + 1, 1 - u, 0)
                    kv_tile(n, u, 2)
                    if more:
                        k_tile(n + 1, 1 - u, 1)
                    kv_tile(n, u, 3)

            pair_loop(body_a)

            pe_block.wait_ge(a_kadd, HEAD + (SUB - 1) * NB + 1)
            sum_k(a_ksum).then_inc(a_sumdone, 1)

            def conv(n, k):
                if k == 0:
                    pe_block.wait_ge(b_gathered, HEAD + 8 * n - 1)
                elif k != 2:
                    pe_block.wait_ge(b_gathered, HEAD + 8 * n + (0 if k == 1 else k - 2))
                if k % 2 == 0:
                    pe_block.wait_ge(b_vlo, HEAD + 4 * n + k // 2 + 1)
                for j in range(CT):
                    last = mm3(pe, bank[CONV_BANKS[k]][:, :],
                               [b_V[k // 2][h][:, j, (k % 2) * P:(k % 2 + 1) * P] for h in range(2)],
                               [b_lw[h][:, k // 2 * CT + j, :] for h in range(2)], j == 0, j == CT - 1)
                last.then_inc(b_convps, 1)

            def tokens(v, g, t):
                return v[:, g, :].rearrange("p (h i e) -> p h e i", h=2, e=2)[:, t // 2, t % 2, :]

            def att(n, t):
                pe_block.wait_ge(b_rope, HEAD + 2 * n + 2)
                pe_block.wait_ge(b_tstep, HEAD + 4 * n + t - 1)
                for g in range(4):
                    last = pe.matmul(bank[2 + t % 2][:, g * P:(g + 1) * P], tokens(b_qr, g, t), b_kv[:, g, :],
                                     start=True, stop=True)
                last.then_inc(b_aps, 1)

            pe_block.wait_ge(b_qwlo, HEAD + CT)
            pe_block.wait_ge(a_acts, HEAD + 4 * NB)

            def body_b(i, last):
                for u in range(2):
                    n = 2 * i + u
                    pe_block.wait_ge(b_xT_load, 32 * n + 32)
                    for t in range(4):
                        pe_block.wait_ge(b_acts, HEAD + 4 * n + t - 1)
                        for j in range(CT):
                            mm = mm3(pe, bank[t % 2][:, :], [b_w[h][:, j, t * P:(t + 1) * P] for h in range(2)],
                                     [b_xT[h][:, j, 1:1 + T] for h in range(2)], j == 0, j == CT - 1)
                        mm.then_inc(b_qps, 1)
                    pe_block.wait_ge(b_wlo, HEAD + 4 * CT)
                    conv(n, 0)
                    conv(n, 1)
                    conv(n, 2)
                    conv(n, 3)
                    pe_block.wait_ge(b_kvset, HEAD + 3)
                    att(n, 0)
                    att(n, 1)
                    conv(n, 4)
                    pe_block.wait_ge(b_kvset, HEAD + 5)
                    pe_block.wait_ge(b_qlo, HEAD + n + 1)
                    for t in range(SUB):
                        for g in range(4):
                            mm = mm3(pe, bank[6][:, t * NH:(t + 1) * NH], [tokens(b_q16[h], g, t) for h in range(2)],
                                     [b_km16[h][:, g, :] for h in range(2)], g == 0, g == 3)
                    mm.then_inc(b_zps, 1)
                    conv(n, 5)
                    att(n, 2)
                    att(n, 3)
                    conv(n, 6)
                    conv(n, 7)

            pair_loop(body_b)

            pe_block.wait_ge(s_wload, 5 * 16)
            pe_block.wait_ge(b_gathered, HEAD + 8 * NB)
            for m in range(8):
                w, r = (s_raw[0], s_raw[1]) if m < 4 else (s_raw[2], s_raw[3])
                if m >= 4:
                    pe_block.wait_ge(s_lo, HEAD + m - 3)
                if m == 4:
                    pe_block.wait_ge(s_vload, 32)
                for j in range(CT):
                    mm = pe.matmul(bank[m % 4][:, :], w[:, j, (m % 4) * P:(m % 4 + 1) * P], r[:, j, :],
                                   start=j == 0, stop=j == CT - 1)
                mm.then_inc(s_prod, 1)
                if m == 3:
                    for g in range(4):
                        for j in range(CT):
                            mm = pe.matmul(bank[6][:, g:g + 1], w[:, j, g * P:(g + 1) * P], s_bq[:, j:j + 1],
                                           start=j == 0, stop=j == CT - 1)
                    mm.then_inc(s_prod, 1)
            pe_block.wait_ge(s_bvw_ready, HEAD + 1)
            for j in range(CT):
                mm = pe.matmul(bank[7][:, :], s_bvw[:, j, :], s_raw[3][:, j, :], start=j == 0, stop=j == CT - 1)
            mm.then_inc(s_prod, 1)
            pe_block.wait_ge(f_add, HEAD + NB)
            for t in range(HT):
                mm = pe.matmul(bank[5][:, t:t + 1], f_sum[0][:, t * P:(t + 1) * P], ones[:, 0:1], start=True, stop=True)
            mm.then_inc(f_aps, 1)
            pe_block.wait_ge(f_fold, HEAD + 2)
            pe.matmul(bank[4][:, :], ones[:, :], f_sum[1][:, 0:C], start=True, stop=True).then_inc(f_aps, 1)
            pe_block.wait_ge(s_lo, HEAD + 9)

            def k_chunk(n, u, w):
                pe_block.wait_ge(s_clo, HEAD + 4 * n + 4)
                for j in range(CT):
                    pe_block.wait_ge(s_klo, HEAD + 4 * n + j - 3)
                    for q in range(CT):
                        mm = mm3(pe, bank[j][:, 0:w], [s_A[h][:, q, j * P:(j + 1) * P] for h in range(2)],
                                 [s_ctxp[u][h][:, q, 0:w] for h in range(2)], q == 0, q == CT - 1)
                    mm.then_inc(s_kps, 1)

            def v_chunk(n, u, nt):
                pe_block.wait_ge(f_alpha, HEAD + 3)
                pe_block.wait_ge(s_kbs, HEAD + 2 * n)
                for t in range(nt):
                    for q in range(CT):
                        pe.matmul(bank[6][:, 2 * t:2 * t + 2], s_ctxp[u][0][:, q, t * P:(t + 1) * P], s_u[:, q, :],
                                  start=q == 0, stop=False)
                        mm = pe.matmul(bank[6][:, 2 * t:2 * t + 2], s_ctxp[u][1][:, q, t * P:(t + 1) * P], s_u[:, q, :],
                                       start=False, stop=q == CT - 1)
                mm.then_inc(s_bps, 1)
                for t in range(nt):
                    pe_block.wait_ge(s_vlo, HEAD + 4 * n + t - 1)
                    for q in range(CT):
                        mm = mm3(pe, bank[4 + t % 2][:, :], [s_ctxp[u][h][:, q, t * P:(t + 1) * P] for h in range(2)],
                                 [s_B[h][:, q, :] for h in range(2)], q == 0, q == CT - 1)
                    mm.then_inc(s_vps, 1)

            with pe_block.Fori(0, CH // 2) as i:
                for u in range(2):
                    k_chunk(2 * i + u, u, T)
                    v_chunk(2 * i + u, u, 4)
            k_chunk(CH, 0, P + KX)
            pe_block.wait_ge(s_vlo, HEAD + 4 * CH)
            pe_block.wait_ge(s_kbs, HEAD + 2 * CH)
            Cn.tensor_turn(pe_block, 0, 0)
            pe_block.wait_ge(s_klo, HEAD + 4 * CH + 4)
            for q in range(CT):
                mm = mm3(pe, bank[0][:, :], [s_ctxp[0][h][:, q, 0:P] for h in range(2)],
                         [s_B[h][:, q, :] for h in range(2)], q == 0, q == CT - 1)
            mm.then_inc(s_vps, 1)
            for q in range(CT):
                pe.matmul(bank[1][:, 0:2], s_ctxp[0][0][:, q, 0:P], s_u[:, q, :], start=q == 0, stop=False)
                mm = pe.matmul(bank[1][:, 0:2], s_ctxp[0][1][:, q, 0:P], s_u[:, q, :], start=False, stop=q == CT - 1)
            mm.then_inc(s_bps, 1)
            for q in range(CT):
                mm = mm3(pe, bank[2][0:KX, :], [s_ctxp[0][h][:, q, P:P + KX] for h in range(2)],
                         [s_B[h][:, q, :] for h in range(2)], q == 0, q == CT - 1)
            mm.then_inc(s_tailps, 1)
            pe_block.wait_ge(s_uw_ready, HEAD + 1)
            for q in range(CT):
                mm = pe.matmul(bank[3][:, 0:KX], s_uw[:, q, :], s_ctx[0][:, q, P:P + KX], start=q == 0, stop=q == CT - 1)
            mm.then_inc(s_tailps, 1)


            def scores(n):
                pe_block.wait_ge(Cn.lo, HEAD + 4 * n + 4)
                for t in range(KT):
                    if t >= 3:
                        pe_block.wait_ge(c_score, HEAD + KT * n + t - 2)
                    for j in range(CT):
                        mm = mm3(pe, bank[4 + t % 3][:, :], [kp[h][:, j, t * P:(t + 1) * P] for h in range(2)],
                                 [c_xT[0][h][:, j, :] for h in range(2)], j == 0, j == CT - 1)
                    mm.then_inc(c_scoreps, 1)
                pe_block.wait_ge(c_score, HEAD + KT * n + KT - 2)
                for q in range(SUB):
                    o = q * 2 * KX
                    for j in range(CT):
                        if j == CT - 1:
                            for k in range(CT):
                                pe.matmul(bank[5][:, o:o + KX], c_xT[0][1][:, k, q * P:(q + 1) * P],
                                          tail_k_v[:, k, 0:KX], start=False, stop=False)
                        mm = pe.matmul(bank[5][:, o:o + 2 * KX], c_xT[0][0][:, j, q * P:(q + 1) * P],
                                       tail_k_v[:, j, :], start=j == 0, stop=j == CT - 1)
                mm.then_inc(c_tailps, 1)

            def turn_max(n):
                pe_block.wait_ge(c_max, HEAD + (KT - 1) * (n + 1))
                for q in range(SUB):
                    mm = pe.transpose(bank[7][:, q * P:(q + 1) * P], c_mx[:, q * P:(q + 1) * P], ident[:, :])
                mm.then_inc(c_max_turned, 1)

            def spread_max(n):
                pe_block.wait_ge(c_mstep, HEAD + 3 * n + 3)
                for q in range(SUB):
                    mm = pe.matmul(bank[7][:, q * P:(q + 1) * P], ones[:, :], c_diag[:, q, :], start=True, stop=True)
                mm.then_inc(c_mps, 1)

            def pv(n, t):
                pe_block.wait_ge(c_lo, HEAD + KT * n + t + 1)
                for q in range(SUB):
                    if t == 0:
                        pe_block.wait_ge(c_x2, HEAD + 4 * n + q - 3)
                    mm = mm3(pe, bank[q][:, :], [r[t % RING][:, q * P:(q + 1) * P] for r in (c_ph, c_pl)],
                             [vp[h][:, t, :] for h in range(2)], t == 0, t == KT - 1)
                    if t == KT - 1 and q < SUB - 1:
                        mm.then_inc(c_out, 1)
                mm.then_inc(c_pv, 1)

            def sums(n):
                pe_block.wait_ge(c_add, HEAD + (KT - 1) * (n + 1))
                for q in range(SUB):
                    mm = pe.matmul(bank[6][:, q:q + 1], c_sum[:, q * P:(q + 1) * P], ones[:, 0:1], start=True, stop=True)
                mm.then_inc(c_sumps, 1)

            scores(0)
            turn_max(0)
            spread_max(0)
            after_s(pe_block)
            pe_block.wait_ge(s_tailstore, HEAD + 48)

            def body_c(i, last):
                for u in range(2):
                    n = 2 * i + u
                    more = not (last and u)
                    for t in range(KT - HELD):
                        if t == 5:
                            pe_block.wait_ge(c_tstep, HEAD + 7 * n + 6)
                            for q in range(SUB):
                                mm = pe.transpose(bank[5][0:3 * KX, q * P:(q + 1) * P], c_t3[:, q, :], ident[:, :])
                            mm.then_inc(c_tail_turned, 1)
                        if t == 12:
                            if more:
                                Cn.tensor_turn(pe_block, n + 1, 0)
                            else:
                                Dn.tensor_turn(pe_block, 0, 0)
                        pv(n, t)
                        if t == 11:
                            pe_block.wait_ge(c_tail_rows, HEAD + n + 1)
                            for q in range(SUB):
                                pe.matmul(bank[q][:, :], c_tT[0:3 * KX, q * P:(q + 1) * P], tail_v[0:3 * KX, :],
                                          start=False, stop=False)
                    if more:
                        scores(n + 1)
                    pv(n, KT - 4)
                    if more:
                        turn_max(n + 1)
                    pv(n, KT - 3)
                    if more:
                        spread_max(n + 1)
                    pv(n, KT - 2)
                    pe_block.wait_ge(c_score, HEAD + KT * n + KT + (KT if more else 0))
                    if not more:
                        pe_block.wait_ge(Dn.lo, HEAD + 4)
                    sums(n)
                    pv(n, KT - 1)

            pair_loop(body_c)

            pe_block.wait_ge(d_wload, 32)
            pe_block.wait_ge(c_rinvstep, HEAD + 2 * NB)

            def body_d(i, last):
                for u in range(2):
                    n = 2 * i + u
                    more = not (last and u)

                    def ffn2(t):
                        pe_block.wait_ge(d_glo, HEAD + HT * n + t + 1)
                        if t == 0:
                            pe_block.wait_ge(c_x2, HEAD + 4 * NB)
                            pe_block.wait_ge(d_out, HEAD + 4 * n)
                        for q in range(SUB):
                            for h, g in enumerate((d_gh, d_gl)):
                                mm = pe.matmul(bank[q][:, :], g[:, t, q * P:(q + 1) * P], d_w2[:, t, :],
                                               start=t == 0 and h == 0, stop=t == HT - 1 and h == 1)
                            if t == HT - 1:
                                mm.then_inc(d_ops, 1)
                        if t < HT - 1:
                            mm.then_inc(d_f2, 1)

                    pe_block.wait_ge(Dn.lo, HEAD + 4 * n + 4)
                    for t in range(HT + LAG):
                        if t < HT:
                            if t >= 4:
                                pe_block.wait_ge(d_gelu, HEAD + HT * n + t - 3)
                            for j in range(CT):
                                for h in range(2):
                                    mm = pe.matmul(bank[4 + t % 4][:, :], d_w1[:, j, t * P:(t + 1) * P], d_xT[0][h][:, j, :],
                                                   start=j == 0 and h == 0, stop=j == CT - 1 and h == 1)
                            mm.then_inc(d_hps, 1)
                        if more and t == HT + 1:
                            pe_block.wait_ge(d_gelu, HEAD + HT * n + HT)
                            Dn.tensor_turn(pe_block, n + 1, 0)
                        if t >= LAG:
                            ffn2(t - LAG)

            pair_loop(body_d)


def kernel(x, ctx_1024, L0_attn_qk_w, L0_attn_qk_b, L0_attn_lepe_w, L0_attn_lepe_b, L0_xattn_Wk, L0_xattn_Wv,
           L0_xattn_bv, L0_xattn_Wq, L0_xattn_bq, L0_xattn_Wo, L0_xattn_bo, L0_ffn_w1, L0_ffn_b1, L0_ffn_w2,
           L0_ffn_b2):
    import numpy as np
    import concourse.bacc as bacc
    from concourse.bass_utils import run_bass_kernel_spmd as run

    theta = np.float32(1.0) / (10000.0 ** (np.arange(HALF) / HALF)).astype(np.float32)
    angles = np.arange(N, dtype=np.float32)[:, None] * theta
    cos, sin = np.cos(angles), np.sin(angles)

    def cont(v):
        return np.ascontiguousarray(v)

    def column(v):
        return cont(np.reshape(v, (-1, P)).T)

    w1_groups = np.reshape(np.asarray(L0_ffn_w1).T, (4, P, H))
    w2_groups = np.reshape(np.transpose(np.reshape(np.asarray(L0_ffn_w2).T, (4, 4, P, C)), (0, 2, 1, 3)), (4, P, 4 * C))
    ffn_w = cont(np.stack([w1_groups, w2_groups], axis=1).reshape(8, P, 4 * C))
    qk_w, qk_b = np.asarray(L0_attn_qk_w), np.asarray(L0_attn_qk_b)

    def halves(v):
        return np.concatenate([v[..., 0::2], v[..., 1::2]], axis=-1)

    arrays = {
        "x": cont(np.asarray(x)[0]),
        "ctxT": cont(np.asarray(ctx_1024)[0].T),
        "wq_rope": cont(halves(qk_w[:, :C])), "wk_rope": cont(halves(qk_w[:, C:])),
        "bq_rope": column(halves(qk_b[:C])), "bk_rope": cont(halves(qk_b[C:])),
        "lepe_w": cont(np.reshape(L0_attn_lepe_w, (3 * C, C))), "lepe_b": cont(L0_attn_lepe_b),
        "xk": cont(L0_xattn_Wk), "xq": cont(L0_xattn_Wq), "xv": cont(L0_xattn_Wv),
        "xoT": cont(np.asarray(L0_xattn_Wo).T),
        "xbq": column(L0_xattn_bq), "xbv": column(L0_xattn_bv), "xbo": cont(L0_xattn_bo),
        "ffn_w": ffn_w,
        "b1": column(L0_ffn_b1), "b2": cont(L0_ffn_b2),
        "cos": cont(cos), "sin": cont(sin), "cosT": cont(cos.T), "sinT": cont(sin.T),
    }
    nc = bacc.Bacc("TRN2", target_bir_lowering=False, num_devices=1)
    d = {k: nc.dram_tensor(k, v.shape, mybir.dt.from_np(v.dtype), kind="ExternalInput").ap() for k, v in arrays.items()}
    for name, shape, dt in (("x1", (N, C), F32), ("x2", (N, C), F32), ("xT_hi", (C, N + 2 * EDGE), F16),
                            ("xT_lo", (C, N + 2 * EDGE), F16),
                            ("signs", (8, P, 4 * C), F16)):
        d[name] = nc.dram_tensor(name, shape, dt, kind="Internal").ap()
    d["out"] = nc.dram_tensor("out", (N, C), F32, kind="ExternalOutput").ap()
    build(nc, d)
    r = run(nc, [arrays], core_ids=[0])
    return np.reshape(r.results[0]["out"], (1, N, C))
```
